# Optimizing a Trainium2 kernel written in Bass

```python
import numpy as np
import jax
import jax.numpy as jnp

def _softmax(x, axis=-1):
    return jax.nn.softmax(x, axis=axis)

def _gelu(x):
    return jax.nn.gelu(x, approximate=True)

def _silu(x):
    return jax.nn.silu(x)

def _sigmoid(x):
    return jax.nn.sigmoid(x)

def _layernorm(x, axis=-1, eps=1e-05):
    m = jnp.mean(x, axis=axis, keepdims=True)
    v = jnp.var(x, axis=axis, keepdims=True)
    return (x - m) / jnp.sqrt(v + eps)

def _scatter_add(tgt, idx, src, axis=0):
    return tgt.at[idx].add(src)

def _segment_sum(src, seg, n):
    return jax.ops.segment_sum(src, seg, n)
kernel_name = 'mk_sandwich_d2_jaxref_r4_47f5c3'

def setup_inputs(seed: int=0):
    np.random.seed(seed)
    _w = jnp.asarray

    def _L0_attn_setup():
        import jax, jax.numpy as jnp
        import numpy as np
        D_MODEL = 256
        N_HEADS = 16
        D_HEAD = D_MODEL // N_HEADS
        SCALE = 1.0 / np.sqrt(D_HEAD)
        key = jax.random.key(seed)
        ks = jax.random.split(key, 5)
        B, T, C = (4, 512, D_MODEL)
        s = 0.02
        return {'x': jax.random.normal(ks[0], (B, T, C), dtype=jnp.float32), 'W_qkv': jax.random.normal(ks[1], (C, 3 * C), dtype=jnp.float32) * s, 'b_qkv': jnp.zeros((3 * C,), dtype=jnp.float32), 'W_proj': jax.random.normal(ks[2], (C, C), dtype=jnp.float32) * s, 'b_proj': jnp.zeros((C,), dtype=jnp.float32)}
    _L0_attn_in = _L0_attn_setup()

    def _L0_ffn_setup():
        import jax, jax.numpy as jnp
        import numpy as np
        R = 64
        key = jax.random.key(seed)
        k1, k2, k3 = jax.random.split(key, 3)
        B, S, D_IN, D_OUT = (8, 1024, 256, 256)
        x = jax.random.normal(k1, (B, S, D_IN), dtype=jnp.float32)
        weight = jax.random.normal(k2, (D_OUT, D_IN), dtype=jnp.float32) * (1.0 / np.sqrt(D_IN))
        disha = jax.random.normal(k3, (R, D_OUT), dtype=jnp.float32) * 0.01
        return {'x': x, 'weight': weight, 'disha': disha}
    _L0_ffn_in = _L0_ffn_setup()

    def _L1_attn_setup():
        import jax, jax.numpy as jnp
        import numpy as np
        B, T, D = (1, 512, 256)
        H, DH, DV, DF = (16, 64, 64, 1024)
        EPS_LN = 1e-05
        EPS_DEN = 1e-06

        def _layernorm(x, g, b):
            m = jnp.mean(x, axis=-1, keepdims=True)
            v = jnp.mean((x - m) ** 2, axis=-1, keepdims=True)
            return (x - m) / jnp.sqrt(v + EPS_LN) * g + b

        def _phi(x):
            return jax.nn.elu(x) + 1.0

        def _linear_attention(x, Wq, Wk, Wv, Wo):
            b, t, d = x.shape
            Q = _phi((x @ Wq).reshape(b, t, H, DH)).transpose(0, 2, 1, 3)
            K = _phi((x @ Wk).reshape(b, t, H, DH)).transpose(0, 2, 1, 3)
            V = (x @ Wv).reshape(b, t, H, DV).transpose(0, 2, 1, 3)
            KV = jnp.einsum('bhti,bhtj->bhtij', K, V)
            S = jnp.cumsum(KV, axis=2)
            z = jnp.cumsum(K, axis=2)
            num = jnp.einsum('bhti,bhtij->bhtj', Q, S)
            den = jnp.maximum(jnp.einsum('bhti,bhti->bht', Q, z), EPS_DEN)[..., None]
            out = (num / den).transpose(0, 2, 1, 3).reshape(b, t, H * DV)
            return out @ Wo
        key = jax.random.key(seed)
        ks = jax.random.split(key, 8)
        s = 0.02
        return {'x': jax.random.normal(ks[0], (B, T, D), dtype=jnp.float32), 'ln1_g': jnp.ones((D,), jnp.float32), 'ln1_b': jnp.zeros((D,), jnp.float32), 'Wq': jax.random.normal(ks[1], (D, H * DH), jnp.float32) * s, 'Wk': jax.random.normal(ks[2], (D, H * DH), jnp.float32) * s, 'Wv': jax.random.normal(ks[3], (D, H * DV), jnp.float32) * s, 'Wo': jax.random.normal(ks[4], (H * DV, D), jnp.float32) * s, 'ln2_g': jnp.ones((D,), jnp.float32), 'ln2_b': jnp.zeros((D,), jnp.float32), 'Wf1': jax.random.normal(ks[5], (D, DF), jnp.float32) * s, 'Wf2': jax.random.normal(ks[6], (DF, D), jnp.float32) * s}
    _L1_attn_in = _L1_attn_setup()

    def _L1_ffn_setup():
        import math
        import jax, jax.numpy as jnp
        import numpy as np
        B, S, D, H, E, K = (4, 512, 256, 1024, 8, 2)
        CAPACITY_RATIO = 1.05
        key = jax.random.key(seed)
        k0, k1, k2, k3 = jax.random.split(key, 4)
        x = jax.random.normal(k0, (B, S, D), jnp.float32)
        Wg = jax.random.normal(k1, (D, E), jnp.float32) * 0.02
        W1 = jax.random.normal(k2, (E, D, H), jnp.float32) * 0.02
        b1 = jnp.zeros((E, H), jnp.float32)
        W2 = jax.random.normal(k3, (E, H, D), jnp.float32) * 0.02
        b2 = jnp.zeros((E, D), jnp.float32)
        return {'x': x, 'Wg': Wg, 'W1': W1, 'b1': b1, 'W2': W2, 'b2': b2}
    _L1_ffn_in = _L1_ffn_setup()
    _d = {'L0_attn_x': _L0_attn_in['x'], 'L0_attn_W_qkv': _L0_attn_in['W_qkv'], 'L0_attn_b_qkv': _L0_attn_in['b_qkv'], 'L0_attn_W_proj': _L0_attn_in['W_proj'], 'L0_attn_b_proj': _L0_attn_in['b_proj'], 'L0_ffn_weight': _L0_ffn_in['weight'], 'L0_ffn_disha': _L0_ffn_in['disha'], 'L1_attn_ln1_g': _L1_attn_in['ln1_g'], 'L1_attn_ln1_b': _L1_attn_in['ln1_b'], 'L1_attn_Wq': _L1_attn_in['Wq'], 'L1_attn_Wk': _L1_attn_in['Wk'], 'L1_attn_Wv': _L1_attn_in['Wv'], 'L1_attn_Wo': _L1_attn_in['Wo'], 'L1_attn_ln2_g': _L1_attn_in['ln2_g'], 'L1_attn_ln2_b': _L1_attn_in['ln2_b'], 'L1_attn_Wf1': _L1_attn_in['Wf1'], 'L1_attn_Wf2': _L1_attn_in['Wf2'], 'L1_ffn_Wg': _L1_ffn_in['Wg'], 'L1_ffn_W1': _L1_ffn_in['W1'], 'L1_ffn_b1': _L1_ffn_in['b1'], 'L1_ffn_W2': _L1_ffn_in['W2'], 'L1_ffn_b2': _L1_ffn_in['b2']}
    _x0 = _d['L0_attn_x']
    _d['L0_attn_x'] = jax.random.normal(jax.random.fold_in(jax.random.key(seed), 1), (8, 1024, 256), dtype=_x0.dtype)
    del _x0
    return _d

def reference(L0_attn_x, L0_attn_W_qkv, L0_attn_b_qkv, L0_attn_W_proj, L0_attn_b_proj, L0_ffn_weight, L0_ffn_disha, L1_attn_ln1_g, L1_attn_ln1_b, L1_attn_Wq, L1_attn_Wk, L1_attn_Wv, L1_attn_Wo, L1_attn_ln2_g, L1_attn_ln2_b, L1_attn_Wf1, L1_attn_Wf2, L1_ffn_Wg, L1_ffn_W1, L1_ffn_b1, L1_ffn_W2, L1_ffn_b2):

    def _L0_attn_ref(x, W_qkv, b_qkv, W_proj, b_proj):
        import jax, jax.numpy as jnp
        import numpy as np
        D_MODEL = 256
        N_HEADS = 16
        D_HEAD = D_MODEL // N_HEADS
        SCALE = 1.0 / np.sqrt(D_HEAD)
        B, T, C = x.shape
        qkv = x @ W_qkv + b_qkv
        q, k, v = jnp.split(qkv, 3, axis=-1)
        q = q.reshape(B, T, N_HEADS, D_HEAD).transpose(0, 2, 1, 3)
        k = k.reshape(B, T, N_HEADS, D_HEAD).transpose(0, 2, 1, 3)
        v = v.reshape(B, T, N_HEADS, D_HEAD).transpose(0, 2, 1, 3)
        att = jnp.einsum('bhqd,bhkd->bhqk', q, k) * SCALE
        causal = jnp.tril(jnp.ones((T, T), dtype=bool))
        att = jnp.where(causal, att, -jnp.inf)
        att = jax.nn.softmax(att, axis=-1)
        y = jnp.einsum('bhqk,bhkd->bhqd', att, v)
        y = y.transpose(0, 2, 1, 3).reshape(B, T, C)
        return y @ W_proj + b_proj

    def _L0_ffn_ref(x, weight, disha):
        import jax, jax.numpy as jnp
        import numpy as np
        R = 64
        result = jnp.einsum('bsd,od->bso', x, weight)
        r = disha.shape[0]
        pooled = x.reshape(*x.shape[:-1], x.shape[-1] // r, r).sum(axis=-2)
        return result + pooled @ disha

    def _L1_attn_ref(x, ln1_g, ln1_b, Wq, Wk, Wv, Wo, ln2_g, ln2_b, Wf1, Wf2):
        import jax, jax.numpy as jnp
        import numpy as np
        B, T, D = (1, 512, 256)
        H, DH, DV, DF = (16, 64, 64, 1024)
        EPS_LN = 1e-05
        EPS_DEN = 1e-06

        def _layernorm(x, g, b):
            m = jnp.mean(x, axis=-1, keepdims=True)
            v = jnp.mean((x - m) ** 2, axis=-1, keepdims=True)
            return (x - m) / jnp.sqrt(v + EPS_LN) * g + b

        def _phi(x):
            return jax.nn.elu(x) + 1.0

        def _linear_attention(x, Wq, Wk, Wv, Wo):
            b, t, d = x.shape
            Q = _phi((x @ Wq).reshape(b, t, H, DH)).transpose(0, 2, 1, 3)
            K = _phi((x @ Wk).reshape(b, t, H, DH)).transpose(0, 2, 1, 3)
            V = (x @ Wv).reshape(b, t, H, DV).transpose(0, 2, 1, 3)
            KV = jnp.einsum('bhti,bhtj->bhtij', K, V)
            S = jnp.cumsum(KV, axis=2)
            z = jnp.cumsum(K, axis=2)
            num = jnp.einsum('bhti,bhtij->bhtj', Q, S)
            den = jnp.maximum(jnp.einsum('bhti,bhti->bht', Q, z), EPS_DEN)[..., None]
            out = (num / den).transpose(0, 2, 1, 3).reshape(b, t, H * DV)
            return out @ Wo
        x = x + _linear_attention(_layernorm(x, ln1_g, ln1_b), Wq, Wk, Wv, Wo)
        h = _layernorm(x, ln2_g, ln2_b)
        x = x + jax.nn.gelu(h @ Wf1, approximate=False) @ Wf2
        return x

    def _L1_ffn_ref(x, Wg, W1, b1, W2, b2):
        import math
        import jax, jax.numpy as jnp
        import numpy as np
        B, S, D, H, E, K = (4, 512, 256, 1024, 8, 2)
        CAPACITY_RATIO = 1.05
        b, s, d = x.shape
        e = Wg.shape[1]
        n = b * s
        cap = int(math.ceil(n * K / e * CAPACITY_RATIO))
        xf = x.reshape(n, d)
        probs = jax.nn.softmax(xf @ Wg, axis=-1)
        topv, topi = jax.lax.top_k(probs, K)
        gates = topv / jnp.sum(topv, axis=-1, keepdims=True)
        eidx = topi.reshape(-1)
        oh = jax.nn.one_hot(eidx, e, dtype=jnp.int32)
        pos = jnp.sum(jnp.cumsum(oh, axis=0) * oh, axis=-1) - 1
        keep = pos < cap
        dest = jnp.where(keep, eidx * cap + pos, e * cap)
        xr = jnp.repeat(xf, K, axis=0)
        buf = jnp.zeros((e * cap + 1, d), x.dtype).at[dest].set(xr)
        expert_in = buf[:e * cap].reshape(e, cap, d)
        h = jax.nn.gelu(jnp.einsum('ecd,edh->ech', expert_in, W1) + b1[:, None, :])
        y = jnp.einsum('ech,ehd->ecd', h, W2) + b2[:, None, :]
        yf = jnp.concatenate([y.reshape(e * cap, d), jnp.zeros((1, d), y.dtype)], axis=0)
        gathered = yf[dest]
        w = (gates.reshape(-1) * keep.astype(gates.dtype))[:, None]
        out = (gathered * w).reshape(n, K, d).sum(axis=1).reshape(b, s, d)
        return out
    x = L0_attn_x
    x = x + _layernorm(_L0_attn_ref(_layernorm(x, axis=-1), L0_attn_W_qkv, L0_attn_b_qkv, L0_attn_W_proj, L0_attn_b_proj), axis=-1)
    x = x + _layernorm(_L0_ffn_ref(_layernorm(x, axis=-1), L0_ffn_weight, L0_ffn_disha), axis=-1)
    x = x + _layernorm(_L1_attn_ref(_layernorm(x, axis=-1), L1_attn_ln1_g, L1_attn_ln1_b, L1_attn_Wq, L1_attn_Wk, L1_attn_Wv, L1_attn_Wo, L1_attn_ln2_g, L1_attn_ln2_b, L1_attn_Wf1, L1_attn_Wf2), axis=-1)
    x = x + _layernorm(_L1_ffn_ref(_layernorm(x, axis=-1), L1_ffn_Wg, L1_ffn_W1, L1_ffn_b1, L1_ffn_W2, L1_ffn_b2), axis=-1)
    return x

_drawn_inputs = setup_inputs


def setup_inputs(seed=0):
    import zlib

    import numpy as np

    out = dict(_drawn_inputs(seed))
    spreads = {'L0_attn_b_qkv': (0.0, 0.1),
     'L0_attn_b_proj': (0.0, 0.1),
     'L1_attn_ln1_g': (1.0, 0.2),
     'L1_attn_ln1_b': (0.0, 0.1),
     'L1_attn_ln2_g': (1.0, 0.2),
     'L1_attn_ln2_b': (0.0, 0.272),
     'L1_ffn_b1': (0.0, 0.1),
     'L1_ffn_b2': (0.0, 0.1)}
    factors = {'L1_attn_Wq': 8.0, 'L1_attn_Wk': 8.0}
    for name, (base, spread) in spreads.items():
        noise = np.random.default_rng([zlib.crc32(name.encode()), seed]).standard_normal(out[name].shape)
        drawn = base * np.exp(spread * noise) if base else spread * noise
        out[name] = jnp.asarray(drawn.astype(out[name].dtype))
    for name, factor in factors.items():
        out[name] = (out[name] * factor).astype(out[name].dtype)
    return out
```

```python
from contextlib import ExitStack

import concourse.bass as bass
from concourse import mybir

F32 = mybir.dt.float32
BF16 = mybir.dt.bfloat16
I32 = mybir.dt.int32
U32 = mybir.dt.uint32
ALU = mybir.AluOpType
ACT = mybir.ActivationFunctionType
AX = mybir.AxisListType

P = 128
B, T, D = 8, 1024, 256
N = B * T
CD = D // P
TT = T // P
HALF = 512
EPS = 1e-5
EPS_DEN = 1e-6
NEG = -1e30

H0, DH0 = 16, 16
SCALE = DH0 ** -0.5
QTERM = (0, 1, 2, 0, 1, 0)
KTERM = (0, 0, 0, 1, 1, 2)
KS = DH0 * len(QTERM)
KM = KS + 3

H1, DH1 = 16, 64
E1 = H1 * DH1
DF = 1024
MF = DF // P
G4 = 4
SUP = T // (G4 * P)
DV = DH1 + 1

E, HE = 8, 1024
CAP = -(-N * 2 * 105 // (E * 100))
CT = -(-CAP // P)
SLOTS = E * CT * P


class Ring:

    def __init__(self, sem, name, slots, units):
        assert units % slots == 0
        self.slots, self.per = slots, units // slots
        self.start = 1 + self.per
        self.full = [sem(f"{name}_full{s}") for s in range(slots)]
        self.evacuated = [sem(f"{name}_evacuated{s}") for s in range(slots)]

    def slot(self, u):
        return u % self.slots

    def wait_free(self, eng, b, u):
        eng.wait_ge(self.evacuated[u % self.slots], b * self.per + self.start + u // self.slots)

    def wait_full(self, eng, b, u):
        eng.wait_ge(self.full[u % self.slots], b * self.per + u // self.slots + 1)

    def wait_evacuated(self, eng, b, u):
        eng.wait_ge(self.evacuated[u % self.slots], b * self.per + self.start + u // self.slots + 1)

    def wait_evacuated_before(self, eng, b, u):
        eng.wait_ge(self.evacuated[u % self.slots], b * self.per + u // self.slots + 2)

    def begin(self, eng):
        for s in self.evacuated:
            eng.sem_inc(s, self.start)


class Chain:

    def __init__(self, sem, name, per):
        self.sem, self.per, self.at = sem(name), per, 0

    def link(self, eng, b, ins):
        self.at += 1
        ins.then_inc(self.sem, 1)
        eng.wait_ge(self.sem, b * self.per + self.at)

    def done(self):
        assert self.at == self.per, (self.sem.name, self.at)


def batch_view(dram):
    return dram.rearrange("(b j p) d -> b p j d", p=P, j=TT)


def of_batch(view, b):
    return view[bass.ds(b, 1), :, :, :].rearrange("a p j d -> p (a j) d")


def build(nc, x, W_qkv, b_qkv, W_proj, b_proj, weight, disha, g1, be1, Wq, Wk, Wv, Wo, g2, be2,
          Wf1, Wf2, Wg, W1, b1, W2, b2, out):
    x_rows = x.rearrange("b t d -> (b t) d")
    out_rows = out.rearrange("b t d -> (b t) d")
    x2_dram = nc.dram_tensor("x2_scratch", (N, D), F32).ap()
    x3_dram = nc.dram_tensor("x3_scratch", (N, D), F32).ap()
    xf_dram = nc.dram_tensor("xf_scratch", (N, D), F32).ap()
    rows_dram = nc.dram_tensor("expert_rows_scratch", (SLOTS, D), F32).ap()
    y_dram = nc.dram_tensor("expert_out_scratch", (SLOTS + P, D), F32).ap()

    with ExitStack() as whole:
        def sb(name, shape, dt=F32):
            return whole.enter_context(nc.sbuf_tensor(name, shape, dt))

        ident = sb("ident", [P, P])
        ident_bf = sb("ident_bf", [P, P], BF16)
        logits = sb("logits", [P, N // P, E])
        minus_half = sb("minus_half", [P, TT])
        constants(nc, ident, ident_bf, minus_half)
        softmax_layer(nc, ident, ident_bf, minus_half, x_rows, W_qkv, b_qkv, W_proj, b_proj, weight,
                      disha, x2_dram, rows_dram, y_dram)
        linear_layer(nc, ident, minus_half, x2_dram, g1, be1, Wq, Wk, Wv, Wo, g2, be2, Wf1, Wf2, Wg,
                     x3_dram, xf_dram, logits)
        with ExitStack() as ctx:
            w1 = ctx.enter_context(nc.sbuf_tensor("w_first", [P, N // P], F32))
            w2 = ctx.enter_context(nc.sbuf_tensor("w_second", [P, N // P], F32))
            from1 = ctx.enter_context(nc.sbuf_tensor("from_first", [P, N // P], I32))
            from2 = ctx.enter_context(nc.sbuf_tensor("from_second", [P, N // P], I32))
            routing(nc, logits, xf_dram, rows_dram, w1, w2, from1, from2)
            experts(nc, ident, rows_dram, W1, b1, W2, b2, y_dram)
            combine(nc, minus_half, y_dram, x3_dram, w1, w2, from1, from2, out_rows)


def constants(nc, ident, ident_bf, minus_half):
    with ExitStack() as ctx:
        cleared = ctx.enter_context(nc.semaphore("c_cleared"))
        made = ctx.enter_context(nc.semaphore("c_made"))
        with nc.Block() as block:
            @block.gpsimd
            def _(pool):
                nc.gpsimd.memset(ident[:, :], 0.0).then_inc(cleared, 1)
                nc.gpsimd.memset(ident_bf[:, :], 0.0).then_inc(cleared, 1)
                nc.gpsimd.memset(minus_half[:, :], -0.5).then_inc(made, 1)
                pool.wait_ge(cleared, 2)
                for m in (ident, ident_bf):
                    nc.gpsimd.affine_select(out=m[:, :], in_=m[:, :], compare_op=ALU.not_equal,
                                            fill=1.0, base=0, pattern=[[-1, P]],
                                            channel_multiplier=1).then_inc(made, 1)
                pool.wait_ge(made, 3)


class LayerNorm:

    def __init__(self, nc, ctx, sem, name, n, calls, minus_half, var_eps=EPS):
        self.nc, self.n, self.calls, self.minus_half = nc, n, calls, minus_half
        self.stats = ctx.enter_context(nc.sbuf_tensor(f"{name}_stats", [P, n, 6], F32))
        self.sums = ctx.enter_context(nc.sbuf_tensor(f"{name}_sums", [P, 3, n], F32))
        self.square = ctx.enter_context(nc.sbuf_tensor(f"{name}_square", [P, 2, n], F32))
        self.mean = ctx.enter_context(nc.sbuf_tensor(f"{name}_mean", [P, n], F32))
        self.ve = ctx.enter_context(nc.sbuf_tensor(f"{name}_ve", [P, n], F32))
        self.rstd = ctx.enter_context(nc.sbuf_tensor(f"{name}_rstd", [P, n], F32))
        self.var_ready, self.rstd_ready = sem(f"{name}_var_ready"), sem(f"{name}_rstd_ready")

    def variance(self, dve, b, call, chain, tile):
        nc = self.nc
        for j in range(self.n):
            last = nc.vector.bn_stats(self.stats[:, j, :], tile(j))
        chain.link(dve, b, last)
        st, sums, sq = self.stats, self.sums, self.square
        nc.vector.tensor_tensor(sums[:, 0, :], st[:, :, 1], st[:, :, 4], ALU.add)
        nc.vector.tensor_tensor(sums[:, 1, :], st[:, :, 1], st[:, :, 4], ALU.subtract)
        chain.link(dve, b, nc.vector.tensor_tensor(sums[:, 2, :], st[:, :, 2], st[:, :, 5], ALU.add))
        nc.vector.tensor_scalar(self.mean[:, :], sums[:, 0, :], 0.5, None, ALU.mult)
        nc.vector.scalar_tensor_tensor(out=sq[:, 0, :], in0=sums[:, 1, :], scalar=0.25,
                                       in1=sums[:, 1, :], op0=ALU.mult, op1=ALU.mult)
        chain.link(dve, b, nc.vector.tensor_scalar(sq[:, 1, :], sums[:, 2, :], 1.0 / D, EPS,
                                                   ALU.mult, ALU.add))
        nc.vector.tensor_tensor(self.ve[:, :], sq[:, 0, :], sq[:, 1, :],
                                ALU.add).then_inc(self.var_ready, 1)
        dve.wait_ge(self.rstd_ready, b * self.calls + call + 1)

    def power(self, pool, b, call):
        pool.wait_ge(self.var_ready, b * self.calls + call + 1)
        self.nc.gpsimd.tensor_tensor(self.rstd[:, :], self.ve[:, :], self.minus_half[:, 0:self.n],
                                     ALU.pow).then_inc(self.rstd_ready, 1)

    def apply(self, j, out, in_):
        return self.nc.vector.tensor_scalar(out, in_, self.mean[:, j:j + 1], self.rstd[:, j:j + 1],
                                            ALU.subtract, ALU.mult)


def softmax_layer(nc, ident, ident_bf, minus_half, x_rows, W_qkv, b_qkv, W_proj, b_proj, weight,
                  disha, x2_dram, rows_dram, y_dram):
    HG = H0 // 4
    HB = H0 // 8
    V_W = 32
    SEGS = [(i, 0, i * P) for i in range(4)] + [(i, 1, max(i * P, HALF)) for i in range(TT)]
    NSEG = len(SEGS)
    U_T1, U_QK, U_V, U_M, U_DEN, U_P, U_T2, U_F = 0, 4, 12, 16, 18, 26, 30, 34
    U_ALL = 38

    with ExitStack() as ctx:
        def sb(name, shape, dt=F32):
            return ctx.enter_context(nc.sbuf_tensor(name, shape, dt))

        def sem(name):
            return ctx.enter_context(nc.semaphore(name))

        psum_s = ctx.enter_context(nc.psum_tensor("a_scores", [P, 2, 2, HALF], F32))
        psum_g = ctx.enter_context(nc.psum_tensor("a_general", [P, 2, HALF], F32))
        psum_o = ctx.enter_context(nc.psum_tensor("a_attended", [P, 2, HALF], F32))

        w_qkv = sb("w_qkv", [P, CD, 3 * D])
        w_proj = sb("w_proj", [P, HG, D])
        w_ffn = sb("w_ffn", [P, CD, D])
        bias_qk = sb("bias_qk", [P, 2 * HB])
        bias_v = sb("bias_v", [P, D])
        bias_p = sb("bias_p", [P, D])
        mask_qk = sb("mask_qk", [P, P], BF16)
        mask_kq = sb("mask_kq", [P, P], BF16)
        spread = sb("spread", [P, P])
        x_in = sb("x_in", [P, TT, D])
        x_res = sb("x_res", [P, TT, D])
        xn = sb("xn", [P, TT, D])
        att = sb("att", [P, TT, D])
        yT = sb("yT", [P, HG, T])
        xnT = yT[:, 0:CD, :]
        qk_f = sb("qk_f", [P, 2, HALF])
        rest1 = sb("rest1", [P, HALF])
        one = sb("one", [P, 1])
        parts = sb("parts", [P, 2, 3, T], BF16)
        q_st = sb("q_st", [P, H0, T], BF16)
        k_st = sb("k_st", [P, H0, T], BF16)
        v_aug = sb("v_aug", [P, TT, H0, V_W])
        mx = sb("mx", [P, HB, 8 * TT])
        nm = sb("nm", [8 * TT, HB, P])
        nm_rest = sb("nm_rest", [8 * TT, 2, P])
        nm_parts = sb("nm_parts", [8 * TT, HB, 3, P], BF16)
        probs = sb("probs", [P, 2, 4, HALF])
        oT = sb("oT", [P, 2, HALF])
        rden = sb("rden", [P, HALF])
        zero = sb("zero", [P, D])

        load = sem("a_weights_loaded")
        prep = sem("a_cleared")
        made = sem("a_masks_made")
        turned = sem("a_weight_turned")
        filled = sem("a_constants_filled")
        w_raw = x_in[:, :, :].rearrange("p j d -> p (j d)")[:, 0:CD * 2 * D].rearrange(
            "p (c n) -> p c n", c=CD)
        weight_sb, disha_sb = att[:, 0:CD, :], att[:, CD, :]
        with nc.Block() as block:
            @block.sync
            def _(sp):
                w_view = W_qkv.rearrange("(c p) n -> p c n", p=P)
                sp.dma_start(w_raw, w_view[:, :, 0:2 * D]).then_inc(load, 16)
                sp.dma_start(w_qkv[:, :, 2 * D:3 * D], w_view[:, :, 2 * D:3 * D]).then_inc(load, 16)
                sp.dma_start(weight_sb, weight.rearrange("(c p) n -> p c n", p=P)).then_inc(load, 16)
                for a in range(2):
                    sp.dma_start(att[64 * a:64 * a + 64, CD, :], disha).then_inc(load, 16)
                sp.dma_start(bias_v[:, :], b_qkv[2 * D:3 * D].partition_broadcast(P)).then_inc(load, 16)
                sp.dma_start(bias_p[:, :], b_proj.partition_broadcast(P)).then_inc(load, 16)
                for n in range(2 * HB):
                    src = b_qkv[n * P:(n + 1) * P].rearrange("(h d) -> d h", d=DH0)
                    sp.dma_start(bias_qk[:, n:n + 1], src,
                                 allow_slow_non_contiguous=True).then_inc(load, 16)
                sp.wait_ge(prep, 1)
                for h in range(4):
                    src = W_proj.rearrange("(g h d) n -> h d g n", h=4, d=DH0)[h]
                    sp.dma_start(w_proj[32 * h:32 * h + DH0, :, :], src).then_inc(load, 16)
                sp.wait_ge(load, 16 * (7 + 2 * HB + 4))

            @block.vector
            def _(dve):
                nc.vector.memset(w_proj[:, :, :], 0.0).then_inc(prep, 1)
                nc.vector.memset(v_aug[:, :, :, :], 0.0).then_inc(filled, 1)
                nc.vector.memset(k_st[96:99, :, :], 1.0).then_inc(filled, 1)
                nc.vector.memset(zero[:, :], 0.0).then_inc(filled, 1)
                nc.vector.memset(one[:, :], 1.0).then_inc(filled, 1)
                dve.wait_ge(filled, 1)
                nc.vector.memset(v_aug[:, :, :, DH0:DH0 + 1], 1.0).then_inc(filled, 1)
                dve.wait_ge(load, 16 * (7 + 2 * HB + 4))
                nc.vector.tensor_scalar(bias_qk[:, 0:HB], bias_qk[:, 0:HB], SCALE, None,
                                        ALU.mult).then_inc(filled, 1)
                for c in range(CD):
                    for n in range(2 * HB):
                        cols = slice(n * P, (n + 1) * P)
                        nc.vector.tensor_copy(
                            w_qkv[:, c, cols].rearrange("p (d h) -> p d h", d=DH0),
                            w_raw[:, c, cols].rearrange("p (h d) -> p d h", d=DH0)
                            ).then_inc(filled, 1)
                dve.wait_ge(turned, 1)
                for c in range(CD):
                    nc.vector.tensor_tensor(w_ffn[:, c, :], psum_g[:, c, 0:D], disha_sb,
                                            ALU.add).then_inc(filled, 1)
                dve.wait_ge(filled, 6 + 2 * HB * CD + CD)

            @block.gpsimd
            def _(pool):
                nc.gpsimd.memset(mask_qk[:, :], 0.0).then_inc(made, 1)
                nc.gpsimd.memset(mask_kq[:, :], 0.0).then_inc(made, 1)
                nc.gpsimd.memset(spread[:, :], 0.0).then_inc(made, 1)
                pool.wait_ge(made, 3)
                nc.gpsimd.affine_select(out=mask_qk[:, :], in_=mask_qk[:, :], compare_op=ALU.is_ge,
                                        fill=NEG, base=0, pattern=[[-1, P]],
                                        channel_multiplier=1).then_inc(made, 1)
                nc.gpsimd.affine_select(out=mask_kq[:, :], in_=mask_kq[:, :], compare_op=ALU.is_ge,
                                        fill=NEG, base=0, pattern=[[1, P]],
                                        channel_multiplier=-1).then_inc(made, 1)
                sp4 = spread[:, :].rearrange("p (g w) -> p g w", g=4)
                nc.gpsimd.affine_select(out=sp4, in_=sp4, compare_op=ALU.not_equal, fill=1.0,
                                        base=-DH0, pattern=[[-32, 4], [0, 32]],
                                        channel_multiplier=1).then_inc(made, 1)
                pool.wait_ge(made, 6)

            @block.tensor
            def _(pe):
                pe.wait_ge(load, 16 * (7 + 2 * HB + 4))
                for c in range(CD):
                    for o in range(CD):
                        last = nc.tensor.transpose(psum_g[:, c, o * P:(o + 1) * P],
                                                   weight_sb[:, o, c * P:(c + 1) * P], ident[:, :])
                last.then_inc(turned, 1)

        G = Ring(sem, "a_general", 2, U_ALL)
        NS1 = HB * 8 * TT
        S = Ring(sem, "a_scores", 2, NS1 + HG * NSEG * 2)
        attended_out = [sem(f"a_attended_out{s}") for s in range(2)]
        x_loaded = sem("a_x_loaded")
        res_loaded = sem("a_residual_loaded")
        x2_ready = sem("a_x2_ready")
        x2_stored = sem("a_x2_stored")
        xn_ready = sem("a_xn_ready")
        split_done = sem("a_split_done")
        stacked = [sem("a_q_stacked"), sem("a_k_stacked")]
        nm_ready = sem("a_minus_max_ready")
        nm_placed = [sem(f"a_minus_max_placed{m}") for m in range(HB)]
        pv_done = sem("a_probs_used")
        yT_ready = sem("a_yT_ready")
        zeroed = sem("a_rows_zeroed")
        chain = Chain(sem, "a_dve_chain", 15 + HB * 3)
        pchain = Chain(sem, "a_pool_chain", 2 * HB * 2 * 3)
        ln = LayerNorm(nc, ctx, sem, "a_ln", TT, 4, minus_half)
        GROUP = 16 * len(QTERM)
        with nc.Block() as block:
            @block.sync
            def _(sp):
                G.begin(sp)
                S.begin(sp)
                for s in attended_out:
                    sp.sem_inc(s, 1)
                sp.sem_inc(split_done, 2)
                sp.sem_inc(x2_stored, 16)
                sp.sem_inc(pv_done, 2)
                for s in stacked:
                    sp.sem_inc(s, GROUP)
                sp.sem_inc(xn_ready, 2)
                xv, x2v = batch_view(x_rows), batch_view(x2_dram)
                zv = rows_dram.rearrange("(e b p) d -> b p e d", p=P, e=SLOTS // P // B)
                with sp.Fori(0, B) as b:
                    sp.wait_ge(x2_stored, b * 16 + 16)
                    sp.wait_ge(xn_ready, b * 2 + 1)
                    sp.dma_start(x_in[:, :, :], of_batch(xv, b)).then_inc(x_loaded, 16)
                    sp.dma_start(x_res[:, :, :], of_batch(xv, b)).then_inc(res_loaded, 16)
                    sp.wait_ge(pv_done, b * HG * NSEG + 2)
                    for m in range(HB):
                        for qk, terms, st in ((0, QTERM, q_st), (1, KTERM, k_st)):
                            sp.wait_ge(split_done, b * 8 + 4 * m + 2 * qk + 2 + 2)
                            for t, part in enumerate(terms):
                                sp.dma_start(st[DH0 * t:DH0 * t + DH0, 8 * m:8 * m + 8, :],
                                             parts[:, qk, part, :]).then_inc(stacked[qk], 16)
                    for m in range(HB):
                        sp.wait_ge(nm_ready, b * HB + m + 1)
                        for t in range(3):
                            sp.dma_start(q_st[KS + t:KS + t + 1, 8 * m:8 * m + 8, :],
                                         nm_parts[:, m, t, :]).then_inc(nm_placed[m], 16)
                    sp.dma_start(zv[bass.ds(b, 1), :, :, :].rearrange("a p e d -> p (a e) d"),
                                 zero[:, :].rearrange("p (a d) -> p a d", a=1).broadcast_to(
                                     [P, SLOTS // P // B, D])).then_inc(zeroed, 16)
                    sp.wait_ge(x2_ready, b + 1)
                    sp.dma_start(of_batch(x2v, b), x_res[:, :, :]).then_inc(x2_stored, 16)
                sp.wait_ge(x2_stored, B * 16 + 16)
                sp.dma_start(y_dram[SLOTS:SLOTS + P, :], zero[:, :]).then_inc(zeroed, 16)
                sp.wait_ge(zeroed, 16 * (B + 1))

            @block.tensor
            def _(pe):
                def turn(b, u0, k):
                    pe.wait_ge(xn_ready, b * 2 + k + 2)
                    for half in range(2):
                        for c in range(CD):
                            u = u0 + half * CD + c
                            G.wait_free(pe, b, u)
                            for j in range(4):
                                last = nc.tensor.transpose(
                                    psum_g[:, G.slot(u), j * P:(j + 1) * P],
                                    xn[:, half * 4 + j, c * P:(c + 1) * P], ident[:, :])
                            last.then_inc(G.full[G.slot(u)], 1)

                with pe.Fori(0, B) as b:
                    turn(b, U_T1, 1)
                    for u in (U_T1 + 2, U_T1 + 3):
                        G.wait_evacuated(pe, b, u)
                    for m in range(HB):
                        for qk in range(2):
                            for half in range(2):
                                u = U_QK + 4 * m + 2 * qk + half
                                G.wait_free(pe, b, u)
                                for c in range(CD):
                                    last = nc.tensor.matmul(
                                        psum_g[:, G.slot(u), :],
                                        w_qkv[:, c, qk * D + m * P:qk * D + (m + 1) * P],
                                        xnT[:, c, half * HALF:(half + 1) * HALF],
                                        start=(c == 0), stop=(c == CD - 1))
                                last.then_inc(G.full[G.slot(u)], 1)
                    for u2 in range(4):
                        u = U_V + u2
                        G.wait_free(pe, b, u)
                        for jj in range(2):
                            j = 2 * u2 + jj
                            for c in range(CD):
                                last = nc.tensor.matmul(
                                    psum_g[:, G.slot(u), jj * D:(jj + 1) * D],
                                    xnT[:, c, j * P:(j + 1) * P], w_qkv[:, c, 2 * D:3 * D],
                                    start=(c == 0), stop=(c == CD - 1))
                        last.then_inc(G.full[G.slot(u)], 1)
                    for m in range(HB):
                        for st in stacked:
                            pe.wait_ge(st, b * (HB * GROUP) + (m + 2) * GROUP)
                        for h8 in range(8):
                            h = 8 * m + h8
                            for j in range(TT):
                                u = (m * 8 + h8) * TT + j
                                S.wait_free(pe, b, u)
                                s = psum_s[:, S.slot(u), :, :].rearrange("p a n -> p (a n)")
                                w = (j + 1) * P
                                for k0 in range(0, w, HALF):
                                    k1 = min(k0 + HALF, w)
                                    nc.tensor.matmul(s[:, k0:k1], q_st[0:KS, h, j * P:(j + 1) * P],
                                                     k_st[0:KS, h, k0:k1], start=True, stop=False,
                                                     skip_group_check=True)
                                nc.tensor.matmul(s[:, j * P:w], ident_bf[:, :], mask_qk[:, :],
                                                 start=False, stop=True, skip_group_check=True
                                                 ).then_inc(S.full[S.slot(u)], 1)
                        S.wait_evacuated(pe, b, (m * 8 + 7) * TT + TT - 1)
                        G.wait_free(pe, b, U_M + m)
                        nc.tensor.matmul(psum_g[0:8 * TT, G.slot(U_M + m), 0:P], mx[:, m, :],
                                         ident[:, :], start=True, stop=True
                                         ).then_inc(G.full[G.slot(U_M + m)], 1)
                    for u in (U_V + 2, U_V + 3):
                        G.wait_evacuated(pe, b, u)

                    def attend(hg, n):
                        i, half, q0 = SEGS[n]
                        k = hg * NSEG + n
                        w = (half + 1) * HALF - q0
                        v = hg * 2 + half
                        if i == 0:
                            pe.wait_ge(attended_out[v % 2], b * HG + v // 2 + 1)
                        for pair in range(2):
                            S.wait_evacuated(pe, b, NS1 + k * 2 + pair)
                        for h4 in range(4):
                            last = nc.tensor.matmul(
                                psum_o[32 * h4:32 * h4 + 32, v % 2, q0 - half * HALF:HALF],
                                v_aug[:, i, hg * 4 + h4, :], probs[:, k % 2, h4, 0:w],
                                start=(i == 0), stop=True, skip_group_check=True)
                        last.then_inc(pv_done, 1)

                    def denominators(v):
                        u = U_DEN + v
                        pe.wait_ge(attended_out[v % 2], b * HG + v // 2 + 2)
                        G.wait_free(pe, b, u)
                        nc.tensor.matmul(psum_g[:, G.slot(u), :], spread[:, :], oT[:, v % 2, :],
                                         start=True, stop=True).then_inc(G.full[G.slot(u)], 1)

                    todo = []
                    for hg in range(HG):
                        if hg % 2 == 0:
                            pe.wait_ge(nm_placed[hg // 2], b * 48 + 48)
                        for n, (i, half, q0) in enumerate(SEGS):
                            w = (half + 1) * HALF - q0
                            diagonal = q0 == i * P
                            for pair in range(2):
                                u = NS1 + (hg * NSEG + n) * 2 + pair
                                S.wait_free(pe, b, u)
                                for p2 in range(2):
                                    h = hg * 4 + pair * 2 + p2
                                    s = psum_s[:, S.slot(u), p2, :]
                                    last = nc.tensor.matmul(
                                        s[:, 0:w], k_st[0:KM, h, i * P:(i + 1) * P],
                                        q_st[0:KM, h, q0:q0 + w], start=True, stop=not diagonal,
                                        skip_group_check=True)
                                    if diagonal:
                                        last = nc.tensor.matmul(s[:, 0:P], ident_bf[:, :],
                                                                mask_kq[:, :], start=False, stop=True,
                                                                skip_group_check=True)
                                last.then_inc(S.full[S.slot(u)], 1)
                            if todo:
                                ph, pn = todo.pop()
                                attend(ph, pn)
                            todo.append((hg, n))
                            if n == 4 and hg > 0:
                                denominators(hg * 2 - 1)
                            if n == 8:
                                denominators(hg * 2)
                    attend(*todo.pop())
                    denominators(HG * 2 - 1)
                    pe.wait_ge(yT_ready, b * 2 * HG + 2 * HG)
                    for u2 in range(4):
                        u = U_P + u2
                        G.wait_free(pe, b, u)
                        for jj in range(2):
                            j = 2 * u2 + jj
                            for g in range(HG):
                                last = nc.tensor.matmul(psum_g[:, G.slot(u), jj * D:(jj + 1) * D],
                                                        yT[:, g, j * P:(j + 1) * P], w_proj[:, g, :],
                                                        start=(g == 0), stop=(g == HG - 1))
                        last.then_inc(G.full[G.slot(u)], 1)
                    turn(b, U_T2, 2)
                    for u in (U_T2 + 2, U_T2 + 3):
                        G.wait_evacuated(pe, b, u)
                    for u2 in range(4):
                        u = U_F + u2
                        G.wait_free(pe, b, u)
                        for jj in range(2):
                            j = 2 * u2 + jj
                            for c in range(CD):
                                last = nc.tensor.matmul(psum_g[:, G.slot(u), jj * D:(jj + 1) * D],
                                                        xnT[:, c, j * P:(j + 1) * P], w_ffn[:, c, :],
                                                        start=(c == 0), stop=(c == CD - 1))
                        last.then_inc(G.full[G.slot(u)], 1)

            @block.scalar
            def _(act):
                def turned_rows(b, u0):
                    for half in range(2):
                        for c in range(CD):
                            u = u0 + half * CD + c
                            G.wait_full(act, b, u)
                            nc.scalar.copy(xnT[:, c, half * HALF:(half + 1) * HALF],
                                           psum_g[:, G.slot(u), :]).then_inc(G.evacuated[G.slot(u)], 1)

                with act.Fori(0, B) as b:
                    turned_rows(b, U_T1)
                    for i in range(8):
                        u = U_QK + i
                        qk, m = i // 2 % 2, i // 4
                        G.wait_full(act, b, u)
                        act.wait_ge(split_done, b * 8 + i + 1)
                        nc.scalar.activation(qk_f[:, i % 2, :], psum_g[:, G.slot(u), :], ACT.Identity,
                                             bias=bias_qk[:, qk * HB + m:qk * HB + m + 1],
                                             scale=SCALE if qk == 0 else 1.0
                                             ).then_inc(G.evacuated[G.slot(u)], 1)
                    for k in range(HG * NSEG):
                        i, half, q0 = SEGS[k % NSEG]
                        w = (half + 1) * HALF - q0
                        act.wait_ge(pv_done, b * HG * NSEG + k + 1)
                        for pair in range(2):
                            u = NS1 + k * 2 + pair
                            S.wait_full(act, b, u)
                            nc.scalar.activation(probs[:, k % 2, 2 * pair:2 * pair + 2, 0:w],
                                                 psum_s[:, S.slot(u), :, 0:w],
                                                 ACT.Exp).then_inc(S.evacuated[S.slot(u)], 1)
                    turned_rows(b, U_T2)

            @block.gpsimd
            def _(pool):
                with pool.Fori(0, B) as b:
                    ln.power(pool, b, 0)
                    for i in range(8):
                        qk, m, half = i // 2 % 2, i // 4, i % 2
                        cols = slice(half * HALF, (half + 1) * HALF)
                        G.wait_evacuated(pool, b, U_QK + i)
                        if half == 0:
                            pool.wait_ge(stacked[qk], b * (HB * GROUP) + (m + 1) * GROUP)
                        f = qk_f[:, i % 2, :]
                        ones = one[:, :].broadcast_to([P, HALF])
                        pchain.link(pool, b, nc.gpsimd.tensor_tensor(parts[:, qk, 0, cols], f, ones, ALU.mult))
                        pchain.link(pool, b, nc.gpsimd.tensor_tensor(rest1[:, :], f, parts[:, qk, 0, cols],
                                                                     ALU.subtract))
                        pchain.link(pool, b, nc.gpsimd.tensor_tensor(parts[:, qk, 1, cols], rest1[:, :],
                                                                     ones, ALU.mult))
                        nc.gpsimd.tensor_tensor(parts[:, qk, 2, cols], rest1[:, :],
                                                parts[:, qk, 1, cols],
                                                ALU.subtract).then_inc(split_done, 1)
                        pool.wait_ge(split_done, b * 8 + i + 3)
                    pchain.done()
                    for call in range(1, 4):
                        ln.power(pool, b, call)

            @block.vector
            def _(dve):
                with dve.Fori(0, B) as b:
                    dve.wait_ge(x_loaded, b * 16 + 16)
                    ln.variance(dve, b, 0, chain, lambda j: x_in[:, j, :])
                    for j in range(TT):
                        last = ln.apply(j, xn[:, j, :], x_in[:, j, :])
                    last.then_inc(xn_ready, 1)
                    for u2 in range(4):
                        u = U_V + u2
                        G.wait_full(dve, b, u)
                        nc.vector.tensor_tensor(
                            v_aug[:, 2 * u2:2 * u2 + 2, :, 0:DH0],
                            psum_g[:, G.slot(u), :].rearrange("p (j h d) -> p j h d", j=2, d=DH0),
                            bias_v[:, :].rearrange("p (a h d) -> p a h d", a=1, d=DH0).broadcast_to(
                                [P, 2, H0, DH0]),
                            ALU.add).then_inc(G.evacuated[G.slot(u)], 1)
                    for m in range(HB):
                        for n in range(8 * TT):
                            u = m * 8 * TT + n
                            w = (n % TT + 1) * P
                            S.wait_full(dve, b, u)
                            s = psum_s[:, S.slot(u), :, :].rearrange("p a n -> p (a n)")
                            nc.vector.tensor_reduce(mx[:, m, n:n + 1], s[:, 0:w], AX.X,
                                                    ALU.max).then_inc(S.evacuated[S.slot(u)], 1)
                        u = U_M + m
                        G.wait_full(dve, b, u)
                        f = nm[:, m, :]
                        nc.vector.tensor_scalar(f, psum_g[0:8 * TT, G.slot(u), 0:P], -1.0, None,
                                                ALU.mult).then_inc(G.evacuated[G.slot(u)], 1)
                        G.wait_evacuated(dve, b, u)
                        chain.link(dve, b, nc.vector.tensor_copy(nm_parts[:, m, 0, :], f))
                        chain.link(dve, b, nc.vector.tensor_tensor(nm_rest[:, 0, :], f, nm_parts[:, m, 0, :],
                                                                   ALU.subtract))
                        chain.link(dve, b, nc.vector.tensor_copy(nm_parts[:, m, 1, :], nm_rest[:, 0, :]))
                        nc.vector.tensor_tensor(nm_parts[:, m, 2, :], nm_rest[:, 0, :],
                                                nm_parts[:, m, 1, :],
                                                ALU.subtract).then_inc(nm_ready, 1)

                    def normalise(v):
                        hg, half = v // 2, v % 2
                        u = U_DEN + v
                        G.wait_full(dve, b, u)
                        nc.vector.reciprocal(rden[:, :], psum_g[:, G.slot(u), :]
                                             ).then_inc(G.evacuated[G.slot(u)], 1)
                        G.wait_evacuated(dve, b, u)
                        nc.vector.tensor_tensor(
                            yT[:, hg, half * HALF:(half + 1) * HALF], oT[:, v % 2, :], rden[:, :],
                            ALU.mult).then_inc(yT_ready, 1)
                        dve.wait_ge(yT_ready, b * 2 * HG + v + 1)

                    for v in range(2 * HG):
                        dve.wait_ge(pv_done, b * HG * NSEG + v // 2 * NSEG + (4, NSEG)[v % 2] + 2)
                        nc.vector.tensor_copy(oT[:, v % 2, :], psum_o[:, v % 2, :]
                                              ).then_inc(attended_out[v % 2], 1)
                        dve.wait_ge(attended_out[v % 2], b * HG + v // 2 + 2)
                        if v >= 1:
                            normalise(v - 1)
                    normalise(2 * HG - 1)
                    for u2 in range(4):
                        u = U_P + u2
                        G.wait_full(dve, b, u)
                        nc.vector.tensor_tensor(
                            att[:, 2 * u2:2 * u2 + 2, :],
                            psum_g[:, G.slot(u), :].rearrange("p (j d) -> p j d", j=2),
                            bias_p[:, :].rearrange("p (a d) -> p a d", a=1).broadcast_to([P, 2, D]),
                            ALU.add).then_inc(G.evacuated[G.slot(u)], 1)
                    for u in (U_P + 2, U_P + 3):
                        G.wait_evacuated(dve, b, u)

                    def add_norm(call):
                        ln.variance(dve, b, call, chain, lambda j: att[:, j, :])
                        for j in range(TT):
                            last = ln.apply(j, att[:, j, :], att[:, j, :])
                        chain.link(dve, b, last)
                        return nc.vector.tensor_tensor(x_res[:, :, :], x_res[:, :, :], att[:, :, :],
                                                       ALU.add)

                    dve.wait_ge(res_loaded, b * 16 + 16)
                    chain.link(dve, b, add_norm(1))
                    ln.variance(dve, b, 2, chain, lambda j: x_res[:, j, :])
                    for j in range(TT):
                        last = ln.apply(j, xn[:, j, :], x_res[:, j, :])
                    last.then_inc(xn_ready, 1)
                    for u2 in range(4):
                        u = U_F + u2
                        G.wait_full(dve, b, u)
                        nc.vector.tensor_copy(att[:, 2 * u2:2 * u2 + 2, :],
                                              psum_g[:, G.slot(u), :].rearrange("p (j d) -> p j d", j=2)
                                              ).then_inc(G.evacuated[G.slot(u)], 1)
                    for u in (U_F + 2, U_F + 3):
                        G.wait_evacuated(dve, b, u)
                    add_norm(3).then_inc(x2_ready, 1)
                    chain.done()


def linear_layer(nc, ident, minus_half, x2_dram, g1, be1, Wq, Wk, Wv, Wo, g2, be2, Wf1, Wf2, Wg,
                 x3_dram, xf_dram, logits):
    NP = H1 // 2
    NG = H1 // 4
    ME = E1 // P
    U_T1, U_Q, U_K, U_V, U_KT, U_O, U_W, U_T2, U_F1, U_F2, U_T3, U_L = (
        0, 2, 10, 18, 26, 34, 42, 44, 46, 54, 56, 58)
    U_ALL = 60
    NCH = G4 * NG

    with ExitStack() as ctx:
        def sb(name, shape, dt=F32):
            return ctx.enter_context(nc.sbuf_tensor(name, shape, dt))

        def sem(name):
            return ctx.enter_context(nc.semaphore(name))

        psum_g = ctx.enter_context(nc.psum_tensor("l_general", [P, 4, HALF], F32))
        psum_a = ctx.enter_context(nc.psum_tensor("l_scores", [P, 2, HALF], F32))
        psum_n = ctx.enter_context(nc.psum_tensor("l_num", [P, HALF], F32))
        psum_u = ctx.enter_context(nc.psum_tensor("l_update", [P, HALF], F32))

        wq = sb("l_wq", [P, CD, E1])
        wk = sb("l_wk", [P, CD, E1])
        wv = sb("l_wv", [P, CD, E1])
        wo = sb("l_wo", [P, ME, D])
        wf1 = sb("l_wf1", [P, CD, DF])
        wf2 = sb("l_wf2", [P, MF, D])
        wg = sb("l_wg", [P, CD, E])
        affine = sb("l_affine", [P, CD, 4])
        keep = sb("l_keep", [P, P])
        x2 = sb("l_x2", [P, G4, D])
        a3 = sb("l_a3", [P, G4, D])
        norm = sb("l_norm", [P, G4, D])
        nT = sb("l_nT", [P, CD, HALF])
        qT = sb("l_qT", [P, NP, HALF])
        kT = sb("l_kT", [P, NP, HALF])
        kt = sb("l_k", [P, G4, E1])
        v_aug = sb("l_v", [P, G4, H1, DV])
        state = sb("l_state", [P, NP, 2 * DV])
        neg = sb("l_neg", [P, 2, HALF])
        ex = sb("l_exp", [P, 2, HALF])
        scores = sb("l_scores_kept", [P, 2, 2, 4, P])
        den = sb("l_den", [P, 2, 4])
        o = sb("l_o", [P, 2, E1])
        oT = sb("l_oT", [P, ME, HALF])
        hT = qT
        x3 = x2
        xf_buf = norm

        load = sem("l_weights_loaded")
        made = sem("l_mask_made")
        filled = sem("l_constants_filled")
        n_load = 7 + 4
        with nc.Block() as block:
            @block.sync
            def _(sp):
                for dst, w in ((wq, Wq), (wk, Wk), (wv, Wv), (wo, Wo), (wf1, Wf1), (wf2, Wf2), (wg, Wg)):
                    sp.dma_start(dst[:, :, :], w.rearrange("(c p) n -> p c n", p=P)).then_inc(load, 16)
                for n, w in enumerate((g1, be1, g2, be2)):
                    sp.dma_start(affine[:, :, n], w.rearrange("(c p) -> p c", p=P),
                                 allow_slow_non_contiguous=True).then_inc(load, 16)
                sp.wait_ge(load, 16 * n_load)

            @block.gpsimd
            def _(pool):
                nc.gpsimd.memset(keep[:, :], 1.0).then_inc(made, 1)
                pool.wait_ge(made, 1)
                nc.gpsimd.affine_select(out=keep[:, :], in_=keep[:, :], compare_op=ALU.is_ge,
                                        fill=0.0, base=0, pattern=[[1, P]],
                                        channel_multiplier=-1).then_inc(made, 1)
                pool.wait_ge(made, 2)

            @block.vector
            def _(dve):
                nc.vector.memset(v_aug[:, :, :, DH1:DV], 1.0).then_inc(filled, 1)
                dve.wait_ge(filled, 1)

        G = Ring(sem, "l_general", 4, U_ALL)
        A = Ring(sem, "l_scores", 2, NCH)
        NUM = Ring(sem, "l_num", 1, NCH)
        UP = Ring(sem, "l_update", 1, NCH)
        x2_loaded = sem("l_x2_loaded")
        stored = sem("l_stored")
        norm_ready = sem("l_norm_ready")
        ex_ready = sem("l_exp_ready")
        below = sem("l_below")
        x_out_ready = sem("l_x_out_ready")
        cleared = sem("l_state_cleared")
        chain = Chain(sem, "l_dve_chain", 49)
        ln = LayerNorm(nc, ctx, sem, "l_ln", G4, 5, minus_half)
        NQK = 2 * NP

        def group_view(dram):
            return dram.rearrange("(b s j p) d -> b s p j d", p=P, j=G4, s=SUP)

        def of_group(view, b, s):
            return view[bass.ds(b, 1), s, :, :, :].rearrange("a p j d -> p (a j) d")

        with nc.Block() as block:
            @block.sync
            def _(sp):
                for ring in (G, A, NUM, UP):
                    ring.begin(sp)
                sp.sem_inc(stored, 32)
                x2v, x3v, xfv = group_view(x2_dram), group_view(x3_dram), group_view(xf_dram)
                with sp.Fori(0, B) as b:
                    for s in range(SUP):
                        g = b * SUP + s
                        sp.wait_ge(stored, g * 32 + 32)
                        sp.dma_start(x2[:, :, :], of_group(x2v, b, s)).then_inc(x2_loaded, 16)
                        sp.wait_ge(x_out_ready, g + 1)
                        sp.dma_start(of_group(x3v, b, s), x3[:, :, :]).then_inc(stored, 16)
                        sp.wait_ge(norm_ready, g * 3 + 3)
                        sp.dma_start(of_group(xfv, b, s), xf_buf[:, :, :]).then_inc(stored, 16)
                sp.wait_ge(stored, B * SUP * 32 + 32)

            @block.tensor
            def _(pe):
                def turn(g, u0, k):
                    pe.wait_ge(norm_ready, g * 3 + k)
                    for c in range(CD):
                        u = u0 + c
                        G.wait_free(pe, g, u)
                        for j in range(G4):
                            last = nc.tensor.transpose(psum_g[:, G.slot(u), j * P:(j + 1) * P],
                                                       norm[:, j, c * P:(c + 1) * P], ident[:, :])
                        last.then_inc(G.full[G.slot(u)], 1)
                    for c in range(CD):
                        G.wait_evacuated(pe, g, u0 + c)

                def by_feature(g, u, w, c_cols):
                    G.wait_free(pe, g, u)
                    for c in range(CD):
                        last = nc.tensor.matmul(psum_g[:, G.slot(u), :], w[:, c, c_cols], nT[:, c, :],
                                                start=(c == 0), stop=(c == CD - 1))
                    last.then_inc(G.full[G.slot(u)], 1)

                def two_tiles(g, u, i, lhs, rhs, nk):
                    G.wait_free(pe, g, u)
                    for jj in range(2):
                        j = 2 * i + jj
                        for k in range(nk):
                            last = nc.tensor.matmul(psum_g[:, G.slot(u), jj * D:(jj + 1) * D],
                                                    lhs[:, k, j * P:(j + 1) * P], rhs[:, k, :],
                                                    start=(k == 0), stop=(k == nk - 1))
                    last.then_inc(G.full[G.slot(u)], 1)

                def score(g, d):
                    j = d // 2
                    cols = slice(j * P, (j + 1) * P)
                    for h2 in range(2):
                        A.wait_free(pe, g, 2 * d + h2)
                    for i in range(4):
                        for h2 in range(2):
                            p, rows = d % 2 * 4 + i, slice(64 * h2, 64 * h2 + 64)
                            last = nc.tensor.matmul(psum_a[:, h2, i * P:(i + 1) * P],
                                                    kT[rows, p, cols], qT[rows, p, cols],
                                                    start=True, stop=True)
                            if i == 3:
                                last.then_inc(A.full[h2], 1)

                def turn_o(g, j):
                    NUM.wait_evacuated(pe, g, j * NG + NG - 1)
                    for half in range(2):
                        u = U_O + 2 * j + half
                        G.wait_free(pe, g, u)
                        for m in range(4):
                            last = nc.tensor.transpose(psum_g[:, G.slot(u), m * P:(m + 1) * P],
                                                       o[:, j % 2, (4 * half + m) * P:(4 * half + m + 1) * P],
                                                       ident[:, :])
                        last.then_inc(G.full[G.slot(u)], 1)

                with pe.Fori(0, B) as b:
                    for s in range(SUP):
                        g = b * SUP + s
                        turn(g, U_T1, 1)
                        for m in range(NP):
                            by_feature(g, U_Q + m, wq, slice(m * P, (m + 1) * P))
                        for m in range(NP):
                            by_feature(g, U_K + m, wk, slice(m * P, (m + 1) * P))
                        for j in range(G4):
                            for half in range(2):
                                u = U_V + 2 * j + half
                                G.wait_free(pe, g, u)
                                for c in range(CD):
                                    last = nc.tensor.matmul(psum_g[:, G.slot(u), :],
                                                            nT[:, c, j * P:(j + 1) * P],
                                                            wv[:, c, half * HALF:(half + 1) * HALF],
                                                            start=(c == 0), stop=(c == CD - 1))
                                last.then_inc(G.full[G.slot(u)], 1)
                        for u in range(U_V - 4, U_V):
                            G.wait_evacuated(pe, g, u)
                        for j in range(G4):
                            for half in range(2):
                                u = U_KT + 2 * j + half
                                G.wait_free(pe, g, u)
                                for m in range(4):
                                    last = nc.tensor.transpose(psum_g[:, G.slot(u), m * P:(m + 1) * P],
                                                               kT[:, 4 * half + m, j * P:(j + 1) * P],
                                                               ident[:, :])
                                last.then_inc(G.full[G.slot(u)], 1)
                        for u in range(U_O - 4, U_O):
                            G.wait_evacuated(pe, g, u)
                        if s == 0:
                            pe.wait_ge(cleared, b + 1)
                        score(g, 0)
                        for n in range(NCH):
                            j, g4 = n // NG, n % NG
                            d = n // 2
                            if n % 2 == 0 and d + 1 < NCH // 2:
                                score(g, d + 1)
                            NUM.wait_free(pe, g, n)
                            if n % 2 == 0:
                                for h2 in range(2):
                                    A.wait_evacuated(pe, g, 2 * d + h2)
                            for p2 in range(2):
                                p = 2 * g4 + p2
                                nc.tensor.matmul(psum_n[:, p2 * 2 * DV:(p2 + 1) * 2 * DV],
                                                 qT[:, p, j * P:(j + 1) * P], state[:, p, :],
                                                 start=True, stop=False, skip_group_check=True)
                                for h2 in range(2):
                                    h4 = 2 * p2 + h2
                                    last = nc.tensor.matmul(
                                        psum_n[:, h4 * DV:(h4 + 1) * DV],
                                        scores[:, d % 2, h2, p % 4, :],
                                        v_aug[:, j, 4 * g4 + h4, :], start=False, stop=True,
                                        skip_group_check=True)
                            last.then_inc(NUM.full[0], 1)
                            UP.wait_free(pe, g, n)
                            for p2 in range(2):
                                p = 2 * g4 + p2
                                last = nc.tensor.matmul(psum_u[:, p2 * 2 * DV:(p2 + 1) * 2 * DV],
                                                        kt[:, j, p * P:(p + 1) * P],
                                                        v_aug[:, j, 2 * p:2 * p + 2, :],
                                                        start=True, stop=True)
                            last.then_inc(UP.full[0], 1)
                            if g4 == 1 and j > 0:
                                turn_o(g, j - 1)
                        turn_o(g, G4 - 1)
                        for u in range(U_O + 4, U_O + 8):
                            G.wait_evacuated(pe, g, u)
                        for i in range(2):
                            two_tiles(g, U_W + i, i, oT, wo, ME)
                        turn(g, U_T2, 2)
                        for m in range(MF):
                            by_feature(g, U_F1 + m, wf1, slice(m * P, (m + 1) * P))
                        for u in range(U_F1 + 4, U_F1 + 8):
                            G.wait_evacuated(pe, g, u)
                        for i in range(2):
                            two_tiles(g, U_F2 + i, i, hT, wf2, MF)
                        turn(g, U_T3, 3)
                        for i in range(2):
                            u = U_L + i
                            G.wait_free(pe, g, u)
                            for jj in range(2):
                                j = 2 * i + jj
                                for c in range(CD):
                                    last = nc.tensor.matmul(psum_g[:, G.slot(u), jj * E:(jj + 1) * E],
                                                            nT[:, c, j * P:(j + 1) * P], wg[:, c, :],
                                                            start=(c == 0), stop=(c == CD - 1))
                            last.then_inc(G.full[G.slot(u)], 1)

            @block.scalar
            def _(act):
                def turned(g, u0, n):
                    for c in range(CD):
                        u = u0 + c
                        G.wait_full(act, g, u)
                        if n is None:
                            ins = nc.scalar.copy(nT[:, c, :], psum_g[:, G.slot(u), :])
                        else:
                            ins = nc.scalar.activation(nT[:, c, :], psum_g[:, G.slot(u), :], ACT.Identity,
                                                       bias=affine[:, c, n + 1:n + 2],
                                                       scale=affine[:, c, n:n + 1])
                        ins.then_inc(G.evacuated[G.slot(u)], 1)

                with act.Fori(0, B) as b:
                    for s in range(SUP):
                        g = b * SUP + s
                        turned(g, U_T1, 0)
                        for i in range(NQK):
                            if i >= 2:
                                G.wait_evacuated(act, g, U_Q + i - 2)
                            G.wait_full(act, g, U_Q + i)
                            nc.scalar.activation(neg[:, i % 2, :], psum_g[:, G.slot(U_Q + i), :],
                                                 ACT.Relu, scale=-1.0).then_inc(below, 1)
                            act.wait_ge(below, g * NQK + i + 1)
                            nc.scalar.activation(ex[:, i % 2, :], neg[:, i % 2, :], ACT.Exp,
                                                 scale=-1.0).then_inc(ex_ready, 1)
                        for i in range(16):
                            u = U_V + i
                            j, half = i % 8 // 2, i % 2
                            G.wait_full(act, g, u)
                            src = psum_g[:, G.slot(u), :]
                            if i < 8:
                                dst = v_aug[:, j, 8 * half:8 * half + 8, 0:DH1]
                                src = src.rearrange("p (h d) -> p h d", d=DH1)
                            else:
                                dst = kt[:, j, half * HALF:(half + 1) * HALF]
                            nc.scalar.copy(dst, src).then_inc(G.evacuated[G.slot(u)], 1)
                        for j in range(G4):
                            for half in range(2):
                                u = U_O + 2 * j + half
                                G.wait_full(act, g, u)
                                nc.scalar.copy(oT[:, 4 * half:4 * half + 4, j * P:(j + 1) * P],
                                               psum_g[:, G.slot(u), :].rearrange("p (m q) -> p m q", m=4)
                                               ).then_inc(G.evacuated[G.slot(u)], 1)
                        turned(g, U_T2, 2)
                        for m in range(MF):
                            u = U_F1 + m
                            G.wait_full(act, g, u)
                            nc.scalar.activation(hT[:, m, :], psum_g[:, G.slot(u), :],
                                                 ACT.Gelu).then_inc(G.evacuated[G.slot(u)], 1)
                        turned(g, U_T3, None)

            @block.gpsimd
            def _(pool):
                with pool.Fori(0, B) as b:
                    for s in range(SUP):
                        g = b * SUP + s
                        ln.power(pool, g, 0)
                        if s == 0:
                            nc.gpsimd.memset(state[:, :, :], 0.0).then_inc(cleared, 1)
                        ln.power(pool, g, 1)
                        for call in range(2, 5):
                            ln.power(pool, g, call)

            @block.vector
            def _(dve):
                def mask_scores(g, d):
                    for h2 in range(2):
                        A.wait_full(dve, g, 2 * d + h2)
                        nc.vector.tensor_tensor(
                            scores[:, d % 2, h2, :, :],
                            psum_a[:, h2, :].rearrange("p (h q) -> p h q", h=4),
                            keep[:, :].rearrange("p (a q) -> p a q", a=1).broadcast_to([P, 4, P]),
                            ALU.mult).then_inc(A.evacuated[h2], 1)

                with dve.Fori(0, B) as b:
                    for s in range(SUP):
                        g = b * SUP + s
                        chain.at = 0

                        dve.wait_ge(x2_loaded, g * 16 + 16)
                        ln.variance(dve, g, 0, chain, lambda j: x2[:, j, :])
                        for j in range(G4):
                            last = ln.apply(j, a3[:, j, :], x2[:, j, :])
                        chain.link(dve, g, last)
                        ln.variance(dve, g, 1, chain, lambda j: a3[:, j, :])
                        dve.wait_ge(stored, g * 32 + 32)
                        for j in range(G4):
                            last = ln.apply(j, norm[:, j, :], a3[:, j, :])
                        last.then_inc(norm_ready, 1)
                        for i in range(NQK):
                            dst = (qT if i < NP else kT)[:, i % NP, :]
                            dve.wait_ge(ex_ready, g * NQK + i + 1)
                            nc.vector.scalar_tensor_tensor(
                                out=dst, in0=psum_g[:, G.slot(U_Q + i), :], scalar=0.0,
                                in1=ex[:, i % 2, :], op0=ALU.max, op1=ALU.add
                                ).then_inc(G.evacuated[G.slot(U_Q + i)], 1)
                        mask_scores(g, 0)
                        for n in range(NCH):
                            j, g4 = n // NG, n % NG
                            if n % 2 == 0 and n // 2 + 1 < NCH // 2:
                                mask_scores(g, n // 2 + 1)
                            NUM.wait_full(dve, g, n)
                            num = psum_n[:, 0:4 * DV].rearrange("p (h d) -> p h d", d=DV)
                            chain.link(dve, g, nc.vector.tensor_scalar(den[:, 0, :], num[:, :, DH1],
                                                                       EPS_DEN, None, ALU.max))
                            chain.link(dve, g, nc.vector.reciprocal(den[:, 1, :], den[:, 0, :]))
                            nc.vector.tensor_tensor(
                                o[:, j % 2, g4 * 4 * DH1:(g4 + 1) * 4 * DH1].rearrange(
                                    "p (h d) -> p h d", d=DH1),
                                num[:, :, 0:DH1],
                                den[:, 1, :].rearrange("p (h a) -> p h a", a=1).broadcast_to([P, 4, DH1]),
                                ALU.mult).then_inc(NUM.evacuated[0], 1)
                            UP.wait_full(dve, g, n)
                            up = psum_u[:, 0:4 * DV].rearrange("p (a d) -> p a d", a=2)
                            for h2 in range(2):
                                rows, cols = slice(64 * h2, 64 * h2 + 64), slice(h2 * DV, h2 * DV + DV)
                                st = state[rows, 2 * g4:2 * g4 + 2, cols]
                                last = nc.vector.tensor_tensor(st, st, up[rows, :, cols], ALU.add)
                            last.then_inc(UP.evacuated[0], 1)
                        for i in range(2):
                            u = U_W + i
                            G.wait_full(dve, g, u)
                            nc.vector.tensor_tensor(a3[:, 2 * i:2 * i + 2, :],
                                                    psum_g[:, G.slot(u), :].rearrange("p (j d) -> p j d", j=2),
                                                    a3[:, 2 * i:2 * i + 2, :],
                                                    ALU.add).then_inc(G.evacuated[G.slot(u)], 1)
                        for i in range(2):
                            G.wait_evacuated(dve, g, U_W + i)
                        ln.variance(dve, g, 2, chain, lambda j: a3[:, j, :])
                        for j in range(G4):
                            last = ln.apply(j, norm[:, j, :], a3[:, j, :])
                        last.then_inc(norm_ready, 1)
                        for i in range(2):
                            u = U_F2 + i
                            G.wait_full(dve, g, u)
                            nc.vector.tensor_tensor(a3[:, 2 * i:2 * i + 2, :],
                                                    psum_g[:, G.slot(u), :].rearrange("p (j d) -> p j d", j=2),
                                                    a3[:, 2 * i:2 * i + 2, :],
                                                    ALU.add).then_inc(G.evacuated[G.slot(u)], 1)
                        for i in range(2):
                            G.wait_evacuated(dve, g, U_F2 + i)
                        ln.variance(dve, g, 3, chain, lambda j: a3[:, j, :])
                        for j in range(G4):
                            last = ln.apply(j, a3[:, j, :], a3[:, j, :])
                        chain.link(dve, g, last)
                        nc.vector.tensor_tensor(x3[:, :, :], x2[:, :, :], a3[:, :, :],
                                                ALU.add).then_inc(x_out_ready, 1)
                        dve.wait_ge(x_out_ready, g + 1)
                        ln.variance(dve, g, 4, chain, lambda j: x3[:, j, :])
                        for j in range(G4):
                            last = ln.apply(j, norm[:, j, :], x3[:, j, :])
                        last.then_inc(norm_ready, 1)
                        for i in range(2):
                            u = U_L + i
                            G.wait_full(dve, g, u)
                            dst = logits[:, bass.ds(g * G4 + 2 * i, 2), :]
                            nc.vector.tensor_copy(dst, psum_g[:, G.slot(u), 0:2 * E].rearrange(
                                "p (j e) -> p j e", j=2)).then_inc(G.evacuated[G.slot(u)], 1)
                        chain.done()


def routing(nc, logits, xf_dram, rows_dram, w1, w2, from1, from2):
    NT = N // P
    with ExitStack() as ctx:
        def sb(name, shape, dt=F32):
            return ctx.enter_context(nc.sbuf_tensor(name, shape, dt))

        def sem(name):
            return ctx.enter_context(nc.semaphore(name))

        psum = ctx.enter_context(nc.psum_tensor("r_psum", [P, 2, HALF], F32))
        before = sb("r_before", [P, P])
        ones = sb("r_ones", [P, P])
        index = sb("r_index", [P, E])
        best = [sb("r_best", [P, NT]), sb("r_second", [P, NT])]
        place = [sb("r_place_first", [P, NT]), sb("r_place_second", [P, NT])]
        picked = [sb("r_picked_first", [P, NT, E]), sb("r_picked_second", [P, NT, E])]
        left = sb("r_left", [P, NT, E])
        t0 = sb("r_t0", [P, NT, E])
        both = sb("r_both", [P, NT, E])
        count = [sb("r_count0", [P, NT, E]), sb("r_count1", [P, NT, E])]
        kept = sb("r_kept", [P, NT])
        row = sb("r_row", [P, NT])
        gap = sb("r_gap", [P, NT])
        gate = [sb("r_gate_first", [P, NT]), sb("r_gate_second", [P, NT])]
        to = [sb("r_to_first", [P, NT], I32), sb("r_to_second", [P, NT], I32)]
        XG = 4
        xf = sb("r_xf", [P, 4, XG, D])

        made = sem("r_made")
        step = sem("r_step")
        gap_ready = sem("r_gap_ready")
        exp_ready = sem("r_exp_ready")
        picked_ready = sem("r_picked_ready")
        counted = sem("r_counted")
        to_ready = sem("r_to_ready")
        xf_loaded = [sem(f"r_xf_loaded{i}") for i in range(4)]
        scattered = [sem(f"r_scattered{i}") for i in range(4)]

        def spread(t):
            return t[:, :].rearrange("p (t a) -> p t a", a=1).broadcast_to([P, NT, E])

        with nc.Block() as block:
            @block.gpsimd
            def _(pool):
                for e in range(E):
                    nc.gpsimd.memset(index[:, e:e + 1], float(e - E)).then_inc(made, 1)
                nc.gpsimd.memset(ones[:, :], 1.0).then_inc(made, 1)
                nc.gpsimd.memset(before[:, :], 1.0).then_inc(made, 1)
                pool.wait_ge(made, E + 2)
                nc.gpsimd.affine_select(out=before[:, :], in_=before[:, :], compare_op=ALU.is_ge,
                                        fill=0.0, base=-1, pattern=[[1, P]],
                                        channel_multiplier=-1).then_inc(made, 1)
                pool.wait_ge(made, E + 3)
                pool.wait_ge(to_ready, 1)
                for g in range(NT // XG):
                    pool.wait_ge(xf_loaded[g % 4], 16 * (g // 4 + 1))
                    for j in range(XG):
                        for k in range(2):
                            nc.gpsimd.indirect_dma_start(
                                out=rows_dram,
                                out_offset=bass.IndirectOffsetOnAxis(
                                    ap=to[k][:, g * XG + j:g * XG + j + 1], axis=0),
                                in_=xf[:, g % 4, j, :], in_offset=None,
                                bounds_check=SLOTS - 1, oob_is_err=False
                            ).then_inc(scattered[g % 4], 16)
                for i in range(4):
                    pool.wait_ge(scattered[i], 16 * 2 * XG * (NT // XG // 4))

            @block.sync
            def _(sp):
                xv = xf_dram.rearrange("(g j p) d -> g p j d", p=P, j=XG)
                for g in range(NT // XG):
                    if g >= 4:
                        sp.wait_ge(scattered[g % 4], 16 * 2 * XG * (g // 4))
                    sp.dma_start(xf[:, g % 4, :, :], xv[g]).then_inc(xf_loaded[g % 4], 16)

            @block.tensor
            def _(pe):
                pe.wait_ge(made, E + 3)
                pe.wait_ge(picked_ready, 1)
                sel = both[:, :, :].rearrange("p t e -> p (t e)")
                nc.tensor.matmul(psum[:, 0, 0:NT * E], before[:, :], sel, start=True, stop=True)
                nc.tensor.matmul(psum[:, 1, 0:NT * E], ones[:, :], sel, start=True,
                                 stop=True).then_inc(counted, 1)

            @block.scalar
            def _(act):
                act.wait_ge(gap_ready, 1)
                nc.scalar.activation(gap[:, :], gap[:, :], ACT.Exp).then_inc(exp_ready, 1)

            @block.vector
            def _(dve):
                at = [0]

                def link(ins):
                    at[0] += 1
                    ins.then_inc(step, 1)
                    dve.wait_ge(step, at[0])

                idx = index[:, :].rearrange("p (a e) -> p a e", a=1).broadcast_to([P, NT, E])
                dve.wait_ge(made, E)
                src = logits
                for k in range(2):
                    link(nc.vector.tensor_reduce(best[k][:, :], src[:, :, :], AX.X, ALU.max))
                    link(nc.vector.tensor_tensor(t0[:, :, :], src[:, :, :], spread(best[k]), ALU.is_equal))
                    link(nc.vector.tensor_tensor(t0[:, :, :], t0[:, :, :], idx, ALU.mult))
                    link(nc.vector.tensor_reduce(place[k][:, :], t0[:, :, :], AX.X, ALU.min))
                    link(nc.vector.tensor_tensor(picked[k][:, :, :], idx, spread(place[k]), ALU.is_equal))
                    if k == 0:
                        link(nc.vector.scalar_tensor_tensor(out=left[:, :, :], in0=picked[0][:, :, :],
                                                            scalar=NEG, in1=logits[:, :, :],
                                                            op0=ALU.mult, op1=ALU.add))
                        src = left
                nc.vector.tensor_tensor(gap[:, :], best[1][:, :], best[0][:, :],
                                        ALU.subtract).then_inc(gap_ready, 1)
                nc.vector.tensor_tensor(both[:, :, :], picked[0][:, :, :], picked[1][:, :, :],
                                        ALU.add).then_inc(picked_ready, 1)
                dve.wait_ge(counted, 1)
                total = psum[:, 1, 0:NT * E].rearrange("p (t e) -> p t e", e=E)
                within = psum[:, 0, 0:NT * E].rearrange("p (t e) -> p t e", e=E)
                nc.vector.memset(count[0][:, 0:1, :], 0.0)
                link(nc.vector.tensor_copy(count[0][:, 1:NT, :], total[:, 0:NT - 1, :]))
                a, d = 0, 1
                while d < NT:
                    nc.vector.tensor_copy(count[1 - a][:, 0:d, :], count[a][:, 0:d, :])
                    link(nc.vector.tensor_tensor(count[1 - a][:, d:NT, :], count[a][:, d:NT, :],
                                                 count[a][:, 0:NT - d, :], ALU.add))
                    a, d = 1 - a, 2 * d
                link(nc.vector.tensor_tensor(count[a][:, :, :], count[a][:, :, :], within, ALU.add))
                dve.wait_ge(exp_ready, 1)
                link(nc.vector.tensor_scalar(gate[1][:, :], gap[:, :], 1.0, None, ALU.add))
                link(nc.vector.reciprocal(gate[0][:, :], gate[1][:, :]))
                link(nc.vector.tensor_tensor(gate[1][:, :], gate[0][:, :], gap[:, :], ALU.mult))
                for k, (w, source) in enumerate(((w1, from1), (w2, from2))):
                    link(nc.vector.tensor_tensor(t0[:, :, :], picked[k][:, :, :], count[a][:, :, :],
                                                 ALU.mult))
                    link(nc.vector.tensor_reduce(row[:, :], t0[:, :, :], AX.X, ALU.add))
                    link(nc.vector.tensor_scalar(kept[:, :], row[:, :], float(CAP), None, ALU.is_lt))
                    link(nc.vector.scalar_tensor_tensor(out=row[:, :], in0=place[k][:, :],
                                                        scalar=float(CT * P), in1=row[:, :],
                                                        op0=ALU.mult, op1=ALU.add))
                    link(nc.vector.tensor_tensor(row[:, :], row[:, :], kept[:, :], ALU.mult))
                    nc.vector.tensor_scalar(source[:, :], row[:, :], float(SLOTS), None, ALU.add)
                    ins = nc.vector.tensor_scalar(to[k][:, :], row[:, :], float(SLOTS), None, ALU.add)
                    link(ins)
                    link(nc.vector.tensor_tensor(w[:, :], gate[k][:, :], kept[:, :], ALU.mult))
                dve.sem_inc(to_ready, 1)


def experts(nc, ident, rows_dram, W1, b1, W2, b2, y_dram):
    MH = HE // P
    sizes = [CT // 5 + (i < CT % 5) for i in range(5)]
    GROUPS = [(sum(sizes[:i]), n) for i, n in enumerate(sizes)]
    NGR = len(GROUPS)
    NQ = 2 * NGR
    assert max(sizes) == 4 and min(sizes) == 3
    with ExitStack() as ctx:
        def sb(name, shape, dt=F32):
            return ctx.enter_context(nc.sbuf_tensor(name, shape, dt))

        def sem(name):
            return ctx.enter_context(nc.semaphore(name))

        psum_t = ctx.enter_context(nc.psum_tensor("e_turned", [P, 2, HALF], F32))
        psum_h = ctx.enter_context(nc.psum_tensor("e_hidden", [P, 4, HALF], F32))
        psum_y = ctx.enter_context(nc.psum_tensor("e_out", [P, 2, HALF], F32))
        w1 = sb("e_w1", [P, 2, CD, HE])
        w2 = sb("e_w2", [P, 2, MH, D])
        b1_sb = sb("e_b1", [P, 2, MH])
        b2_sb = sb("e_b2", [P, 2, D])
        rows = sb("e_rows", [P, 4, D])
        rT = sb("e_rT", [P, 2, CD, HALF])
        hT = sb("e_hT", [P, 2, MH, HALF])
        y = sb("e_y", [P, 2, 4, D])

        TU = Ring(sem, "e_turned", 2, NQ * CD)
        HU = Ring(sem, "e_hidden", 4, NQ * MH)
        YU = Ring(sem, "e_out", 2, NQ * 2)
        w_loaded = [sem(f"e_weights_loaded{i}") for i in range(2)]
        rows_loaded = sem("e_rows_loaded")
        y_stored = [sem(f"e_y_stored{i}") for i in range(2)]

        def of_expert(w, e, pattern, **sizes):
            return w[bass.ds(e, 1), :, :].rearrange(pattern, **sizes)

        with nc.Block() as block:
            @block.sync
            def _(sp):
                for ring in (TU, HU, YU):
                    ring.begin(sp)
                for s in y_stored:
                    sp.sem_inc(s, 16)
                rv = rows_dram.rearrange("(e t p) d -> e p t d", p=P, t=CT)
                with sp.Fori(0, E // 2) as i:
                    for q in range(NQ):
                        e2, (t0, n) = q // NGR, GROUPS[q % NGR]
                        e = i * 2 + e2
                        if q % NGR == 0:
                            YU.wait_evacuated_before(sp, i, 2 * (e2 * NGR + NGR) - 1)
                            sp.dma_start(w1[:, e2, :, :],
                                         of_expert(W1, e, "a (c p) n -> p (a c) n", p=P)
                                         ).then_inc(w_loaded[e2], 16)
                            sp.dma_start(w2[:, e2, :, :],
                                         of_expert(W2, e, "a (c p) n -> p (a c) n", p=P)
                                         ).then_inc(w_loaded[e2], 16)
                            sp.dma_start(b1_sb[:, e2, :], b1[bass.ds(e, 1), :].rearrange(
                                "a (m p) -> p (a m)", p=P), allow_slow_non_contiguous=True
                                ).then_inc(w_loaded[e2], 16)
                            sp.dma_start(b2_sb[:, e2, :], b2[bass.ds(e, 1), :].rearrange(
                                "a d -> (a d)").partition_broadcast(P)).then_inc(w_loaded[e2], 16)
                        if q == 0:
                            TU.wait_evacuated_before(sp, i, NQ * CD - 1)
                        else:
                            TU.wait_evacuated(sp, i, q * CD - 1)
                        sp.dma_start(rows[:, 0:n, :],
                                     rv[bass.ds(e, 1), :, t0:t0 + n, :].rearrange("a p t d -> p (a t) d")
                                     ).then_inc(rows_loaded, 16)

            @block.tensor
            def _(pe):
                def turn(i, q):
                    n = GROUPS[q % NGR][1]
                    pe.wait_ge(rows_loaded, i * (16 * NQ) + 16 * q + 16)
                    for c in range(CD):
                        u = q * CD + c
                        TU.wait_free(pe, i, u)
                        for j in range(n):
                            last = nc.tensor.transpose(psum_t[:, c, j * P:(j + 1) * P],
                                                       rows[:, j, c * P:(c + 1) * P], ident[:, :])
                        last.then_inc(TU.full[c], 1)

                def hidden(i, q):
                    e2, n = q // NGR, GROUPS[q % NGR][1]
                    for c in range(CD):
                        TU.wait_evacuated(pe, i, q * CD + c)
                    if q % NGR == 0:
                        pe.wait_ge(w_loaded[e2], i * 64 + 64)
                    for m in range(MH):
                        u = q * MH + m
                        HU.wait_free(pe, i, u)
                        for c in range(CD):
                            last = nc.tensor.matmul(psum_h[:, HU.slot(u), 0:n * P],
                                                    w1[:, e2, c, m * P:(m + 1) * P],
                                                    rT[:, q % 2, c, 0:n * P],
                                                    start=(c == 0), stop=(c == CD - 1))
                        last.then_inc(HU.full[HU.slot(u)], 1)

                def outer(i, q):
                    e2, n = q // NGR, GROUPS[q % NGR][1]
                    for u in range(q * MH + 4, q * MH + 8):
                        HU.wait_evacuated(pe, i, u)
                    for a in range(2):
                        YU.wait_free(pe, i, 2 * q + a)
                        for j in range(2 * a, min(2 * a + 2, n)):
                            for m in range(MH):
                                last = nc.tensor.matmul(
                                    psum_y[:, a, (j - 2 * a) * D:(j - 2 * a + 1) * D],
                                    hT[:, q % 2, m, j * P:(j + 1) * P], w2[:, e2, m, :],
                                    start=(m == 0), stop=(m == MH - 1))
                        last.then_inc(YU.full[a], 1)

                with pe.Fori(0, E // 2) as i:
                    turn(i, 0)
                    for q in range(NQ):
                        if q + 1 < NQ:
                            turn(i, q + 1)
                        hidden(i, q)
                        if q > 0:
                            outer(i, q - 1)
                    outer(i, NQ - 1)

            @block.scalar
            def _(act):
                yv = y_dram[0:SLOTS, :].rearrange("(e t p) d -> e p t d", p=P, t=CT)

                def store(i, q):
                    e2, (t0, n) = q // NGR, GROUPS[q % NGR]
                    for a in range(2):
                        YU.wait_evacuated(act, i, 2 * q + a)
                    act.dma_start(yv[bass.ds(i * 2 + e2, 1), :, t0:t0 + n, :].rearrange(
                        "a p t d -> p (a t) d"), y[:, q % 2, 0:n, :]).then_inc(y_stored[q % 2], 16)

                with act.Fori(0, E // 2) as i:
                    for q in range(NQ):
                        e2, n = q // NGR, GROUPS[q % NGR][1]
                        if q % NGR == 0:
                            act.wait_ge(w_loaded[e2], i * 64 + 64)
                        for m in range(MH):
                            u = q * MH + m
                            if m == 4 and q >= 2:
                                store(i, q - 2)
                            HU.wait_full(act, i, u)
                            nc.scalar.activation(hT[:, q % 2, m, 0:n * P],
                                                 psum_h[:, HU.slot(u), 0:n * P], ACT.Gelu_apprx_tanh,
                                                 bias=b1_sb[:, e2, m:m + 1]
                                                 ).then_inc(HU.evacuated[HU.slot(u)], 1)
                    store(i, NQ - 2)
                    store(i, NQ - 1)
                for s in y_stored:
                    act.wait_ge(s, 16 * (E // 2 * NGR + 1))

            @block.vector
            def _(dve):
                def turned(i, q):
                    n = GROUPS[q % NGR][1]
                    for c in range(CD):
                        TU.wait_full(dve, i, q * CD + c)
                        nc.vector.tensor_copy(rT[:, q % 2, c, 0:n * P], psum_t[:, c, 0:n * P]
                                              ).then_inc(TU.evacuated[c], 1)

                def finish(i, q):
                    e2, n = q // NGR, GROUPS[q % NGR][1]
                    dve.wait_ge(y_stored[q % 2], i * (16 * NGR) + q // 2 * 16 + 16)
                    if q % NGR == 0:
                        dve.wait_ge(w_loaded[e2], i * 64 + 64)
                    for a in range(2):
                        j0, k = 2 * a, min(2, n - 2 * a)
                        YU.wait_full(dve, i, 2 * q + a)
                        nc.vector.tensor_tensor(
                            y[:, q % 2, j0:j0 + k, :],
                            psum_y[:, a, 0:k * D].rearrange("p (j d) -> p j d", d=D),
                            b2_sb[:, e2:e2 + 1, :].broadcast_to([P, k, D]),
                            ALU.add).then_inc(YU.evacuated[a], 1)

                with dve.Fori(0, E // 2) as i:
                    turned(i, 0)
                    for q in range(NQ):
                        if q + 1 < NQ:
                            turned(i, q + 1)
                        if q > 0:
                            finish(i, q - 1)
                    finish(i, NQ - 1)


def combine(nc, minus_half, y_dram, x3_dram, w1, w2, from1, from2, out_rows):
    XG = 4
    NG = N // P // XG
    R = 4
    with ExitStack() as ctx:
        def sb(name, shape, dt=F32):
            return ctx.enter_context(nc.sbuf_tensor(name, shape, dt))

        def sem(name):
            return ctx.enter_context(nc.semaphore(name))

        y1 = sb("f_y_first", [P, R, XG, D])
        y2 = sb("f_y_second", [P, R, XG, D])
        x3 = sb("f_x3", [P, R, XG, D])
        gathered = [sem(f"f_gathered{i}") for i in range(R)]
        x3_loaded = [sem(f"f_x3_loaded{i}") for i in range(R)]
        stored = [sem(f"f_stored{i}") for i in range(R)]
        weighed = sem("f_weighed")
        out_ready = sem("f_out_ready")
        chain = Chain(sem, "f_dve_chain", 5 * NG)
        ln = LayerNorm(nc, ctx, sem, "f_ln", XG, NG, minus_half)
        xv = x3_dram.rearrange("(g j p) d -> g p j d", p=P, j=XG)
        ov = out_rows.rearrange("(g j p) d -> g p j d", p=P, j=XG)
        with nc.Block() as block:
            @block.gpsimd
            def _(pool):
                def gather(g):
                    if g >= R:
                        pool.wait_ge(out_ready, g - R + 1)
                    for j in range(XG):
                        t = g * XG + j
                        for dst, idx in ((y1, from1), (y2, from2)):
                            nc.gpsimd.indirect_dma_start(
                                out=dst[:, g % R, j, :], out_offset=None, in_=y_dram,
                                in_offset=bass.IndirectOffsetOnAxis(ap=idx[:, t:t + 1], axis=0)
                            ).then_inc(gathered[g % R], 16)

                gather(0)
                gather(1)
                for g in range(NG):
                    if g + 2 < NG:
                        gather(g + 2)
                    ln.power(pool, 0, g)

            @block.sync
            def _(sp):
                for g in range(NG):
                    if g >= R:
                        sp.wait_ge(stored[g % R], 16 * (g // R))
                    sp.dma_start(x3[:, g % R, :, :], xv[g]).then_inc(x3_loaded[g % R], 16)

            @block.scalar
            def _(act):
                for g in range(NG):
                    act.wait_ge(out_ready, g + 1)
                    act.dma_start(ov[g], x3[:, g % R, :, :]).then_inc(stored[g % R], 16)
                for s in stored:
                    act.wait_ge(s, 16 * (NG // R))

            @block.vector
            def _(dve):
                for g in range(NG):
                    r = g % R
                    dve.wait_ge(gathered[r], 32 * XG * (g // R + 1))
                    for j in range(XG):
                        t = g * XG + j
                        last = nc.vector.tensor_scalar(y1[:, r, j, :], y1[:, r, j, :], w1[:, t:t + 1],
                                                       None, ALU.mult)
                    chain.link(dve, 0, last)
                    for j in range(XG):
                        t = g * XG + j
                        last = nc.vector.scalar_tensor_tensor(
                            out=y1[:, r, j, :], in0=y2[:, r, j, :], scalar=w2[:, t:t + 1],
                            in1=y1[:, r, j, :], op0=ALU.mult, op1=ALU.add)
                    last.then_inc(weighed, 1)
                    dve.wait_ge(weighed, g + 1)
                    ln.variance(dve, 0, g, chain, lambda j: y1[:, r, j, :])
                    for j in range(XG):
                        last = ln.apply(j, y1[:, r, j, :], y1[:, r, j, :])
                    chain.link(dve, 0, last)
                    dve.wait_ge(x3_loaded[r], 16 * (g // R + 1))
                    nc.vector.tensor_tensor(x3[:, r, :, :], x3[:, r, :, :], y1[:, r, :, :],
                                            ALU.add).then_inc(out_ready, 1)
                chain.done()


_INS = ['L0_attn_x', 'L0_attn_W_qkv', 'L0_attn_b_qkv', 'L0_attn_W_proj', 'L0_attn_b_proj',
        'L0_ffn_weight', 'L0_ffn_disha', 'L1_attn_ln1_g', 'L1_attn_ln1_b', 'L1_attn_Wq', 'L1_attn_Wk',
        'L1_attn_Wv', 'L1_attn_Wo', 'L1_attn_ln2_g', 'L1_attn_ln2_b', 'L1_attn_Wf1', 'L1_attn_Wf2',
        'L1_ffn_Wg', 'L1_ffn_W1', 'L1_ffn_b1', 'L1_ffn_W2', 'L1_ffn_b2']


def kernel(**inputs):
    import numpy as _np
    import concourse.bacc as _bacc
    from concourse.bass_utils import run_bass_kernel_spmd as _run

    nc = _bacc.Bacc("TRN2", target_bir_lowering=False, num_devices=1)
    arrays, args = {}, []
    for name in _INS:
        a = _np.ascontiguousarray(inputs[name])
        arrays[f"in_{name}_dram"] = a
        args.append(nc.dram_tensor(f"in_{name}_dram", a.shape, mybir.dt.from_np(a.dtype),
                                   kind="ExternalInput").ap())
    args.append(nc.dram_tensor("out_0_dram", (B, T, D), F32, kind="ExternalOutput").ap())
    build(nc, *args)
    r = _run(nc, [arrays], core_ids=[0])
    return r.results[0]["out_0_dram"]
```

```python
from contextlib import ExitStack

import concourse.bass as bass
from concourse import mybir

F32 = mybir.dt.float32
BF16 = mybir.dt.bfloat16
I32 = mybir.dt.int32
U32 = mybir.dt.uint32
ALU = mybir.AluOpType
ACT = mybir.ActivationFunctionType
AX = mybir.AxisListType

P = 128
B, T, D = 8, 1024, 256
N = B * T
CD = D // P
TT = T // P
HALF = 512
EPS = 1e-5
EPS_DEN = 1e-6
NEG = -1e30

H0, DH0 = 16, 16
SCALE = DH0 ** -0.5
QTERM = (0, 1, 2, 0, 1, 0)
KTERM = (0, 0, 0, 1, 1, 2)
KS = DH0 * len(QTERM)
KM = KS + 3

H1, DH1 = 16, 64
E1 = H1 * DH1
DF = 1024
MF = DF // P
G4 = 4
SUP = T // (G4 * P)
DV = DH1 + 1

E, HE = 8, 1024
CAP = -(-N * 2 * 105 // (E * 100))
CT = -(-CAP // P)
SLOTS = E * CT * P


class Ring:

    def __init__(self, sem, name, slots, units):
        assert units % slots == 0
        self.slots, self.per = slots, units // slots
        self.start = 1 + self.per
        self.full = [sem(f"{name}_full{s}") for s in range(slots)]
        self.evacuated = [sem(f"{name}_evacuated{s}") for s in range(slots)]

    def slot(self, u):
        return u % self.slots

    def wait_free(self, eng, b, u):
        eng.wait_ge(self.evacuated[u % self.slots], b * self.per + self.start + u // self.slots)

    def wait_full(self, eng, b, u):
        eng.wait_ge(self.full[u % self.slots], b * self.per + u // self.slots + 1)

    def wait_evacuated(self, eng, b, u):
        eng.wait_ge(self.evacuated[u % self.slots], b * self.per + self.start + u // self.slots + 1)

    def wait_evacuated_before(self, eng, b, u):
        eng.wait_ge(self.evacuated[u % self.slots], b * self.per + u // self.slots + 2)

    def begin(self, eng):
        for s in self.evacuated:
            eng.sem_inc(s, self.start)


class Chain:

    def __init__(self, sem, name, per):
        self.sem, self.per, self.at = sem(name), per, 0

    def link(self, eng, b, ins):
        self.at += 1
        ins.then_inc(self.sem, 1)
        eng.wait_ge(self.sem, b * self.per + self.at)

    def done(self):
        assert self.at == self.per, (self.sem.name, self.at)


def batch_view(dram):
    return dram.rearrange("(b j p) d -> b p j d", p=P, j=TT)


def of_batch(view, b):
    return view[bass.ds(b, 1), :, :, :].rearrange("a p j d -> p (a j) d")


def build(nc, x, W_qkv, b_qkv, W_proj, b_proj, weight, disha, g1, be1, Wq, Wk, Wv, Wo, g2, be2,
          Wf1, Wf2, Wg, W1, b1, W2, b2, out):
    x_rows = x.rearrange("b t d -> (b t) d")
    out_rows = out.rearrange("b t d -> (b t) d")
    x2_dram = nc.dram_tensor("x2_scratch", (N, D), F32).ap()
    x3_dram = nc.dram_tensor("x3_scratch", (N, D), F32).ap()
    xf_dram = nc.dram_tensor("xf_scratch", (N, D), F32).ap()
    rows_dram = nc.dram_tensor("expert_rows_scratch", (SLOTS, D), F32).ap()
    y_dram = nc.dram_tensor("expert_out_scratch", (SLOTS + P, D), F32).ap()

    with ExitStack() as whole:
        def sb(name, shape, dt=F32):
            return whole.enter_context(nc.sbuf_tensor(name, shape, dt))

        ident = sb("ident", [P, P])
        ident_bf = sb("ident_bf", [P, P], BF16)
        logits = sb("logits", [P, N // P, E])
        minus_half = sb("minus_half", [P, TT])
        constants(nc, ident, ident_bf, minus_half)
        softmax_layer(nc, ident, ident_bf, minus_half, x_rows, W_qkv, b_qkv, W_proj, b_proj, weight,
                      disha, x2_dram, rows_dram, y_dram)
        linear_layer(nc, ident, minus_half, x2_dram, g1, be1, Wq, Wk, Wv, Wo, g2, be2, Wf1, Wf2, Wg,
                     x3_dram, xf_dram, logits)
        with ExitStack() as ctx:
            w1 = ctx.enter_context(nc.sbuf_tensor("w_first", [P, N // P], F32))
            w2 = ctx.enter_context(nc.sbuf_tensor("w_second", [P, N // P], F32))
            from1 = ctx.enter_context(nc.sbuf_tensor("from_first", [P, N // P], I32))
            from2 = ctx.enter_context(nc.sbuf_tensor("from_second", [P, N // P], I32))
            routing(nc, logits, xf_dram, rows_dram, w1, w2, from1, from2)
            experts(nc, ident, rows_dram, W1, b1, W2, b2, y_dram)
            combine(nc, minus_half, y_dram, x3_dram, w1, w2, from1, from2, out_rows)


def constants(nc, ident, ident_bf, minus_half):
    with ExitStack() as ctx:
        cleared = ctx.enter_context(nc.semaphore("c_cleared"))
        made = ctx.enter_context(nc.semaphore("c_made"))
        with nc.Block() as block:
            @block.gpsimd
            def _(pool):
                nc.gpsimd.memset(ident[:, :], 0.0).then_inc(cleared, 1)
                nc.gpsimd.memset(ident_bf[:, :], 0.0).then_inc(cleared, 1)
                nc.gpsimd.memset(minus_half[:, :], -0.5).then_inc(made, 1)
                pool.wait_ge(cleared, 2)
                for m in (ident, ident_bf):
                    nc.gpsimd.affine_select(out=m[:, :], in_=m[:, :], compare_op=ALU.not_equal,
                                            fill=1.0, base=0, pattern=[[-1, P]],
                                            channel_multiplier=1).then_inc(made, 1)
                pool.wait_ge(made, 3)


class LayerNorm:

    def __init__(self, nc, ctx, sem, name, n, calls, minus_half, var_eps=EPS):
        self.nc, self.n, self.calls, self.minus_half = nc, n, calls, minus_half
        self.stats = ctx.enter_context(nc.sbuf_tensor(f"{name}_stats", [P, n, 6], F32))
        self.sums = ctx.enter_context(nc.sbuf_tensor(f"{name}_sums", [P, 3, n], F32))
        self.square = ctx.enter_context(nc.sbuf_tensor(f"{name}_square", [P, 2, n], F32))
        self.mean = ctx.enter_context(nc.sbuf_tensor(f"{name}_mean", [P, n], F32))
        self.ve = ctx.enter_context(nc.sbuf_tensor(f"{name}_ve", [P, n], F32))
        self.rstd = ctx.enter_context(nc.sbuf_tensor(f"{name}_rstd", [P, n], F32))
        self.var_ready, self.rstd_ready = sem(f"{name}_var_ready"), sem(f"{name}_rstd_ready")

    def variance(self, dve, b, call, chain, tile):
        nc = self.nc
        for j in range(self.n):
            last = nc.vector.bn_stats(self.stats[:, j, :], tile(j))
        chain.link(dve, b, last)
        st, sums, sq = self.stats, self.sums, self.square
        nc.vector.tensor_tensor(sums[:, 0, :], st[:, :, 1], st[:, :, 4], ALU.add)
        nc.vector.tensor_tensor(sums[:, 1, :], st[:, :, 1], st[:, :, 4], ALU.subtract)
        chain.link(dve, b, nc.vector.tensor_tensor(sums[:, 2, :], st[:, :, 2], st[:, :, 5], ALU.add))
        nc.vector.tensor_scalar(self.mean[:, :], sums[:, 0, :], 0.5, None, ALU.mult)
        nc.vector.scalar_tensor_tensor(out=sq[:, 0, :], in0=sums[:, 1, :], scalar=0.25,
                                       in1=sums[:, 1, :], op0=ALU.mult, op1=ALU.mult)
        chain.link(dve, b, nc.vector.tensor_scalar(sq[:, 1, :], sums[:, 2, :], 1.0 / D, EPS,
                                                   ALU.mult, ALU.add))
        nc.vector.tensor_tensor(self.ve[:, :], sq[:, 0, :], sq[:, 1, :],
                                ALU.add).then_inc(self.var_ready, 1)
        dve.wait_ge(self.rstd_ready, b * self.calls + call + 1)

    def power(self, pool, b, call):
        pool.wait_ge(self.var_ready, b * self.calls + call + 1)
        self.nc.gpsimd.tensor_tensor(self.rstd[:, :], self.ve[:, :], self.minus_half[:, 0:self.n],
                                     ALU.pow).then_inc(self.rstd_ready, 1)

    def apply(self, j, out, in_):
        return self.nc.vector.tensor_scalar(out, in_, self.mean[:, j:j + 1], self.rstd[:, j:j + 1],
                                            ALU.subtract, ALU.mult)


def softmax_layer(nc, ident, ident_bf, minus_half, x_rows, W_qkv, b_qkv, W_proj, b_proj, weight,
                  disha, x2_dram, rows_dram, y_dram):
    HG = H0 // 4
    HB = H0 // 8
    DV0 = DH0 + 1
    SEGS = [(i, 0, i * P) for i in range(4)] + [(i, 1, max(i * P, HALF)) for i in range(TT)]
    NSEG = len(SEGS)

    with ExitStack() as ctx:
        def sb(name, shape, dt=F32):
            return ctx.enter_context(nc.sbuf_tensor(name, shape, dt))

        def sem(name):
            return ctx.enter_context(nc.semaphore(name))

        psum_s = ctx.enter_context(nc.psum_tensor("a_scores", [P, 2, 2, HALF], F32))
        psum_g = ctx.enter_context(nc.psum_tensor("a_general", [P, 2, HALF], F32))
        psum_o = ctx.enter_context(nc.psum_tensor("a_attended", [P, 2, HALF], F32))

        w_qkv = sb("w_qkv", [P, CD, 3 * D])
        w_proj = sb("w_proj", [P, HG, D])
        w_ffn = sb("w_ffn", [P, CD, D])
        bias_qk = sb("bias_qk", [P, 2 * HB])
        bias_v = sb("bias_v", [P, D])
        bias_p = sb("bias_p", [P, D])
        mask_qk = sb("mask_qk", [P, P], BF16)
        mask_kq = sb("mask_kq", [P, P], BF16)
        spread = sb("spread", [P, P])
        x_in = sb("x_in", [P, TT, D])
        x_res = sb("x_res", [P, TT, D])
        xn = sb("xn", [P, TT, D])
        att = sb("att", [P, TT, D])
        yT = sb("yT", [P, HG, T])
        xnT = sb("xnT", [P, CD, T])
        qk_f = sb("qk_f", [P, 2, HALF])
        rest1 = sb("rest1", [P, HALF])
        one = sb("one", [P, 1])
        parts = sb("parts", [P, 2, 3, T], BF16)
        q_st = sb("q_st", [P, H0, T], BF16)
        k_st = sb("k_st", [P, H0, T], BF16)
        v_new = sb("v_new", [P, TT, D])
        v_aug = sb("v_aug", [P, TT, H0 * DV0 + 32 - DV0])
        mx = sb("mx", [P, HB, 8 * TT])
        nm = sb("nm", [8 * TT, HB, P])
        nm_rest = sb("nm_rest", [8 * TT, P])
        nm_parts = sb("nm_parts", [8 * TT, HB, 3, P], BF16)
        probs = sb("probs", [P, 2, 4, HALF])
        oT = sb("oT", [P, 2, HALF])
        rden = sb("rden", [P, HALF])
        zero = sb("zero", [P, D])

        load = sem("a_weights_loaded")
        prep = sem("a_cleared")
        made = sem("a_masks_made")
        turned = sem("a_weight_turned")
        filled = sem("a_constants_filled")
        w_raw = x_in[:, :, :].rearrange("p j d -> p (j d)")[:, 0:CD * 2 * D].rearrange(
            "p (c n) -> p c n", c=CD)
        weight_sb, disha_sb = att[:, 0:CD, :], att[:, CD, :]
        with nc.Block() as block:
            @block.sync
            def _(sp):
                w_view = W_qkv.rearrange("(c p) n -> p c n", p=P)
                sp.dma_start(w_raw, w_view[:, :, 0:2 * D]).then_inc(load, 16)
                sp.dma_start(w_qkv[:, :, 2 * D:3 * D], w_view[:, :, 2 * D:3 * D]).then_inc(load, 16)
                sp.dma_start(weight_sb, weight.rearrange("(c p) n -> p c n", p=P)).then_inc(load, 16)
                for a in range(2):
                    sp.dma_start(att[64 * a:64 * a + 64, CD, :], disha).then_inc(load, 16)
                sp.dma_start(bias_v[:, :], b_qkv[2 * D:3 * D].partition_broadcast(P)).then_inc(load, 16)
                sp.dma_start(bias_p[:, :], b_proj.partition_broadcast(P)).then_inc(load, 16)
                for n in range(2 * HB):
                    src = b_qkv[n * P:(n + 1) * P].rearrange("(h d) -> d h", d=DH0)
                    sp.dma_start(bias_qk[:, n:n + 1], src,
                                 allow_slow_non_contiguous=True).then_inc(load, 16)
                sp.wait_ge(prep, 1)
                for h in range(4):
                    src = W_proj.rearrange("(g h d) n -> h d g n", h=4, d=DH0)[h]
                    sp.dma_start(w_proj[32 * h:32 * h + DH0, :, :], src).then_inc(load, 16)
                sp.wait_ge(load, 16 * (7 + 2 * HB + 4))

            @block.vector
            def _(dve):
                nc.vector.memset(w_proj[:, :, :], 0.0).then_inc(prep, 1)
                nc.vector.memset(v_aug[:, :, :], 0.0).then_inc(filled, 1)
                nc.vector.memset(k_st[96:99, :, :], 1.0).then_inc(filled, 1)
                nc.vector.memset(zero[:, :], 0.0).then_inc(filled, 1)
                nc.vector.memset(one[:, :], 1.0).then_inc(filled, 1)
                dve.wait_ge(filled, 1)
                heads = v_aug[:, :, 0:H0 * DV0].rearrange("p j (h d) -> p j h d", d=DV0)
                nc.vector.memset(heads[:, :, :, DH0:DV0], 1.0).then_inc(filled, 1)
                dve.wait_ge(load, 16 * (7 + 2 * HB + 4))
                nc.vector.tensor_scalar(bias_qk[:, 0:HB], bias_qk[:, 0:HB], SCALE, None,
                                        ALU.mult).then_inc(filled, 1)
                for c in range(CD):
                    for n in range(2 * HB):
                        cols = slice(n * P, (n + 1) * P)
                        nc.vector.tensor_copy(
                            w_qkv[:, c, cols].rearrange("p (d h) -> p d h", d=DH0),
                            w_raw[:, c, cols].rearrange("p (h d) -> p d h", d=DH0)
                            ).then_inc(filled, 1)
                dve.wait_ge(turned, 1)
                for c in range(CD):
                    nc.vector.tensor_tensor(w_ffn[:, c, :], psum_g[:, c, 0:D], disha_sb,
                                            ALU.add).then_inc(filled, 1)
                dve.wait_ge(filled, 6 + 2 * HB * CD + CD)

            @block.gpsimd
            def _(pool):
                nc.gpsimd.memset(mask_qk[:, :], 0.0).then_inc(made, 1)
                nc.gpsimd.memset(mask_kq[:, :], 0.0).then_inc(made, 1)
                nc.gpsimd.memset(spread[:, :], 0.0).then_inc(made, 1)
                pool.wait_ge(made, 3)
                nc.gpsimd.affine_select(out=mask_qk[:, :], in_=mask_qk[:, :], compare_op=ALU.is_ge,
                                        fill=NEG, base=0, pattern=[[-1, P]],
                                        channel_multiplier=1).then_inc(made, 1)
                nc.gpsimd.affine_select(out=mask_kq[:, :], in_=mask_kq[:, :], compare_op=ALU.is_ge,
                                        fill=NEG, base=0, pattern=[[1, P]],
                                        channel_multiplier=-1).then_inc(made, 1)
                sp4 = spread[:, :].rearrange("p (g w) -> p g w", g=4)
                nc.gpsimd.affine_select(out=sp4, in_=sp4, compare_op=ALU.not_equal, fill=1.0,
                                        base=-DH0, pattern=[[-32, 4], [0, 32]],
                                        channel_multiplier=1).then_inc(made, 1)
                pool.wait_ge(made, 6)

            @block.tensor
            def _(pe):
                pe.wait_ge(load, 16 * (7 + 2 * HB + 4))
                for c in range(CD):
                    for o in range(CD):
                        last = nc.tensor.transpose(psum_g[:, c, o * P:(o + 1) * P],
                                                   weight_sb[:, o, c * P:(c + 1) * P], ident[:, :])
                last.then_inc(turned, 1)

        NS1 = HB * 8 * TT
        NK = HG * NSEG
        IN_MAXIMA = {1: ("P", 0), 2: ("P", 1), 3: ("P", 2), 4: ("P", 3), 6: ("LN", 1), 9: ("LN", 2),
                     14: ("T2", 0), 22: ("F", 0), 24: ("F", 1), 26: ("F", 2), 28: ("F", 3),
                     32: ("LN", 3)}
        IN_ATTEND = {1: ("LN", 0), 4: ("T1", 0), 6: ("QK", 0), 8: ("QK", 1), 10: ("QK", 2),
                     12: ("QK", 3), 14: ("V", 0), 16: ("V", 1), 18: ("V", 2), 20: ("V", 3),
                     34: ("QK", 4), 36: ("QK", 5), 38: ("QK", 6), 40: ("QK", 7)}
        HEAD_ALONE = [("LN", 0), ("T1", 0)] + [("QK", i) for i in range(8)] + [("V", i) for i in range(4)]
        TAIL = [IN_MAXIMA[i] for i in sorted(IN_MAXIMA)]

        def den_after(n):
            return {4: -1, 8: 0}.get(n)

        def turn_units(u0, with_head, with_tail):
            seq = []

            def stage(what):
                name, i = what
                seq.extend({"T1": [("T1", c) for c in range(4)], "T2": [("T2", c) for c in range(4)],
                            "LN": []}.get(name, [what]))
            for n in range(NS1):
                if with_tail and n in IN_MAXIMA:
                    stage(IN_MAXIMA[n])
                if n % (8 * TT) == 8 * TT - 1:
                    seq.append(("M", n // (8 * TT)))
            for k in range(NK):
                if with_head and k in IN_ATTEND:
                    stage(IN_ATTEND[k])
                d = den_after(k % NSEG)
                if d is not None and 2 * (k // NSEG) + d >= 0:
                    seq.append(("DEN", 2 * (k // NSEG) + d))
            seq.append(("DEN", 2 * HG - 1))
            return {what: u0 + i for i, what in enumerate(seq)}

        def alone(u0, names):
            return {what: u0 + i for i, what in enumerate(names)}

        H_UNITS = [("T1", c) for c in range(4)] + [w for w in HEAD_ALONE if w[0] in ("QK", "V")]
        T_UNITS = ([("P", i) for i in range(4)] + [("T2", c) for c in range(4)] +
                   [("F", i) for i in range(4)])
        U_ALL = 2 + 8 + len(H_UNITS) + len(T_UNITS)
        LEAD = len(H_UNITS)
        units_before = alone(0, H_UNITS)
        units_first = turn_units(LEAD, True, False)
        units_turn = turn_units(LEAD - len(T_UNITS), True, True)
        units_last = turn_units(LEAD - len(T_UNITS), False, True)
        units_after = alone(LEAD - len(T_UNITS) + U_ALL - LEAD, T_UNITS)

        G = Ring(sem, "a_general", 2, U_ALL)
        S = Ring(sem, "a_scores", 2, NS1 + NK * 2)
        attended_out = [sem(f"a_attended_out{s}") for s in range(2)]
        x_loaded = sem("a_x_loaded")
        res_loaded = sem("a_residual_loaded")
        x2_ready = sem("a_x2_ready")
        x2_stored = sem("a_x2_stored")
        head_norm = sem("a_head_norm_ready")
        tail_norm = sem("a_tail_norm_ready")
        split_done = sem("a_split_done")
        stacked = [sem("a_q_stacked"), sem("a_k_stacked")]
        nm_ready = sem("a_minus_max_ready")
        nm_placed = [sem(f"a_minus_max_placed{m}") for m in range(HB)]
        pv_done = sem("a_probs_used")
        yT_ready = sem("a_yT_ready")
        v_taken = sem("a_v_taken")
        zeroed = sem("a_rows_zeroed")
        chain_n = Chain(sem, "a_minus_max_chain", HB * 3)
        chain_h = Chain(sem, "a_head_chain", 3)
        chain_t = Chain(sem, "a_tail_chain", 3 * 3 + 3)
        pchain = Chain(sem, "a_pool_chain", 2 * HB * 2 * 3)
        ln_h = LayerNorm(nc, ctx, sem, "a_ln_head", TT, 1, minus_half)
        ln_t = LayerNorm(nc, ctx, sem, "a_ln_tail", TT, 3, minus_half)
        GROUP = 16 * len(QTERM)

        def turns(eng, turn, head, tail):
            for what in HEAD_ALONE:
                head(0, 0, units_before, what)
            turn(0, units_first, True, False)
            with eng.Fori(1, B - 1) as b:
                turn(b, units_turn, True, True)
            turn(B - 1, units_last, False, True)
            for what in TAIL:
                tail(B - 1, B - 1, units_after, what)

        with nc.Block() as block:
            @block.sync
            def _(sp):
                G.begin(sp)
                S.begin(sp)
                for s in attended_out:
                    sp.sem_inc(s, 1)
                sp.sem_inc(split_done, 2)
                sp.sem_inc(x2_stored, 16)
                sp.sem_inc(pv_done, 2)
                for s in stacked:
                    sp.sem_inc(s, GROUP)
                sp.sem_inc(head_norm, 1)
                xv, x2v = batch_view(x_rows), batch_view(x2_dram)
                zv = rows_dram.rearrange("(e b p) d -> b p e d", p=P, e=SLOTS // P // B)

                def load_x(b):
                    sp.wait_ge(head_norm, b + 1)
                    sp.dma_start(x_in[:, :, :], of_batch(xv, b)).then_inc(x_loaded, 16)

                def stack(b, m, used):
                    if used is not None:
                        sp.wait_ge(pv_done, used)
                    if m == 1:
                        sp.dma_start(zv[bass.ds(b, 1), :, :, :].rearrange("a p e d -> p (a e) d"),
                                     zero[:, :].rearrange("p (a d) -> p a d", a=1).broadcast_to(
                                         [P, SLOTS // P // B, D])).then_inc(zeroed, 16)
                    for qk, terms, st in ((0, QTERM, q_st), (1, KTERM, k_st)):
                        sp.wait_ge(split_done, b * 8 + 4 * m + 2 * qk + 2 + 2)
                        for t, part in enumerate(terms):
                            sp.dma_start(st[DH0 * t:DH0 * t + DH0, 8 * m:8 * m + 8, :],
                                         parts[:, qk, part, :]).then_inc(stacked[qk], 16)

                def store_x2(b):
                    sp.wait_ge(x2_ready, b + 1)
                    sp.dma_start(of_batch(x2v, b), x_res[:, :, :]).then_inc(x2_stored, 16)

                def turn(b, with_head, with_tail):
                    for m in range(HB):
                        sp.wait_ge(nm_ready, b * HB + m + 1)
                        for t in range(3):
                            sp.dma_start(q_st[KS + t:KS + t + 1, 8 * m:8 * m + 8, :],
                                         nm_parts[:, m, t, :]).then_inc(nm_placed[m], 16)
                        if m == 0 and with_tail:
                            store_x2(b - 1)
                    sp.wait_ge(x2_stored, b * 16 + 16)
                    sp.dma_start(x_res[:, :, :], of_batch(xv, b)).then_inc(res_loaded, 16)
                    if with_head:
                        for m in range(HB):
                            stack(b + 1, m, b * NK + (m + 1) * (NK // 2) + 2)
                            if m == 0:
                                load_x(b + 2)

                load_x(0)
                stack(0, 0, None)
                load_x(1)
                stack(0, 1, None)
                turn(0, True, False)
                with sp.Fori(1, B - 2) as b:
                    turn(b, True, True)
                b = B - 2
                for m in range(HB):
                    sp.wait_ge(nm_ready, b * HB + m + 1)
                    for t in range(3):
                        sp.dma_start(q_st[KS + t:KS + t + 1, 8 * m:8 * m + 8, :],
                                     nm_parts[:, m, t, :]).then_inc(nm_placed[m], 16)
                    if m == 0:
                        store_x2(b - 1)
                sp.wait_ge(x2_stored, b * 16 + 16)
                sp.dma_start(x_res[:, :, :], of_batch(xv, b)).then_inc(res_loaded, 16)
                for m in range(HB):
                    stack(b + 1, m, b * NK + (m + 1) * (NK // 2) + 2)
                turn(B - 1, False, True)
                store_x2(B - 1)
                sp.wait_ge(x2_stored, B * 16 + 16)
                sp.dma_start(y_dram[SLOTS:SLOTS + P, :], zero[:, :]).then_inc(zeroed, 16)
                sp.wait_ge(zeroed, 16 * (B + 1))

            @block.tensor
            def _(pe):
                def turn_norm(r, U, name):
                    for half in range(2):
                        for c in range(CD):
                            u = U[name, half * CD + c]
                            G.wait_free(pe, r, u)
                            for j in range(4):
                                last = nc.tensor.transpose(
                                    psum_g[:, G.slot(u), j * P:(j + 1) * P],
                                    xn[:, half * 4 + j, c * P:(c + 1) * P], ident[:, :])
                            last.then_inc(G.full[G.slot(u)], 1)

                def two_tiles(r, u, i, lhs, rhs, nk):
                    G.wait_free(pe, r, u)
                    for jj in range(2):
                        j = 2 * i + jj
                        for c in range(nk):
                            last = nc.tensor.matmul(psum_g[:, G.slot(u), jj * D:(jj + 1) * D],
                                                    lhs[:, c, j * P:(j + 1) * P], rhs[:, c, :],
                                                    start=(c == 0), stop=(c == nk - 1))
                    last.then_inc(G.full[G.slot(u)], 1)

                def head(b, r, U, what):
                    name, i = what
                    if name == "T1":
                        pe.wait_ge(head_norm, b + 2)
                        turn_norm(r, U, "T1")
                    elif name == "QK":
                        m, qk, half = i // 4, i // 2 % 2, i % 2
                        u = U[what]
                        if i == 0:
                            for c in (2, 3):
                                G.wait_evacuated(pe, r, U["T1", c])
                        G.wait_free(pe, r, u)
                        for c in range(CD):
                            last = nc.tensor.matmul(psum_g[:, G.slot(u), :],
                                                    w_qkv[:, c, qk * D + m * P:qk * D + (m + 1) * P],
                                                    xnT[:, c, half * HALF:(half + 1) * HALF],
                                                    start=(c == 0), stop=(c == CD - 1))
                        last.then_inc(G.full[G.slot(u)], 1)
                    elif name == "V":
                        two_tiles(r, U[what], i, xnT, w_qkv[:, :, 2 * D:3 * D], CD)

                def tail(b, r, U, what):
                    name, i = what
                    if name == "P":
                        if i == 0:
                            pe.wait_ge(yT_ready, b * 2 * HG + 2 * HG)
                        two_tiles(r, U[what], i, yT, w_proj, HG)
                    elif name == "T2":
                        pe.wait_ge(tail_norm, b + 1)
                        turn_norm(r, U, "T2")
                    elif name == "F":
                        if i == 0:
                            for c in (2, 3):
                                G.wait_evacuated(pe, r, U["T2", c])
                        two_tiles(r, U[what], i, xnT, w_ffn, CD)

                def maxima(b, U, with_tail):
                    for n in range(NS1):
                        if with_tail and n in IN_MAXIMA:
                            tail(b - 1, b, U, IN_MAXIMA[n])
                        m, h8, j = n // (8 * TT), n // TT % 8, n % TT
                        h = 8 * m + h8
                        if n % (8 * TT) == 0:
                            for st in stacked:
                                pe.wait_ge(st, b * (HB * GROUP) + (m + 2) * GROUP)
                        S.wait_free(pe, b, n)
                        s = psum_s[:, S.slot(n), :, :].rearrange("p a n -> p (a n)")
                        w = (j + 1) * P
                        for k0 in range(0, w, HALF):
                            k1 = min(k0 + HALF, w)
                            nc.tensor.matmul(s[:, k0:k1], q_st[0:KS, h, j * P:(j + 1) * P],
                                             k_st[0:KS, h, k0:k1], start=True, stop=False,
                                             skip_group_check=True)
                        nc.tensor.matmul(s[:, j * P:w], ident_bf[:, :], mask_qk[:, :],
                                         start=False, stop=True, skip_group_check=True
                                         ).then_inc(S.full[S.slot(n)], 1)
                        if n % (8 * TT) == 8 * TT - 1:
                            S.wait_evacuated(pe, b, n)
                            u = U["M", m]
                            G.wait_free(pe, b, u)
                            nc.tensor.matmul(psum_g[0:8 * TT, G.slot(u), 0:P], mx[:, m, :],
                                             ident[:, :], start=True, stop=True
                                             ).then_inc(G.full[G.slot(u)], 1)

                def values(b, k):
                    hg, (i, half, q0) = k // NSEG, SEGS[k % NSEG]
                    w = (half + 1) * HALF - q0
                    v = hg * 2 + half
                    if i == 0:
                        pe.wait_ge(attended_out[v % 2], b * HG + v // 2 + 1)
                    for pair in range(2):
                        S.wait_evacuated(pe, b, NS1 + k * 2 + pair)
                    for h4 in range(4):
                        h = hg * 4 + h4
                        last = nc.tensor.matmul(
                            psum_o[32 * h4:32 * h4 + 32, v % 2, q0 - half * HALF:HALF],
                            v_aug[:, i, h * DV0:h * DV0 + 32], probs[:, k % 2, h4, 0:w],
                            start=(i == 0), stop=True, skip_group_check=True)
                    last.then_inc(pv_done, 1)

                def denominators(b, U, v):
                    u = U["DEN", v]
                    pe.wait_ge(attended_out[v % 2], b * HG + v // 2 + 2)
                    G.wait_free(pe, b, u)
                    nc.tensor.matmul(psum_g[:, G.slot(u), :], spread[:, :], oT[:, v % 2, :],
                                     start=True, stop=True).then_inc(G.full[G.slot(u)], 1)

                def attend(b, U, with_head):
                    pe.wait_ge(v_taken, b + 1)
                    for k in range(NK):
                        if with_head and k in IN_ATTEND:
                            head(b + 1, b, U, IN_ATTEND[k])
                        hg, n = k // NSEG, k % NSEG
                        i, half, q0 = SEGS[n]
                        if n == 0 and hg % 2 == 0:
                            pe.wait_ge(nm_placed[hg // 2], b * 48 + 48)
                        w = (half + 1) * HALF - q0
                        diagonal = q0 == i * P
                        for pair in range(2):
                            u = NS1 + k * 2 + pair
                            S.wait_free(pe, b, u)
                            for p2 in range(2):
                                h = hg * 4 + pair * 2 + p2
                                s = psum_s[:, S.slot(u), p2, :]
                                last = nc.tensor.matmul(
                                    s[:, 0:w], k_st[0:KM, h, i * P:(i + 1) * P],
                                    q_st[0:KM, h, q0:q0 + w], start=True, stop=not diagonal,
                                    skip_group_check=True)
                                if diagonal:
                                    last = nc.tensor.matmul(s[:, 0:P], ident_bf[:, :],
                                                            mask_kq[:, :], start=False, stop=True,
                                                            skip_group_check=True)
                            last.then_inc(S.full[S.slot(u)], 1)
                        if k > 0:
                            values(b, k - 1)
                        d = den_after(n)
                        if d is not None and 2 * hg + d >= 0:
                            denominators(b, U, 2 * hg + d)
                    values(b, NK - 1)
                    denominators(b, U, 2 * HG - 1)

                def turn(b, U, with_head, with_tail):
                    maxima(b, U, with_tail)
                    attend(b, U, with_head)

                turns(pe, turn, head, tail)

            @block.scalar
            def _(act):
                def turned(r, U, name):
                    for half in range(2):
                        for c in range(CD):
                            u = U[name, half * CD + c]
                            G.wait_full(act, r, u)
                            nc.scalar.copy(xnT[:, c, half * HALF:(half + 1) * HALF],
                                           psum_g[:, G.slot(u), :]).then_inc(G.evacuated[G.slot(u)], 1)

                def head(b, r, U, what):
                    name, i = what
                    if name == "T1":
                        turned(r, U, "T1")
                    elif name == "QK":
                        u = U[what]
                        qk, m = i // 2 % 2, i // 4
                        G.wait_full(act, r, u)
                        act.wait_ge(split_done, b * 8 + i + 1)
                        nc.scalar.activation(qk_f[:, i % 2, :], psum_g[:, G.slot(u), :], ACT.Identity,
                                             bias=bias_qk[:, qk * HB + m:qk * HB + m + 1],
                                             scale=SCALE if qk == 0 else 1.0
                                             ).then_inc(G.evacuated[G.slot(u)], 1)

                def tail(b, r, U, what):
                    if what[0] == "T2":
                        turned(r, U, "T2")

                def turn(b, U, with_head, with_tail):
                    if with_tail:
                        for what in TAIL:
                            tail(b - 1, b, U, what)
                    for k in range(NK):
                        if with_head and k in IN_ATTEND:
                            head(b + 1, b, U, IN_ATTEND[k])
                        i, half, q0 = SEGS[k % NSEG]
                        w = (half + 1) * HALF - q0
                        act.wait_ge(pv_done, b * NK + k + 1)
                        for pair in range(2):
                            u = NS1 + k * 2 + pair
                            S.wait_full(act, b, u)
                            nc.scalar.activation(probs[:, k % 2, 2 * pair:2 * pair + 2, 0:w],
                                                 psum_s[:, S.slot(u), :, 0:w],
                                                 ACT.Exp).then_inc(S.evacuated[S.slot(u)], 1)

                turns(act, turn, head, tail)

            @block.gpsimd
            def _(pool):
                ones = one[:, :].broadcast_to([P, HALF])

                def head(b, r, U, what):
                    name, i = what
                    if name == "LN":
                        ln_h.power(pool, b, 0)
                    elif name == "QK":
                        qk, m, half = i // 2 % 2, i // 4, i % 2
                        cols = slice(half * HALF, (half + 1) * HALF)
                        G.wait_evacuated(pool, r, U[what])
                        if half == 0:
                            pool.wait_ge(stacked[qk], b * (HB * GROUP) + (m + 1) * GROUP)
                        f = qk_f[:, i % 2, :]
                        pchain.at = 3 * i
                        pchain.link(pool, b, nc.gpsimd.tensor_tensor(parts[:, qk, 0, cols], f, ones,
                                                                     ALU.mult))
                        pchain.link(pool, b, nc.gpsimd.tensor_tensor(rest1[:, :], f, parts[:, qk, 0, cols],
                                                                     ALU.subtract))
                        pchain.link(pool, b, nc.gpsimd.tensor_tensor(parts[:, qk, 1, cols], rest1[:, :],
                                                                     ones, ALU.mult))
                        nc.gpsimd.tensor_tensor(parts[:, qk, 2, cols], rest1[:, :],
                                                parts[:, qk, 1, cols],
                                                ALU.subtract).then_inc(split_done, 1)
                        pool.wait_ge(split_done, b * 8 + i + 3)

                def tail(b, r, U, what):
                    if what[0] == "LN":
                        ln_t.power(pool, b, what[1] - 1)

                def turn(b, U, with_head, with_tail):
                    if with_tail:
                        for what in TAIL:
                            tail(b - 1, b, U, what)
                    if with_head:
                        for k in sorted(IN_ATTEND):
                            head(b + 1, b, U, IN_ATTEND[k])

                turns(pool, turn, head, tail)

            @block.vector
            def _(dve):
                def head(b, r, U, what):
                    name, i = what
                    if name == "LN":
                        dve.wait_ge(x_loaded, b * 16 + 16)
                        chain_h.at = 0
                        ln_h.variance(dve, b, 0, chain_h, lambda j: x_in[:, j, :])
                        for j in range(TT):
                            last = ln_h.apply(j, xn[:, j, :], x_in[:, j, :])
                        last.then_inc(head_norm, 1)
                    elif name == "V":
                        u = U[what]
                        G.wait_full(dve, r, u)
                        nc.vector.tensor_tensor(
                            v_new[:, 2 * i:2 * i + 2, :],
                            psum_g[:, G.slot(u), :].rearrange("p (j n) -> p j n", j=2),
                            bias_v[:, :].rearrange("p (a n) -> p a n", a=1).broadcast_to([P, 2, D]),
                            ALU.add).then_inc(G.evacuated[G.slot(u)], 1)

                def tail(b, r, U, what):
                    name, i = what
                    if name == "P":
                        u = U[what]
                        G.wait_full(dve, r, u)
                        nc.vector.tensor_tensor(
                            att[:, 2 * i:2 * i + 2, :],
                            psum_g[:, G.slot(u), :].rearrange("p (j d) -> p j d", j=2),
                            bias_p[:, :].rearrange("p (a d) -> p a d", a=1).broadcast_to([P, 2, D]),
                            ALU.add).then_inc(G.evacuated[G.slot(u)], 1)
                    elif name == "F":
                        u = U[what]
                        G.wait_full(dve, r, u)
                        nc.vector.tensor_copy(att[:, 2 * i:2 * i + 2, :],
                                              psum_g[:, G.slot(u), :].rearrange("p (j d) -> p j d", j=2)
                                              ).then_inc(G.evacuated[G.slot(u)], 1)
                    elif name == "LN" and i in (1, 3):
                        """x_res += LN(att)"""
                        for n in (2, 3):
                            G.wait_evacuated(dve, r, U["P" if i == 1 else "F", n])
                        if i == 1:
                            dve.wait_ge(res_loaded, b * 16 + 16)
                        chain_t.at = 0 if i == 1 else 8
                        ln_t.variance(dve, b, i - 1, chain_t, lambda j: att[:, j, :])
                        for j in range(TT):
                            last = ln_t.apply(j, att[:, j, :], att[:, j, :])
                        chain_t.link(dve, b, last)
                        last = nc.vector.tensor_tensor(x_res[:, :, :], x_res[:, :, :], att[:, :, :],
                                                       ALU.add)
                        if i == 1:
                            chain_t.link(dve, b, last)
                        else:
                            last.then_inc(x2_ready, 1)
                    elif name == "LN":
                        ln_t.variance(dve, b, 1, chain_t, lambda j: x_res[:, j, :])
                        for j in range(TT):
                            last = ln_t.apply(j, xn[:, j, :], x_res[:, j, :])
                        last.then_inc(tail_norm, 1)

                def maxima(b, U, with_tail):
                    for n in range(NS1):
                        if with_tail and n in IN_MAXIMA:
                            tail(b - 1, b, U, IN_MAXIMA[n])
                        m, w = n // (8 * TT), (n % TT + 1) * P
                        S.wait_full(dve, b, n)
                        s = psum_s[:, S.slot(n), :, :].rearrange("p a n -> p (a n)")
                        nc.vector.tensor_reduce(mx[:, m, n % (8 * TT):n % (8 * TT) + 1], s[:, 0:w],
                                                AX.X, ALU.max).then_inc(S.evacuated[S.slot(n)], 1)
                        if n % (8 * TT) < 8 * TT - 1:
                            continue
                        u = U["M", m]
                        G.wait_full(dve, b, u)
                        f = nm[:, m, :]
                        nc.vector.tensor_scalar(f, psum_g[0:8 * TT, G.slot(u), 0:P], -1.0, None,
                                                ALU.mult).then_inc(G.evacuated[G.slot(u)], 1)
                        G.wait_evacuated(dve, b, u)
                        chain_n.at = 3 * m
                        chain_n.link(dve, b, nc.vector.tensor_copy(nm_parts[:, m, 0, :], f))
                        chain_n.link(dve, b, nc.vector.tensor_tensor(nm_rest[:, :], f, nm_parts[:, m, 0, :],
                                                                     ALU.subtract))
                        chain_n.link(dve, b, nc.vector.tensor_copy(nm_parts[:, m, 1, :], nm_rest[:, :]))
                        nc.vector.tensor_tensor(nm_parts[:, m, 2, :], nm_rest[:, :],
                                                nm_parts[:, m, 1, :],
                                                ALU.subtract).then_inc(nm_ready, 1)

                def copy_out(b, v):
                    dve.wait_ge(pv_done, b * NK + v // 2 * NSEG + (4, NSEG)[v % 2] + 2)
                    nc.vector.tensor_copy(oT[:, v % 2, :], psum_o[:, v % 2, :]
                                          ).then_inc(attended_out[v % 2], 1)
                    dve.wait_ge(attended_out[v % 2], b * HG + v // 2 + 2)

                def normalise(b, U, v):
                    hg, half = v // 2, v % 2
                    u = U["DEN", v]
                    G.wait_full(dve, b, u)
                    nc.vector.reciprocal(rden[:, :], psum_g[:, G.slot(u), :]
                                         ).then_inc(G.evacuated[G.slot(u)], 1)
                    G.wait_evacuated(dve, b, u)
                    nc.vector.tensor_tensor(
                        yT[:, hg, half * HALF:(half + 1) * HALF], oT[:, v % 2, :], rden[:, :],
                        ALU.mult).then_inc(yT_ready, 1)
                    dve.wait_ge(yT_ready, b * 2 * HG + v + 1)

                def turn(b, U, with_head, with_tail):
                    maxima(b, U, with_tail)
                    nc.vector.tensor_copy(
                        v_aug[:, :, 0:H0 * DV0].rearrange("p j (h d) -> p j h d", d=DV0)[:, :, :, 0:DH0],
                        v_new[:, :, :].rearrange("p j (h d) -> p j h d", d=DH0)
                        ).then_inc(v_taken, 1)
                    dve.wait_ge(v_taken, b + 1)
                    for k in range(NK):
                        if with_head and k in IN_ATTEND:
                            head(b + 1, b, U, IN_ATTEND[k])
                        hg, n = k // NSEG, k % NSEG
                        if n == 5:
                            copy_out(b, 2 * hg)
                        if n == 1 and hg > 0:
                            copy_out(b, 2 * hg - 1)
                        d = den_after(n)
                        if d is not None and 2 * hg + d >= 0:
                            normalise(b, U, 2 * hg + d)
                    copy_out(b, 2 * HG - 1)
                    normalise(b, U, 2 * HG - 1)

                turns(dve, turn, head, tail)


def linear_layer(nc, ident, minus_half, x2_dram, g1, be1, Wq, Wk, Wv, Wo, g2, be2, Wf1, Wf2, Wg,
                 x3_dram, xf_dram, logits):
    NP = H1 // 2
    NG = H1 // 4
    ME = E1 // P
    assert SUP == 2
    NGR = B * SUP
    NCH = G4 * NG
    NQK = 2 * NP
    OWN = [("QK", NQK), ("KT", 8), ("O", 8), ("W", 2), ("T2", CD), ("F1", MF), ("F2", 2)]
    OF_NEXT = [("T1", CD), ("V", 8)]
    OF_LAST = [("T3", CD), ("L", 2)]
    ORDER = OWN[0:1] + OF_LAST + OWN[1:4] + OF_NEXT + OWN[4:]
    N_NEXT, N_ALL = sum(n for _, n in OF_NEXT), sum(n for _, n in ORDER)
    N_LAST = sum(n for _, n in OF_LAST)

    def units(u0, stages):
        where = {}
        for name, n in stages:
            where[name] = u0
            u0 += n
        return where

    units_before = units(0, OF_NEXT)
    units_first = units(N_NEXT, [s for s in ORDER if s not in OF_LAST])
    BASE = N_NEXT - N_LAST
    units_group = units(BASE, ORDER)
    units_last = units(BASE, [s for s in ORDER if s not in OF_NEXT])
    units_after = units(BASE + N_ALL - N_NEXT, OF_LAST)

    with ExitStack() as ctx:
        def sb(name, shape, dt=F32):
            return ctx.enter_context(nc.sbuf_tensor(name, shape, dt))

        def sem(name):
            return ctx.enter_context(nc.semaphore(name))

        R = 3
        psum_g = ctx.enter_context(nc.psum_tensor("l_general", [P, R, HALF], F32))
        psum_a = ctx.enter_context(nc.psum_tensor("l_scores", [P, 2, HALF], F32))
        psum_n = ctx.enter_context(nc.psum_tensor("l_num", [P, 2, HALF], F32))
        psum_u = ctx.enter_context(nc.psum_tensor("l_update", [P, HALF], F32))

        wq = sb("l_wq", [P, CD, E1])
        wk = sb("l_wk", [P, CD, E1])
        wv = sb("l_wv", [P, CD, E1])
        wo = sb("l_wo", [P, ME, D])
        wf1 = sb("l_wf1", [P, CD, DF])
        wf2 = sb("l_wf2", [P, MF, D])
        wg = sb("l_wg", [P, CD, E])
        affine = sb("l_affine", [P, CD, 4])
        keep = sb("l_keep", [P, P])
        x2 = sb("l_x2", [P, 2, G4, D])
        a3 = sb("l_a3", [P, 2, G4, D])
        norm1 = sb("l_norm1", [P, G4, D])
        norm2 = sb("l_norm2", [P, G4, D])
        nT1 = sb("l_nT1", [P, CD, HALF])
        nT2 = sb("l_nT2", [P, CD, HALF])
        qT = sb("l_qT", [P, NP, HALF])
        kT = sb("l_kT", [P, NP, HALF])
        kt = sb("l_k", [P, G4, E1])
        v_aug = sb("l_v", [P, G4, H1, DV])
        state = sb("l_state", [P, NP, 2 * DV])
        ex = sb("l_exp", [P, 2, HALF])
        scores = sb("l_scores_kept", [P, 2, 2, 4, P])
        den = sb("l_den", [P, 2, 4])
        o = sb("l_o", [P, 2, E1])
        oT = sb("l_oT", [P, ME, HALF])
        hT = qT

        load = sem("l_weights_loaded")
        made = sem("l_mask_made")
        filled = sem("l_constants_filled")
        n_load = 7 + 4
        with nc.Block() as block:
            @block.sync
            def _(sp):
                for dst, w in ((wq, Wq), (wk, Wk), (wv, Wv), (wo, Wo), (wf1, Wf1), (wf2, Wf2), (wg, Wg)):
                    sp.dma_start(dst[:, :, :], w.rearrange("(c p) n -> p c n", p=P)).then_inc(load, 16)
                for n, w in enumerate((g1, be1, g2, be2)):
                    sp.dma_start(affine[:, :, n], w.rearrange("(c p) -> p c", p=P),
                                 allow_slow_non_contiguous=True).then_inc(load, 16)
                sp.wait_ge(load, 16 * n_load)

            @block.gpsimd
            def _(pool):
                nc.gpsimd.memset(keep[:, :], 1.0).then_inc(made, 1)
                pool.wait_ge(made, 1)
                nc.gpsimd.affine_select(out=keep[:, :], in_=keep[:, :], compare_op=ALU.is_ge,
                                        fill=0.0, base=0, pattern=[[1, P]],
                                        channel_multiplier=-1).then_inc(made, 1)
                nc.gpsimd.memset(state[:, :, :], 0.0).then_inc(made, 1)
                pool.wait_ge(made, 3)

            @block.vector
            def _(dve):
                nc.vector.memset(v_aug[:, :, :, DH1:DV], 1.0).then_inc(filled, 1)
                dve.wait_ge(filled, 1)

        G = Ring(sem, "l_general", R, N_ALL)
        A = Ring(sem, "l_scores", 2, NCH)
        NUM = Ring(sem, "l_num", 2, NCH)
        UP = Ring(sem, "l_update", 1, NCH)
        x2_loaded = [sem(f"l_x2_loaded{i}") for i in range(2)]
        x3_ready = sem("l_x3_ready")
        xf_ready = sem("l_xf_ready")
        x3_stored = sem("l_x3_stored")
        xf_stored = sem("l_xf_stored")
        norm1_ready = sem("l_norm1_ready")
        norm2_ready = sem("l_norm2_ready")
        ex_negated = sem("l_exp_negated")
        ex_ready = sem("l_exp_ready")
        cleared = sem("l_state_cleared")
        den_chain = Chain(sem, "l_den_chain", 2 * NCH)
        chain1 = Chain(sem, "l_norm1_chain", 7)
        chain2 = Chain(sem, "l_norm2_chain", 3)
        chain3 = Chain(sem, "l_norm3_chain", 7)
        ln1 = LayerNorm(nc, ctx, sem, "l_ln1", G4, 2, minus_half)
        ln2 = LayerNorm(nc, ctx, sem, "l_ln2", G4, 1, minus_half)
        ln3 = LayerNorm(nc, ctx, sem, "l_ln3", G4, 2, minus_half)

        def group_view(dram):
            return dram.rearrange("(g j p) d -> g p j d", p=P, j=G4)

        def of_group(view, g):
            return view[bass.ds(g, 1), :, :, :].rearrange("a p j d -> p (a j) d")

        def groups(eng, group):
            group(0, 0, 0, units_first, True, False)
            with eng.Fori(0, B - 1) as t:
                group(t * 2 + 1, t, 1, units_group, False, False)
                group(t * 2 + 2, t + 1, 0, units_group, False, False)
            group(NGR - 1, B - 1, 1, units_last, False, True)

        with nc.Block() as block:
            @block.sync
            def _(sp):
                for ring in (G, A, NUM, UP):
                    ring.begin(sp)
                sp.sem_inc(cleared, 1)
                x2v, x3v, xfv = group_view(x2_dram), group_view(x3_dram), group_view(xf_dram)

                def store(g, s):
                    sp.wait_ge(x3_ready, g + 1)
                    sp.dma_start(of_group(x3v, g), x2[:, s, :, :]).then_inc(x3_stored, 16)
                    sp.wait_ge(xf_ready, g + 1)
                    sp.dma_start(of_group(xfv, g), norm2[:, :, :]).then_inc(xf_stored, 16)

                def group(g, b, s, U, first, last):
                    if first:
                        for n in range(2):
                            sp.dma_start(x2[:, n, :, :], of_group(x2v, n)).then_inc(x2_loaded[n], 16)
                        return
                    store(g - 1, 1 - s)
                    if not last:
                        sp.wait_ge(x3_stored, g * 16)
                        sp.dma_start(x2[:, 1 - s, :, :], of_group(x2v, g + 1)).then_inc(x2_loaded[1 - s], 16)

                groups(sp, group)
                store(NGR - 1, 1)
                sp.wait_ge(x3_stored, NGR * 16)
                sp.wait_ge(xf_stored, NGR * 16)

            @block.tensor
            def _(pe):
                def turn(g, u0, norm):
                    for c in range(CD):
                        u = u0 + c
                        G.wait_free(pe, g, u)
                        for j in range(G4):
                            last = nc.tensor.transpose(psum_g[:, G.slot(u), j * P:(j + 1) * P],
                                                       norm[:, j, c * P:(c + 1) * P], ident[:, :])
                        last.then_inc(G.full[G.slot(u)], 1)

                def by_feature(g, u, w, cols, nT):
                    G.wait_free(pe, g, u)
                    for c in range(CD):
                        last = nc.tensor.matmul(psum_g[:, G.slot(u), :], w[:, c, cols], nT[:, c, :],
                                                start=(c == 0), stop=(c == CD - 1))
                    last.then_inc(G.full[G.slot(u)], 1)

                def two_tiles(g, u, i, lhs, rhs, nk):
                    G.wait_free(pe, g, u)
                    for jj in range(2):
                        j = 2 * i + jj
                        for k in range(nk):
                            last = nc.tensor.matmul(psum_g[:, G.slot(u), jj * D:(jj + 1) * D],
                                                    lhs[:, k, j * P:(j + 1) * P], rhs[:, k, :],
                                                    start=(k == 0), stop=(k == nk - 1))
                    last.then_inc(G.full[G.slot(u)], 1)

                def score(g, d):
                    j = d // 2
                    cols = slice(j * P, (j + 1) * P)
                    for h2 in range(2):
                        A.wait_free(pe, g, 2 * d + h2)
                    for i in range(4):
                        for h2 in range(2):
                            p, rows = d % 2 * 4 + i, slice(64 * h2, 64 * h2 + 64)
                            last = nc.tensor.matmul(psum_a[:, h2, i * P:(i + 1) * P],
                                                    kT[rows, p, cols], qT[rows, p, cols],
                                                    start=True, stop=True)
                            if i == 3:
                                last.then_inc(A.full[h2], 1)

                def turn_o(g, U, j):
                    NUM.wait_evacuated(pe, g, j * NG + NG - 1)
                    for half in range(2):
                        u = U["O"] + 2 * j + half
                        G.wait_free(pe, g, u)
                        for m in range(4):
                            last = nc.tensor.transpose(psum_g[:, G.slot(u), m * P:(m + 1) * P],
                                                       o[:, j % 2, (4 * half + m) * P:(4 * half + m + 1) * P],
                                                       ident[:, :])
                        last.then_inc(G.full[G.slot(u)], 1)

                def begin_next(r, g, U):
                    pe.wait_ge(norm1_ready, g + 1)
                    turn(r, U["T1"], norm1)
                    for c in range(CD):
                        G.wait_evacuated(pe, r, U["T1"] + c)
                    for j in range(G4):
                        for half in range(2):
                            u = U["V"] + 2 * j + half
                            G.wait_free(pe, r, u)
                            for c in range(CD):
                                last = nc.tensor.matmul(psum_g[:, G.slot(u), :],
                                                        nT1[:, c, j * P:(j + 1) * P],
                                                        wv[:, c, half * HALF:(half + 1) * HALF],
                                                        start=(c == 0), stop=(c == CD - 1))
                            last.then_inc(G.full[G.slot(u)], 1)

                def end_last(r, g, U):
                    pe.wait_ge(xf_ready, g + 1)
                    turn(r, U["T3"], norm2)
                    for c in range(CD):
                        G.wait_evacuated(pe, r, U["T3"] + c)
                    for i in range(2):
                        u = U["L"] + i
                        G.wait_free(pe, r, u)
                        for jj in range(2):
                            j = 2 * i + jj
                            for c in range(CD):
                                last = nc.tensor.matmul(psum_g[:, G.slot(u), jj * E:(jj + 1) * E],
                                                        nT2[:, c, j * P:(j + 1) * P], wg[:, c, :],
                                                        start=(c == 0), stop=(c == CD - 1))
                        last.then_inc(G.full[G.slot(u)], 1)

                def group(g, b, s, U, first, last_group):
                    for i in range(NQK):
                        by_feature(g, U["QK"] + i, wq if i < NP else wk,
                                   slice(i % NP * P, (i % NP + 1) * P), nT1)
                    if first:
                        for u in range(U["QK"] + NQK - R, U["QK"] + NQK):
                            G.wait_evacuated(pe, g, u)
                    else:
                        end_last(g, g - 1, U)
                    for j in range(G4):
                        for half in range(2):
                            u = U["KT"] + 2 * j + half
                            G.wait_free(pe, g, u)
                            for m in range(4):
                                last = nc.tensor.transpose(psum_g[:, G.slot(u), m * P:(m + 1) * P],
                                                           kT[:, 4 * half + m, j * P:(j + 1) * P],
                                                           ident[:, :])
                            last.then_inc(G.full[G.slot(u)], 1)
                    score(g, 0)
                    for u in range(U["O"] - R, U["O"]):
                        G.wait_evacuated(pe, g, u)
                    if s == 0:
                        pe.wait_ge(cleared, b + 1)
                    for n in range(NCH):
                        j, g4, d = n // NG, n % NG, n // 2
                        if n % 2 == 0 and d + 1 < NCH // 2:
                            score(g, d + 1)
                        NUM.wait_free(pe, g, n)
                        if n % 2 == 0:
                            for h2 in range(2):
                                A.wait_evacuated(pe, g, 2 * d + h2)
                        for p2 in range(2):
                            p = 2 * g4 + p2
                            nc.tensor.matmul(psum_n[:, NUM.slot(n), p2 * 2 * DV:(p2 + 1) * 2 * DV],
                                             qT[:, p, j * P:(j + 1) * P], state[:, p, :],
                                             start=True, stop=False, skip_group_check=True)
                            for h2 in range(2):
                                h4 = 2 * p2 + h2
                                last = nc.tensor.matmul(
                                    psum_n[:, NUM.slot(n), h4 * DV:(h4 + 1) * DV],
                                    scores[:, d % 2, h2, p % 4, :], v_aug[:, j, 4 * g4 + h4, :],
                                    start=False, stop=True, skip_group_check=True)
                        last.then_inc(NUM.full[NUM.slot(n)], 1)
                        UP.wait_free(pe, g, n)
                        for p2 in range(2):
                            p = 2 * g4 + p2
                            last = nc.tensor.matmul(psum_u[:, p2 * 2 * DV:(p2 + 1) * 2 * DV],
                                                    kt[:, j, p * P:(p + 1) * P],
                                                    v_aug[:, j, 2 * p:2 * p + 2, :],
                                                    start=True, stop=True)
                        last.then_inc(UP.full[0], 1)
                        if g4 == 1 and j > 0:
                            turn_o(g, U, j - 1)
                    turn_o(g, U, G4 - 1)
                    for u in range(U["O"] + 8 - R, U["O"] + 8):
                        G.wait_evacuated(pe, g, u)
                    for i in range(2):
                        two_tiles(g, U["W"] + i, i, oT, wo, ME)
                    if not last_group:
                        begin_next(g, g + 1, U)
                    pe.wait_ge(norm2_ready, g + 1)
                    turn(g, U["T2"], norm2)
                    for c in range(CD):
                        G.wait_evacuated(pe, g, U["T2"] + c)
                    for m in range(MF):
                        by_feature(g, U["F1"] + m, wf1, slice(m * P, (m + 1) * P), nT2)
                    for u in range(U["F2"] - R, U["F2"]):
                        G.wait_evacuated(pe, g, u)
                    for i in range(2):
                        two_tiles(g, U["F2"] + i, i, hT, wf2, MF)

                begin_next(0, 0, units_before)
                groups(pe, group)
                end_last(NGR - 1, NGR - 1, units_after)

            @block.scalar
            def _(act):
                def turned(r, u0, nT, n):
                    for c in range(CD):
                        u = u0 + c
                        G.wait_full(act, r, u)
                        if n is None:
                            ins = nc.scalar.copy(nT[:, c, :], psum_g[:, G.slot(u), :])
                        else:
                            ins = nc.scalar.activation(nT[:, c, :], psum_g[:, G.slot(u), :], ACT.Identity,
                                                       bias=affine[:, c, n + 1:n + 2],
                                                       scale=affine[:, c, n:n + 1])
                        ins.then_inc(G.evacuated[G.slot(u)], 1)

                def begin_next(r, U):
                    turned(r, U["T1"], nT1, 0)
                    for i in range(8):
                        u = U["V"] + i
                        j, half = i // 2, i % 2
                        G.wait_full(act, r, u)
                        nc.scalar.copy(v_aug[:, j, 8 * half:8 * half + 8, 0:DH1],
                                       psum_g[:, G.slot(u), :].rearrange("p (h d) -> p h d", d=DH1)
                                       ).then_inc(G.evacuated[G.slot(u)], 1)

                def group(g, b, s, U, first, last_group):
                    for i in range(NQK):
                        u = U["QK"] + i
                        if i >= 2:
                            G.wait_evacuated(act, g, u - 2)
                        G.wait_full(act, g, u)
                        nc.scalar.activation(ex[:, i % 2, :], psum_g[:, G.slot(u), :],
                                             ACT.Relu, scale=-1.0).then_inc(ex_negated, 1)
                        act.wait_ge(ex_negated, g * NQK + i + 1)
                        nc.scalar.activation(ex[:, i % 2, :], ex[:, i % 2, :], ACT.Exp,
                                             scale=-1.0).then_inc(ex_ready, 1)
                    if not first:
                        turned(g, U["T3"], nT2, None)
                    for i in range(8):
                        u = U["KT"] + i
                        j, half = i // 2, i % 2
                        G.wait_full(act, g, u)
                        nc.scalar.copy(kt[:, j, half * HALF:(half + 1) * HALF],
                                       psum_g[:, G.slot(u), :]).then_inc(G.evacuated[G.slot(u)], 1)
                    for i in range(8):
                        u = U["O"] + i
                        j, half = i // 2, i % 2
                        G.wait_full(act, g, u)
                        nc.scalar.copy(oT[:, 4 * half:4 * half + 4, j * P:(j + 1) * P],
                                       psum_g[:, G.slot(u), :].rearrange("p (m q) -> p m q", m=4)
                                       ).then_inc(G.evacuated[G.slot(u)], 1)
                    if not last_group:
                        begin_next(g, U)
                    turned(g, U["T2"], nT2, 2)
                    for m in range(MF):
                        u = U["F1"] + m
                        G.wait_full(act, g, u)
                        nc.scalar.activation(hT[:, m, :], psum_g[:, G.slot(u), :],
                                             ACT.Gelu).then_inc(G.evacuated[G.slot(u)], 1)

                begin_next(0, units_before)
                groups(act, group)
                turned(NGR - 1, units_after["T3"], nT2, None)

            @block.gpsimd
            def _(pool):
                def group(g, b, s, U, first, last_group):
                    if not first:
                        for call in range(2):
                            ln3.power(pool, g - 1, call)
                    if not last_group:
                        for call in range(2):
                            ln1.power(pool, g + 1, call)
                    ln2.power(pool, g, 0)
                    if s == 1 and not last_group:
                        nc.gpsimd.memset(state[:, :, :], 0.0).then_inc(cleared, 1)

                for call in range(2):
                    ln1.power(pool, 0, call)
                groups(pool, group)
                for call in range(2):
                    ln3.power(pool, NGR - 1, call)

            @block.vector
            def _(dve):
                def first_norms(g, b, s, part):
                    if part == 0:
                        dve.wait_ge(x2_loaded[s], b * 16 + 16)
                        chain1.at = 0
                        ln1.variance(dve, g, 0, chain1, lambda j: x2[:, s, j, :])
                        for j in range(G4):
                            last = ln1.apply(j, a3[:, s, j, :], x2[:, s, j, :])
                        chain1.link(dve, g, last)
                    else:
                        ln1.variance(dve, g, 1, chain1, lambda j: a3[:, s, j, :])
                        for j in range(G4):
                            last = ln1.apply(j, norm1[:, j, :], a3[:, s, j, :])
                        last.then_inc(norm1_ready, 1)
                        chain1.done()

                def last_norms(g, s, part):
                    if part == 0:
                        chain3.at = 0
                        ln3.variance(dve, g, 0, chain3, lambda j: a3[:, s, j, :])
                    elif part == 1:
                        for j in range(G4):
                            last = ln3.apply(j, a3[:, s, j, :], a3[:, s, j, :])
                        chain3.link(dve, g, last)
                        nc.vector.tensor_tensor(x2[:, s, :, :], x2[:, s, :, :], a3[:, s, :, :],
                                                ALU.add).then_inc(x3_ready, 1)
                    elif part == 2:
                        dve.wait_ge(x3_ready, g + 1)
                        ln3.variance(dve, g, 1, chain3, lambda j: x2[:, s, j, :])
                    else:
                        for j in range(G4):
                            last = ln3.apply(j, norm2[:, j, :], x2[:, s, j, :])
                        last.then_inc(xf_ready, 1)
                        chain3.done()

                def keep_logits(r, g, U):
                    for i in range(2):
                        u = U["L"] + i
                        G.wait_full(dve, r, u)
                        dst = logits[:, bass.ds(g * G4 + 2 * i, 2), :]
                        nc.vector.tensor_copy(dst, psum_g[:, G.slot(u), 0:2 * E].rearrange(
                            "p (j e) -> p j e", j=2)).then_inc(G.evacuated[G.slot(u)], 1)

                def mask_scores(g, d):
                    for h2 in range(2):
                        A.wait_full(dve, g, 2 * d + h2)
                        nc.vector.tensor_tensor(
                            scores[:, d % 2, h2, :, :],
                            psum_a[:, h2, :].rearrange("p (h q) -> p h q", h=4),
                            keep[:, :].rearrange("p (a q) -> p a q", a=1).broadcast_to([P, 4, P]),
                            ALU.mult).then_inc(A.evacuated[h2], 1)

                def add_a3(g, s, u0):
                    for i in range(2):
                        G.wait_full(dve, g, u0 + i)
                        nc.vector.tensor_tensor(a3[:, s, 2 * i:2 * i + 2, :],
                                                psum_g[:, G.slot(u0 + i), :].rearrange(
                                                    "p (j d) -> p j d", j=2),
                                                a3[:, s, 2 * i:2 * i + 2, :],
                                                ALU.add).then_inc(G.evacuated[G.slot(u0 + i)], 1)
                    for i in range(2):
                        G.wait_evacuated(dve, g, u0 + i)

                def group(g, b, s, U, first, last_group):
                    for i in range(NQK):
                        if not first and i in (3, 5, 7, 9):
                            last_norms(g - 1, 1 - s, (i - 3) // 2)
                        u = U["QK"] + i
                        dst = (qT if i < NP else kT)[:, i % NP, :]
                        dve.wait_ge(ex_ready, g * NQK + i + 1)
                        nc.vector.scalar_tensor_tensor(
                            out=dst, in0=psum_g[:, G.slot(u), :], scalar=0.0,
                            in1=ex[:, i % 2, :], op0=ALU.max, op1=ALU.add
                            ).then_inc(G.evacuated[G.slot(u)], 1)
                    if not first:
                        keep_logits(g, g - 1, U)
                    mask_scores(g, 0)
                    for n in range(NCH):
                        j, g4 = n // NG, n % NG
                        if not last_group and n in (4, 9):
                            first_norms(g + 1, b + s, 1 - s, (n - 4) // 5)
                        if n % 2 == 0 and n // 2 + 1 < NCH // 2:
                            mask_scores(g, n // 2 + 1)
                        NUM.wait_full(dve, g, n)
                        num = psum_n[:, NUM.slot(n), 0:4 * DV].rearrange("p (h d) -> p h d", d=DV)
                        den_chain.at = 2 * n
                        den_chain.link(dve, g, nc.vector.tensor_scalar(den[:, 0, :], num[:, :, DH1],
                                                                       EPS_DEN, None, ALU.max))
                        den_chain.link(dve, g, nc.vector.reciprocal(den[:, 1, :], den[:, 0, :]))
                        nc.vector.tensor_tensor(
                            o[:, j % 2, g4 * 4 * DH1:(g4 + 1) * 4 * DH1].rearrange(
                                "p (h d) -> p h d", d=DH1),
                            num[:, :, 0:DH1],
                            den[:, 1, :].rearrange("p (h a) -> p h a", a=1).broadcast_to([P, 4, DH1]),
                            ALU.mult).then_inc(NUM.evacuated[NUM.slot(n)], 1)
                        NUM.wait_evacuated(dve, g, n)
                        UP.wait_full(dve, g, n)
                        up = psum_u[:, 0:4 * DV].rearrange("p (a d) -> p a d", a=2)
                        for h2 in range(2):
                            rows, cols = slice(64 * h2, 64 * h2 + 64), slice(h2 * DV, h2 * DV + DV)
                            st = state[rows, 2 * g4:2 * g4 + 2, cols]
                            last = nc.vector.tensor_tensor(st, st, up[rows, :, cols], ALU.add)
                        last.then_inc(UP.evacuated[0], 1)
                    add_a3(g, s, U["W"])
                    chain2.at = 0
                    ln2.variance(dve, g, 0, chain2, lambda j: a3[:, s, j, :])
                    if not first:
                        dve.wait_ge(xf_stored, g * 16)
                    for j in range(G4):
                        last = ln2.apply(j, norm2[:, j, :], a3[:, s, j, :])
                    last.then_inc(norm2_ready, 1)
                    add_a3(g, s, U["F2"])

                for part in range(2):
                    first_norms(0, 0, 0, part)
                groups(dve, group)
                for part in range(4):
                    last_norms(NGR - 1, 1, part)
                keep_logits(NGR - 1, NGR - 1, units_after)


def routing(nc, logits, xf_dram, rows_dram, w1, w2, from1, from2):
    NT = N // P
    with ExitStack() as ctx:
        def sb(name, shape, dt=F32):
            return ctx.enter_context(nc.sbuf_tensor(name, shape, dt))

        def sem(name):
            return ctx.enter_context(nc.semaphore(name))

        psum = ctx.enter_context(nc.psum_tensor("r_psum", [P, 2, HALF], F32))
        before = sb("r_before", [P, P])
        ones = sb("r_ones", [P, P])
        index = sb("r_index", [P, E])
        best = [sb("r_best", [P, NT]), sb("r_second", [P, NT])]
        place = [sb("r_place_first", [P, NT]), sb("r_place_second", [P, NT])]
        picked = [sb("r_picked_first", [P, NT, E]), sb("r_picked_second", [P, NT, E])]
        left = sb("r_left", [P, NT, E])
        t0 = sb("r_t0", [P, NT, E])
        both = sb("r_both", [P, NT, E])
        count = [sb("r_count0", [P, NT, E]), sb("r_count1", [P, NT, E])]
        kept = sb("r_kept", [P, NT])
        row = sb("r_row", [P, NT])
        gap = sb("r_gap", [P, NT])
        gate = [sb("r_gate_first", [P, NT]), sb("r_gate_second", [P, NT])]
        to = [sb("r_to_first", [P, NT], I32), sb("r_to_second", [P, NT], I32)]
        XG = 4
        xf = sb("r_xf", [P, 4, XG, D])

        made = sem("r_made")
        step = sem("r_step")
        gap_ready = sem("r_gap_ready")
        exp_ready = sem("r_exp_ready")
        picked_ready = sem("r_picked_ready")
        counted = sem("r_counted")
        to_ready = sem("r_to_ready")
        xf_loaded = [sem(f"r_xf_loaded{i}") for i in range(4)]
        scattered = [sem(f"r_scattered{i}") for i in range(4)]

        def spread(t):
            return t[:, :].rearrange("p (t a) -> p t a", a=1).broadcast_to([P, NT, E])

        with nc.Block() as block:
            @block.gpsimd
            def _(pool):
                for e in range(E):
                    nc.gpsimd.memset(index[:, e:e + 1], float(e - E)).then_inc(made, 1)
                nc.gpsimd.memset(ones[:, :], 1.0).then_inc(made, 1)
                nc.gpsimd.memset(before[:, :], 1.0).then_inc(made, 1)
                pool.wait_ge(made, E + 2)
                nc.gpsimd.affine_select(out=before[:, :], in_=before[:, :], compare_op=ALU.is_ge,
                                        fill=0.0, base=-1, pattern=[[1, P]],
                                        channel_multiplier=-1).then_inc(made, 1)
                pool.wait_ge(made, E + 3)
                pool.wait_ge(to_ready, 1)
                for g in range(NT // XG):
                    pool.wait_ge(xf_loaded[g % 4], 16 * (g // 4 + 1))
                    for j in range(XG):
                        for k in range(2):
                            nc.gpsimd.indirect_dma_start(
                                out=rows_dram,
                                out_offset=bass.IndirectOffsetOnAxis(
                                    ap=to[k][:, g * XG + j:g * XG + j + 1], axis=0),
                                in_=xf[:, g % 4, j, :], in_offset=None,
                                bounds_check=SLOTS - 1, oob_is_err=False
                            ).then_inc(scattered[g % 4], 16)
                for i in range(4):
                    pool.wait_ge(scattered[i], 16 * 2 * XG * (NT // XG // 4))

            @block.sync
            def _(sp):
                xv = xf_dram.rearrange("(g j p) d -> g p j d", p=P, j=XG)
                for g in range(NT // XG):
                    if g >= 4:
                        sp.wait_ge(scattered[g % 4], 16 * 2 * XG * (g // 4))
                    sp.dma_start(xf[:, g % 4, :, :], xv[g]).then_inc(xf_loaded[g % 4], 16)

            @block.tensor
            def _(pe):
                pe.wait_ge(made, E + 3)
                pe.wait_ge(picked_ready, 1)
                sel = both[:, :, :].rearrange("p t e -> p (t e)")
                nc.tensor.matmul(psum[:, 0, 0:NT * E], before[:, :], sel, start=True, stop=True)
                nc.tensor.matmul(psum[:, 1, 0:NT * E], ones[:, :], sel, start=True,
                                 stop=True).then_inc(counted, 1)

            @block.scalar
            def _(act):
                act.wait_ge(gap_ready, 1)
                nc.scalar.activation(gap[:, :], gap[:, :], ACT.Exp).then_inc(exp_ready, 1)

            @block.vector
            def _(dve):
                at = [0]

                def link(ins):
                    at[0] += 1
                    ins.then_inc(step, 1)
                    dve.wait_ge(step, at[0])

                idx = index[:, :].rearrange("p (a e) -> p a e", a=1).broadcast_to([P, NT, E])
                dve.wait_ge(made, E)
                src = logits
                for k in range(2):
                    link(nc.vector.tensor_reduce(best[k][:, :], src[:, :, :], AX.X, ALU.max))
                    link(nc.vector.tensor_tensor(t0[:, :, :], src[:, :, :], spread(best[k]), ALU.is_equal))
                    link(nc.vector.tensor_tensor(t0[:, :, :], t0[:, :, :], idx, ALU.mult))
                    link(nc.vector.tensor_reduce(place[k][:, :], t0[:, :, :], AX.X, ALU.min))
                    link(nc.vector.tensor_tensor(picked[k][:, :, :], idx, spread(place[k]), ALU.is_equal))
                    if k == 0:
                        link(nc.vector.scalar_tensor_tensor(out=left[:, :, :], in0=picked[0][:, :, :],
                                                            scalar=NEG, in1=logits[:, :, :],
                                                            op0=ALU.mult, op1=ALU.add))
                        src = left
                nc.vector.tensor_tensor(gap[:, :], best[1][:, :], best[0][:, :],
                                        ALU.subtract).then_inc(gap_ready, 1)
                nc.vector.tensor_tensor(both[:, :, :], picked[0][:, :, :], picked[1][:, :, :],
                                        ALU.add).then_inc(picked_ready, 1)
                dve.wait_ge(counted, 1)
                total = psum[:, 1, 0:NT * E].rearrange("p (t e) -> p t e", e=E)
                within = psum[:, 0, 0:NT * E].rearrange("p (t e) -> p t e", e=E)
                nc.vector.memset(count[0][:, 0:1, :], 0.0)
                link(nc.vector.tensor_copy(count[0][:, 1:NT, :], total[:, 0:NT - 1, :]))
                a, d = 0, 1
                while d < NT:
                    nc.vector.tensor_copy(count[1 - a][:, 0:d, :], count[a][:, 0:d, :])
                    link(nc.vector.tensor_tensor(count[1 - a][:, d:NT, :], count[a][:, d:NT, :],
                                                 count[a][:, 0:NT - d, :], ALU.add))
                    a, d = 1 - a, 2 * d
                link(nc.vector.tensor_tensor(count[a][:, :, :], count[a][:, :, :], within, ALU.add))
                dve.wait_ge(exp_ready, 1)
                link(nc.vector.tensor_scalar(gate[1][:, :], gap[:, :], 1.0, None, ALU.add))
                link(nc.vector.reciprocal(gate[0][:, :], gate[1][:, :]))
                link(nc.vector.tensor_tensor(gate[1][:, :], gate[0][:, :], gap[:, :], ALU.mult))
                for k, (w, source) in enumerate(((w1, from1), (w2, from2))):
                    link(nc.vector.tensor_tensor(t0[:, :, :], picked[k][:, :, :], count[a][:, :, :],
                                                 ALU.mult))
                    link(nc.vector.tensor_reduce(row[:, :], t0[:, :, :], AX.X, ALU.add))
                    link(nc.vector.tensor_scalar(kept[:, :], row[:, :], float(CAP), None, ALU.is_lt))
                    link(nc.vector.scalar_tensor_tensor(out=row[:, :], in0=place[k][:, :],
                                                        scalar=float(CT * P), in1=row[:, :],
                                                        op0=ALU.mult, op1=ALU.add))
                    link(nc.vector.tensor_tensor(row[:, :], row[:, :], kept[:, :], ALU.mult))
                    nc.vector.tensor_scalar(source[:, :], row[:, :], float(SLOTS), None, ALU.add)
                    ins = nc.vector.tensor_scalar(to[k][:, :], row[:, :], float(SLOTS), None, ALU.add)
                    link(ins)
                    link(nc.vector.tensor_tensor(w[:, :], gate[k][:, :], kept[:, :], ALU.mult))
                dve.sem_inc(to_ready, 1)


def experts(nc, ident, rows_dram, W1, b1, W2, b2, y_dram):
    MH = HE // P
    sizes = [CT // 5 + (i < CT % 5) for i in range(5)]
    GROUPS = [(sum(sizes[:i]), n) for i, n in enumerate(sizes)]
    NGR = len(GROUPS)
    NQ = 2 * NGR
    assert max(sizes) == 4 and min(sizes) == 3
    with ExitStack() as ctx:
        def sb(name, shape, dt=F32):
            return ctx.enter_context(nc.sbuf_tensor(name, shape, dt))

        def sem(name):
            return ctx.enter_context(nc.semaphore(name))

        psum_t = ctx.enter_context(nc.psum_tensor("e_turned", [P, 2, HALF], F32))
        psum_h = ctx.enter_context(nc.psum_tensor("e_hidden", [P, 4, HALF], F32))
        psum_y = ctx.enter_context(nc.psum_tensor("e_out", [P, 2, HALF], F32))
        w1 = sb("e_w1", [P, 2, CD, HE])
        w2 = sb("e_w2", [P, 2, MH, D])
        b1_sb = sb("e_b1", [P, 2, MH])
        b2_sb = sb("e_b2", [P, 2, D])
        rows = sb("e_rows", [P, 4, D])
        rT = sb("e_rT", [P, 2, CD, HALF])
        hT = sb("e_hT", [P, 2, MH, HALF])
        y = sb("e_y", [P, 2, 4, D])

        TU = Ring(sem, "e_turned", 2, NQ * CD)
        HU = Ring(sem, "e_hidden", 4, NQ * MH)
        YU = Ring(sem, "e_out", 2, NQ * 2)
        w_loaded = [sem(f"e_weights_loaded{i}") for i in range(2)]
        rows_loaded = sem("e_rows_loaded")
        y_stored = [sem(f"e_y_stored{i}") for i in range(2)]

        def of_expert(w, e, pattern, **sizes):
            return w[bass.ds(e, 1), :, :].rearrange(pattern, **sizes)

        with nc.Block() as block:
            @block.sync
            def _(sp):
                for ring in (TU, HU, YU):
                    ring.begin(sp)
                for s in y_stored:
                    sp.sem_inc(s, 16)
                rv = rows_dram.rearrange("(e t p) d -> e p t d", p=P, t=CT)
                with sp.Fori(0, E // 2) as i:
                    for q in range(NQ):
                        e2, (t0, n) = q // NGR, GROUPS[q % NGR]
                        e = i * 2 + e2
                        if q % NGR == 0:
                            YU.wait_evacuated_before(sp, i, 2 * (e2 * NGR + NGR) - 1)
                            sp.dma_start(w1[:, e2, :, :],
                                         of_expert(W1, e, "a (c p) n -> p (a c) n", p=P)
                                         ).then_inc(w_loaded[e2], 16)
                            sp.dma_start(w2[:, e2, :, :],
                                         of_expert(W2, e, "a (c p) n -> p (a c) n", p=P)
                                         ).then_inc(w_loaded[e2], 16)
                            sp.dma_start(b1_sb[:, e2, :], b1[bass.ds(e, 1), :].rearrange(
                                "a (m p) -> p (a m)", p=P), allow_slow_non_contiguous=True
                                ).then_inc(w_loaded[e2], 16)
                            sp.dma_start(b2_sb[:, e2, :], b2[bass.ds(e, 1), :].rearrange(
                                "a d -> (a d)").partition_broadcast(P)).then_inc(w_loaded[e2], 16)
                        if q == 0:
                            TU.wait_evacuated_before(sp, i, NQ * CD - 1)
                        else:
                            TU.wait_evacuated(sp, i, q * CD - 1)
                        sp.dma_start(rows[:, 0:n, :],
                                     rv[bass.ds(e, 1), :, t0:t0 + n, :].rearrange("a p t d -> p (a t) d")
                                     ).then_inc(rows_loaded, 16)

            @block.tensor
            def _(pe):
                def turn(i, q):
                    n = GROUPS[q % NGR][1]
                    pe.wait_ge(rows_loaded, i * (16 * NQ) + 16 * q + 16)
                    for c in range(CD):
                        u = q * CD + c
                        TU.wait_free(pe, i, u)
                        for j in range(n):
                            last = nc.tensor.transpose(psum_t[:, c, j * P:(j + 1) * P],
                                                       rows[:, j, c * P:(c + 1) * P], ident[:, :])
                        last.then_inc(TU.full[c], 1)

                def hidden(i, q):
                    e2, n = q // NGR, GROUPS[q % NGR][1]
                    for c in range(CD):
                        TU.wait_evacuated(pe, i, q * CD + c)
                    if q % NGR == 0:
                        pe.wait_ge(w_loaded[e2], i * 64 + 64)
                    for m in range(MH):
                        u = q * MH + m
                        HU.wait_free(pe, i, u)
                        for c in range(CD):
                            last = nc.tensor.matmul(psum_h[:, HU.slot(u), 0:n * P],
                                                    w1[:, e2, c, m * P:(m + 1) * P],
                                                    rT[:, q % 2, c, 0:n * P],
                                                    start=(c == 0), stop=(c == CD - 1))
                        last.then_inc(HU.full[HU.slot(u)], 1)

                def outer(i, q):
                    e2, n = q // NGR, GROUPS[q % NGR][1]
                    for u in range(q * MH + 4, q * MH + 8):
                        HU.wait_evacuated(pe, i, u)
                    for a in range(2):
                        YU.wait_free(pe, i, 2 * q + a)
                        for j in range(2 * a, min(2 * a + 2, n)):
                            for m in range(MH):
                                last = nc.tensor.matmul(
                                    psum_y[:, a, (j - 2 * a) * D:(j - 2 * a + 1) * D],
                                    hT[:, q % 2, m, j * P:(j + 1) * P], w2[:, e2, m, :],
                                    start=(m == 0), stop=(m == MH - 1))
                        last.then_inc(YU.full[a], 1)

                with pe.Fori(0, E // 2) as i:
                    turn(i, 0)
                    for q in range(NQ):
                        if q + 1 < NQ:
                            turn(i, q + 1)
                        hidden(i, q)
                        if q > 0:
                            outer(i, q - 1)
                    outer(i, NQ - 1)

            @block.scalar
            def _(act):
                yv = y_dram[0:SLOTS, :].rearrange("(e t p) d -> e p t d", p=P, t=CT)

                def store(i, q):
                    e2, (t0, n) = q // NGR, GROUPS[q % NGR]
                    for a in range(2):
                        YU.wait_evacuated(act, i, 2 * q + a)
                    act.dma_start(yv[bass.ds(i * 2 + e2, 1), :, t0:t0 + n, :].rearrange(
                        "a p t d -> p (a t) d"), y[:, q % 2, 0:n, :]).then_inc(y_stored[q % 2], 16)

                with act.Fori(0, E // 2) as i:
                    for q in range(NQ):
                        e2, n = q // NGR, GROUPS[q % NGR][1]
                        if q % NGR == 0:
                            act.wait_ge(w_loaded[e2], i * 64 + 64)
                        for m in range(MH):
                            u = q * MH + m
                            if m == 4 and q >= 2:
                                store(i, q - 2)
                            HU.wait_full(act, i, u)
                            nc.scalar.activation(hT[:, q % 2, m, 0:n * P],
                                                 psum_h[:, HU.slot(u), 0:n * P], ACT.Gelu_apprx_tanh,
                                                 bias=b1_sb[:, e2, m:m + 1]
                                                 ).then_inc(HU.evacuated[HU.slot(u)], 1)
                    store(i, NQ - 2)
                    store(i, NQ - 1)
                for s in y_stored:
                    act.wait_ge(s, 16 * (E // 2 * NGR + 1))

            @block.vector
            def _(dve):
                def turned(i, q):
                    n = GROUPS[q % NGR][1]
                    for c in range(CD):
                        TU.wait_full(dve, i, q * CD + c)
                        nc.vector.tensor_copy(rT[:, q % 2, c, 0:n * P], psum_t[:, c, 0:n * P]
                                              ).then_inc(TU.evacuated[c], 1)

                def finish(i, q):
                    e2, n = q // NGR, GROUPS[q % NGR][1]
                    dve.wait_ge(y_stored[q % 2], i * (16 * NGR) + q // 2 * 16 + 16)
                    if q % NGR == 0:
                        dve.wait_ge(w_loaded[e2], i * 64 + 64)
                    for a in range(2):
                        j0, k = 2 * a, min(2, n - 2 * a)
                        YU.wait_full(dve, i, 2 * q + a)
                        nc.vector.tensor_tensor(
                            y[:, q % 2, j0:j0 + k, :],
                            psum_y[:, a, 0:k * D].rearrange("p (j d) -> p j d", d=D),
                            b2_sb[:, e2:e2 + 1, :].broadcast_to([P, k, D]),
                            ALU.add).then_inc(YU.evacuated[a], 1)

                with dve.Fori(0, E // 2) as i:
                    turned(i, 0)
                    for q in range(NQ):
                        if q + 1 < NQ:
                            turned(i, q + 1)
                        if q > 0:
                            finish(i, q - 1)
                    finish(i, NQ - 1)


def combine(nc, minus_half, y_dram, x3_dram, w1, w2, from1, from2, out_rows):
    XG = 4
    NG = N // P // XG
    R = 4
    with ExitStack() as ctx:
        def sb(name, shape, dt=F32):
            return ctx.enter_context(nc.sbuf_tensor(name, shape, dt))

        def sem(name):
            return ctx.enter_context(nc.semaphore(name))

        y1 = sb("f_y_first", [P, R, XG, D])
        y2 = sb("f_y_second", [P, R, XG, D])
        x3 = sb("f_x3", [P, R, XG, D])
        gathered = [sem(f"f_gathered{i}") for i in range(R)]
        x3_loaded = [sem(f"f_x3_loaded{i}") for i in range(R)]
        stored = [sem(f"f_stored{i}") for i in range(R)]
        weighed = sem("f_weighed")
        out_ready = sem("f_out_ready")
        chain = Chain(sem, "f_dve_chain", 5 * NG)
        ln = LayerNorm(nc, ctx, sem, "f_ln", XG, NG, minus_half)
        xv = x3_dram.rearrange("(g j p) d -> g p j d", p=P, j=XG)
        ov = out_rows.rearrange("(g j p) d -> g p j d", p=P, j=XG)
        with nc.Block() as block:
            @block.gpsimd
            def _(pool):
                def gather(g):
                    if g >= R:
                        pool.wait_ge(out_ready, g - R + 1)
                    for j in range(XG):
                        t = g * XG + j
                        for dst, idx in ((y1, from1), (y2, from2)):
                            nc.gpsimd.indirect_dma_start(
                                out=dst[:, g % R, j, :], out_offset=None, in_=y_dram,
                                in_offset=bass.IndirectOffsetOnAxis(ap=idx[:, t:t + 1], axis=0)
                            ).then_inc(gathered[g % R], 16)

                gather(0)
                gather(1)
                for g in range(NG):
                    if g + 2 < NG:
                        gather(g + 2)
                    ln.power(pool, 0, g)

            @block.sync
            def _(sp):
                for g in range(NG):
                    if g >= R:
                        sp.wait_ge(stored[g % R], 16 * (g // R))
                    sp.dma_start(x3[:, g % R, :, :], xv[g]).then_inc(x3_loaded[g % R], 16)

            @block.scalar
            def _(act):
                for g in range(NG):
                    act.wait_ge(out_ready, g + 1)
                    act.dma_start(ov[g], x3[:, g % R, :, :]).then_inc(stored[g % R], 16)
                for s in stored:
                    act.wait_ge(s, 16 * (NG // R))

            @block.vector
            def _(dve):
                for g in range(NG):
                    r = g % R
                    dve.wait_ge(gathered[r], 32 * XG * (g // R + 1))
                    for j in range(XG):
                        t = g * XG + j
                        last = nc.vector.tensor_scalar(y1[:, r, j, :], y1[:, r, j, :], w1[:, t:t + 1],
                                                       None, ALU.mult)
                    chain.link(dve, 0, last)
                    for j in range(XG):
                        t = g * XG + j
                        last = nc.vector.scalar_tensor_tensor(
                            out=y1[:, r, j, :], in0=y2[:, r, j, :], scalar=w2[:, t:t + 1],
                            in1=y1[:, r, j, :], op0=ALU.mult, op1=ALU.add)
                    last.then_inc(weighed, 1)
                    dve.wait_ge(weighed, g + 1)
                    ln.variance(dve, 0, g, chain, lambda j: y1[:, r, j, :])
                    for j in range(XG):
                        last = ln.apply(j, y1[:, r, j, :], y1[:, r, j, :])
                    chain.link(dve, 0, last)
                    dve.wait_ge(x3_loaded[r], 16 * (g // R + 1))
                    nc.vector.tensor_tensor(x3[:, r, :, :], x3[:, r, :, :], y1[:, r, :, :],
                                            ALU.add).then_inc(out_ready, 1)
                chain.done()


_INS = ['L0_attn_x', 'L0_attn_W_qkv', 'L0_attn_b_qkv', 'L0_attn_W_proj', 'L0_attn_b_proj',
        'L0_ffn_weight', 'L0_ffn_disha', 'L1_attn_ln1_g', 'L1_attn_ln1_b', 'L1_attn_Wq', 'L1_attn_Wk',
        'L1_attn_Wv', 'L1_attn_Wo', 'L1_attn_ln2_g', 'L1_attn_ln2_b', 'L1_attn_Wf1', 'L1_attn_Wf2',
        'L1_ffn_Wg', 'L1_ffn_W1', 'L1_ffn_b1', 'L1_ffn_W2', 'L1_ffn_b2']


def kernel(**inputs):
    import numpy as _np
    import concourse.bacc as _bacc
    from concourse.bass_utils import run_bass_kernel_spmd as _run

    nc = _bacc.Bacc("TRN2", target_bir_lowering=False, num_devices=1)
    arrays, args = {}, []
    for name in _INS:
        a = _np.ascontiguousarray(inputs[name])
        arrays[f"in_{name}_dram"] = a
        args.append(nc.dram_tensor(f"in_{name}_dram", a.shape, mybir.dt.from_np(a.dtype),
                                   kind="ExternalInput").ap())
    args.append(nc.dram_tensor("out_0_dram", (B, T, D), F32, kind="ExternalOutput").ap())
    build(nc, *args)
    r = _run(nc, [arrays], core_ids=[0])
    return r.results[0]["out_0_dram"]
```

```python
from contextlib import ExitStack

import concourse.bass as bass
from concourse import mybir

F32 = mybir.dt.float32
BF16 = mybir.dt.bfloat16
F32R = mybir.dt.float32r
I32 = mybir.dt.int32
U32 = mybir.dt.uint32
ALU = mybir.AluOpType
ACT = mybir.ActivationFunctionType
AX = mybir.AxisListType

P = 128
B, T, D = 8, 1024, 256
N = B * T
CD = D // P
TT = T // P
SPLIT = 4097.0
HALF = 512
EPS = 1e-5
EPS_DEN = 1e-6
NEG = -1e30

H0, DH0 = 16, 16
SCALE = DH0 ** -0.5
QTERM = (0, 1, 2, 0, 1, 0)
KTERM = (0, 0, 0, 1, 1, 2)
KS = DH0 * len(QTERM)
KM = KS + 3

H1, DH1 = 16, 64
E1 = H1 * DH1
DF = 1024
MF = DF // P
G4 = 4
SUP = T // (G4 * P)
DV = DH1 + 1

E, HE = 8, 1024
CAP = -(-N * 2 * 105 // (E * 100))
CT = -(-CAP // P)
SLOTS = E * CT * P


class Ring:

    def __init__(self, sem, name, slots, units):
        assert units % slots == 0
        self.slots, self.per = slots, units // slots
        self.start = 1 + self.per
        self.full = [sem(f"{name}_full{s}") for s in range(slots)]
        self.evacuated = [sem(f"{name}_evacuated{s}") for s in range(slots)]

    def slot(self, u):
        return u % self.slots

    def wait_free(self, eng, b, u):
        eng.wait_ge(self.evacuated[u % self.slots], b * self.per + self.start + u // self.slots)

    def wait_full(self, eng, b, u):
        eng.wait_ge(self.full[u % self.slots], b * self.per + u // self.slots + 1)

    def wait_evacuated(self, eng, b, u):
        eng.wait_ge(self.evacuated[u % self.slots], b * self.per + self.start + u // self.slots + 1)

    def wait_evacuated_before(self, eng, b, u):
        eng.wait_ge(self.evacuated[u % self.slots], b * self.per + u // self.slots + 2)

    def begin(self, eng):
        for s in self.evacuated:
            eng.sem_inc(s, self.start)


class Chain:

    def __init__(self, sem, name, per):
        self.sem, self.per, self.at = sem(name), per, 0

    def link(self, eng, b, ins):
        self.at += 1
        ins.then_inc(self.sem, 1)
        eng.wait_ge(self.sem, b * self.per + self.at)

    def done(self):
        assert self.at == self.per, (self.sem.name, self.at)


def batch_view(dram):
    return dram.rearrange("(b j p) d -> b p j d", p=P, j=TT)


def of_batch(view, b):
    return view[bass.ds(b, 1), :, :, :].rearrange("a p j d -> p (a j) d")


def build(nc, x, W_qkv, b_qkv, W_proj, b_proj, weight, disha, g1, be1, Wq, Wk, Wv, Wo, g2, be2,
          Wf1, Wf2, Wg, W1, b1, W2, b2, out):
    x_rows = x.rearrange("b t d -> (b t) d")
    out_rows = out.rearrange("b t d -> (b t) d")
    x2_dram = nc.dram_tensor("x2_scratch", (N, D), F32).ap()
    x3_dram = nc.dram_tensor("x3_scratch", (N, D), F32).ap()
    xf_dram = nc.dram_tensor("xf_scratch", (N, D), F32).ap()
    rows_dram = nc.dram_tensor("expert_rows_scratch", (SLOTS, D), F32).ap()
    y_dram = nc.dram_tensor("expert_out_scratch", (SLOTS + P, D), F32).ap()

    with ExitStack() as whole:
        def sb(name, shape, dt=F32):
            return whole.enter_context(nc.sbuf_tensor(name, shape, dt))

        ident = sb("ident", [P, P])
        logits = sb("logits", [P, N // P, E])
        minus_half = sb("minus_half", [P, TT])
        with ExitStack() as ctx:
            ident_bf = ctx.enter_context(nc.sbuf_tensor("ident_bf", [P, P], BF16))
            constants(nc, ident, ident_bf, minus_half)
            softmax_layer(nc, ident, ident_bf, minus_half, x_rows, W_qkv, b_qkv, W_proj, b_proj,
                          weight, disha, x2_dram, rows_dram, y_dram)
        linear_layer(nc, ident, minus_half, x2_dram, g1, be1, Wq, Wk, Wv, Wo, g2, be2, Wf1, Wf2, Wg,
                     x3_dram, xf_dram, logits)
        with ExitStack() as ctx:
            w1 = ctx.enter_context(nc.sbuf_tensor("w_first", [P, N // P], F32))
            w2 = ctx.enter_context(nc.sbuf_tensor("w_second", [P, N // P], F32))
            from1 = ctx.enter_context(nc.sbuf_tensor("from_first", [P, N // P], I32))
            from2 = ctx.enter_context(nc.sbuf_tensor("from_second", [P, N // P], I32))
            routing(nc, logits, xf_dram, rows_dram, w1, w2, from1, from2)
            experts(nc, ident, rows_dram, W1, b1, W2, b2, y_dram)
            combine(nc, minus_half, y_dram, x3_dram, w1, w2, from1, from2, out_rows)


def constants(nc, ident, ident_bf, minus_half):
    with ExitStack() as ctx:
        made = ctx.enter_context(nc.semaphore("c_made"))
        with nc.Block() as block:
            @block.gpsimd
            def _(pool):
                nc.gpsimd.memset(ident[:, :], 0.0).then_inc(made, 1)
                nc.gpsimd.memset(ident_bf[:, :], 0.0).then_inc(made, 1)
                nc.gpsimd.memset(minus_half[:, :], -0.5).then_inc(made, 1)
                pool.wait_ge(made, 3)
                for m in (ident, ident_bf):
                    nc.gpsimd.affine_select(out=m[:, :], in_=m[:, :], compare_op=ALU.not_equal,
                                            fill=1.0, base=0, pattern=[[-1, P]],
                                            channel_multiplier=1).then_inc(made, 1)
                pool.wait_ge(made, 5)


class LayerNorm:

    def __init__(self, nc, ctx, sem, name, n, calls, minus_half, on_act=False):
        self.nc, self.n, self.calls, self.minus_half = nc, n, calls, minus_half
        self.on_act = on_act
        self.stats = ctx.enter_context(nc.sbuf_tensor(f"{name}_stats", [P, n, 6], F32))
        self.mean = ctx.enter_context(nc.sbuf_tensor(f"{name}_mean", [P, n], F32))
        self.ve = ctx.enter_context(nc.sbuf_tensor(f"{name}_ve", [P, n], F32))
        self.rstd = ctx.enter_context(nc.sbuf_tensor(f"{name}_rstd", [P, n], F32))
        self.var_ready, self.rstd_ready = sem(f"{name}_var_ready"), sem(f"{name}_rstd_ready")
        if on_act:
            self.shift = ctx.enter_context(nc.sbuf_tensor(f"{name}_shift", [P, n], F32))

    def variance(self, dve, b, call, chain, tile):
        self.statistics(dve, b, chain, tile, range(self.n))
        self.summed(dve, b, call, chain)

    def statistics(self, dve, b, chain, tile, tiles):
        for j in tiles:
            last = self.nc.vector.bn_stats(self.stats[:, j, :], tile(j))
        if j == self.n - 1:
            chain.link(dve, b, last)

    def summed(self, dve, b, call, chain):
        nc = self.nc
        st = [self.stats[:, :, k] for k in range(6)]
        nc.vector.tensor_tensor(st[0], st[1], st[4], ALU.add)
        nc.vector.tensor_tensor(st[3], st[1], st[4], ALU.subtract)
        chain.link(dve, b, nc.vector.tensor_tensor(st[2], st[2], st[5], ALU.add))
        nc.vector.tensor_scalar(self.mean[:, :], st[0], -0.5 if self.on_act else 0.5, None, ALU.mult)
        nc.vector.scalar_tensor_tensor(out=st[1], in0=st[3], scalar=0.25, in1=st[3],
                                       op0=ALU.mult, op1=ALU.mult)
        chain.link(dve, b, nc.vector.tensor_scalar(st[4], st[2], 1.0 / D, EPS, ALU.mult, ALU.add))
        nc.vector.tensor_tensor(self.ve[:, :], st[1], st[4], ALU.add).then_inc(self.var_ready, 1)

    def power(self, pool, b, call):
        pool.wait_ge(self.var_ready, b * self.calls + call + 1)
        self.nc.gpsimd.tensor_tensor(self.rstd[:, :], self.ve[:, :], self.minus_half[:, 0:self.n],
                                     ALU.pow).then_inc(self.rstd_ready, 1)
        if self.on_act:
            pool.wait_ge(self.rstd_ready, b * (2 * self.calls) + 2 * call + 1)
            self.nc.gpsimd.tensor_tensor(self.shift[:, :], self.mean[:, :], self.rstd[:, :],
                                         ALU.mult).then_inc(self.rstd_ready, 1)

    def wait_power(self, eng, b, call):
        per = 2 if self.on_act else 1
        eng.wait_ge(self.rstd_ready, b * (per * self.calls) + per * (call + 1))

    def apply(self, j, out, in_):
        if self.on_act:
            return self.nc.scalar.activation(out, in_, ACT.Identity, bias=self.shift[:, j:j + 1],
                                             scale=self.rstd[:, j:j + 1])
        return self.nc.vector.tensor_scalar(out, in_, self.mean[:, j:j + 1], self.rstd[:, j:j + 1],
                                            ALU.subtract, ALU.mult)


def softmax_layer(nc, ident, ident_bf, minus_half, x_rows, W_qkv, b_qkv, W_proj, b_proj, weight,
                  disha, x2_dram, rows_dram, y_dram):
    HG = H0 // 4
    HB = H0 // 8
    DV0 = DH0 + 1
    SEGS = [(i, 0, i * P) for i in range(4)] + [(i, 1, max(i * P, HALF)) for i in range(TT)]
    NSEG = len(SEGS)
    MAXU = [(0, 1), (2, 3), (4,), (5,), (6,), (7,)]
    NMU = len(MAXU)

    with ExitStack() as ctx:
        def sb(name, shape, dt=F32):
            return ctx.enter_context(nc.sbuf_tensor(name, shape, dt))

        def sem(name):
            return ctx.enter_context(nc.semaphore(name))

        psum_s = ctx.enter_context(nc.psum_tensor("a_scores", [P, 3, 2, HALF], F32))
        psum_g = ctx.enter_context(nc.psum_tensor("a_general", [P, 2, HALF], F32))
        psum_o = psum_s[:, 2, :, :]

        w_qkv = sb("w_qkv", [P, CD, 3 * D])
        w_proj = sb("w_proj", [P, HG, D])
        w_ffn = sb("w_ffn", [P, CD, D])
        bias_qk = sb("bias_qk", [P, 2 * HB])
        bias_v = sb("bias_v", [P, D])
        mask_qk = sb("mask_qk", [P, P], BF16)
        mask_kq = sb("mask_kq", [P, P], BF16)
        spread = sb("spread", [P, P])
        x_in = sb("x_in", [P, TT, D])
        x_res = sb("x_res", [P, TT, D])
        xn = sb("xn", [P, TT, D])
        att = sb("att", [P, TT, D])
        yT = sb("yT", [P, HG, T])
        xnT = sb("xnT", [P, CD, T])
        qk_f = sb("qk_f", [P, 2, HALF])
        rest1 = sb("rest1", [P, HALF])
        one = sb("one", [P, 1])
        parts = sb("parts", [P, 2, 3, T], BF16)
        q_st = sb("q_st", [P, H0, T], BF16)
        k_st = sb("k_st", [P, H0, T], BF16)
        v_new = sb("v_new", [P, TT, D])
        v_aug = sb("v_aug", [P, TT, H0 * DV0 + 32 - DV0])
        mx = sb("mx", [P, HB, 8 * TT])
        nm = sb("nm", [8 * TT, HB, P])
        nm_rest = sb("nm_rest", [8 * TT, P])
        nm_parts = sb("nm_parts", [8 * TT, HB, 3, P], BF16)
        probs = sb("probs", [P, 2, 4, HALF])
        oT = sb("oT", [P, 2, HALF])
        rden = sb("rden", [P, HALF])
        zero = sb("zero", [P, D])

        load = sem("a_weights_loaded")
        prep = sem("a_cleared")
        made = sem("a_masks_made")
        turned = sem("a_weight_turned")
        filled = sem("a_constants_filled")
        x_loaded = sem("a_x_loaded")
        w_raw = x_res[:, :, :].rearrange("p j d -> p (j d)")[:, 0:CD * 2 * D].rearrange(
            "p (c n) -> p c n", c=CD)
        weight_sb, disha_sb = att[:, 0:CD, :], att[:, CD, :]
        with nc.Block() as block:
            @block.sync
            def _(sp):
                sp.dma_start(x_in[:, :, :], x_rows[0:T, :].rearrange("(j p) d -> p j d", p=P)
                             ).then_inc(x_loaded, 16)
                w_view = W_qkv.rearrange("(c p) n -> p c n", p=P)
                sp.dma_start(w_raw, w_view[:, :, 0:2 * D]).then_inc(load, 16)
                sp.dma_start(w_qkv[:, :, 2 * D:3 * D], w_view[:, :, 2 * D:3 * D]).then_inc(load, 16)
                sp.dma_start(weight_sb, weight.rearrange("(c p) n -> p c n", p=P)).then_inc(load, 16)
                for a in range(2):
                    sp.dma_start(att[64 * a:64 * a + 64, CD, :], disha).then_inc(load, 16)
                sp.dma_start(bias_v[:, :], b_qkv[2 * D:3 * D].partition_broadcast(P)).then_inc(load, 16)
                for n in range(2 * HB):
                    src = b_qkv[n * P:(n + 1) * P].rearrange("(h d) -> d h", d=DH0)
                    sp.dma_start(bias_qk[:, n:n + 1], src,
                                 allow_slow_non_contiguous=True).then_inc(load, 16)
                sp.wait_ge(prep, 1)
                for h in range(4):
                    src = W_proj.rearrange("(g h d) n -> h d g n", h=4, d=DH0)[h]
                    sp.dma_start(w_proj[32 * h:32 * h + DH0, :, :], src).then_inc(load, 16)
                sp.dma_start(w_proj[DH0:DH0 + 1, 0, :],
                             b_proj.rearrange("(a d) -> a d", a=1)).then_inc(load, 16)
                sp.wait_ge(load, 16 * (7 + 2 * HB + 4))

            @block.vector
            def _(dve):
                nc.vector.memset(w_proj[:, :, :], 0.0).then_inc(prep, 1)
                nc.vector.memset(v_aug[:, :, :], 0.0).then_inc(filled, 1)
                nc.vector.memset(zero[:, :], 0.0).then_inc(filled, 1)
                nc.vector.memset(one[:, :], 1.0).then_inc(filled, 1)
                dve.wait_ge(filled, 1)
                heads = v_aug[:, :, 0:H0 * DV0].rearrange("p j (h d) -> p j h d", d=DV0)
                nc.vector.memset(heads[:, :, :, DH0:DV0], 1.0).then_inc(filled, 1)
                dve.wait_ge(load, 16 * (7 + 2 * HB + 4))
                nc.vector.tensor_scalar(bias_qk[:, 0:HB], bias_qk[:, 0:HB], SCALE, None,
                                        ALU.mult).then_inc(filled, 1)
                for c in range(CD):
                    for n in range(2 * HB):
                        cols = slice(n * P, (n + 1) * P)
                        nc.vector.tensor_copy(
                            w_qkv[:, c, cols].rearrange("p (d h) -> p d h", d=DH0),
                            w_raw[:, c, cols].rearrange("p (h d) -> p d h", d=DH0)
                            ).then_inc(filled, 1)
                dve.wait_ge(turned, 1)
                for c in range(CD):
                    nc.vector.tensor_tensor(w_ffn[:, c, :], psum_g[:, c, 0:D], disha_sb,
                                            ALU.add).then_inc(filled, 1)
                dve.wait_ge(filled, 5 + 2 * HB * CD + CD)

            @block.gpsimd
            def _(pool):
                nc.gpsimd.memset(mask_qk[:, :], 0.0).then_inc(made, 1)
                nc.gpsimd.memset(mask_kq[:, :], 0.0).then_inc(made, 1)
                nc.gpsimd.memset(spread[:, :], 0.0).then_inc(made, 1)
                pool.wait_ge(made, 3)
                nc.gpsimd.affine_select(out=mask_qk[:, :], in_=mask_qk[:, :], compare_op=ALU.is_ge,
                                        fill=NEG, base=0, pattern=[[-1, P]],
                                        channel_multiplier=1).then_inc(made, 1)
                nc.gpsimd.affine_select(out=mask_kq[:, :], in_=mask_kq[:, :], compare_op=ALU.is_ge,
                                        fill=NEG, base=0, pattern=[[1, P]],
                                        channel_multiplier=-1).then_inc(made, 1)
                sp4 = spread[:, :].rearrange("p (g w) -> p g w", g=4)
                nc.gpsimd.affine_select(out=sp4, in_=sp4, compare_op=ALU.not_equal, fill=1.0,
                                        base=-DH0, pattern=[[-32, 4], [0, 32]],
                                        channel_multiplier=1).then_inc(made, 1)
                pool.wait_ge(made, 6)
                nc.gpsimd.memset(k_st[96:99, :, :].bitcast(U32), 0x3F803F80).then_inc(made, 1)
                pool.wait_ge(made, 7)

            @block.tensor
            def _(pe):
                pe.wait_ge(load, 16 * (7 + 2 * HB + 4))
                for c in range(CD):
                    for o in range(CD):
                        last = nc.tensor.transpose(psum_g[:, c, o * P:(o + 1) * P],
                                                   weight_sb[:, o, c * P:(c + 1) * P], ident[:, :])
                last.then_inc(turned, 1)

        NM = 8 * NMU
        NS1 = HB * NM
        NK = HG * NSEG
        IN_MAXIMA = {2: ("D", 0), 5: ("P", 0), 7: ("P", 1), 9: ("P", 2), 11: ("P", 3), 13: ("P", 4),
                     15: ("P", 5), 17: ("P", 6), 19: ("P", 7), 22: ("LN", 1), 38: ("LN", 2),
                     46: ("T2", 0), 49: ("T2", 1), 51: ("T2", 2), 53: ("T2", 3), 56: ("F", 0),
                     59: ("F", 1), 62: ("F", 2), 65: ("F", 3), 69: ("LN", 3)}
        IN_ATTEND = {1: ("LN", 0), 4: ("T1", 0), 6: ("QK", 0), 8: ("QK", 1), 10: ("QK", 2),
                     12: ("QK", 3), 14: ("V", 0), 16: ("V", 1), 18: ("V", 2), 20: ("V", 3),
                     34: ("QK", 4), 36: ("QK", 5), 38: ("QK", 6), 40: ("QK", 7)}
        HEAD_ALONE = ([("LN", 0), ("T1", 0)] + [("QK", i) for i in range(4)] +
                      [("V", i) for i in range(4)] + [("QK", i) for i in range(4, 8)])
        TAIL = [IN_MAXIMA[i] for i in sorted(IN_MAXIMA)]

        def den_after(n):
            return {4: -1, 8: 0}.get(n)

        def turn_units(u0, with_head, with_tail):
            seq = []

            def stage(what):
                name, i = what
                if name == "T1":
                    seq.extend(("T1", c) for c in range(4))
                elif name == "P":
                    seq.extend([("P", i // 2)] * (i % 2 == 0))
                elif name != "LN":
                    seq.append(what)
            for n in range(NS1):
                if with_tail and n in IN_MAXIMA:
                    stage(IN_MAXIMA[n])
                if n % NM == NM - 1:
                    seq.append(("M", n // NM))
            for k in range(NK):
                if with_head and k in IN_ATTEND:
                    stage(IN_ATTEND[k])
                d = den_after(k % NSEG)
                if d is not None and 2 * (k // NSEG) + d >= 0:
                    seq.append(("DEN", 2 * (k // NSEG) + d))
            return {what: u0 + i for i, what in enumerate(seq)}

        def alone(u0, names):
            return {what: u0 + i for i, what in enumerate(names)}

        H_UNITS = [("T1", c) for c in range(4)] + [w for w in HEAD_ALONE if w[0] in ("QK", "V")]
        T_UNITS = ([("D", 0)] + [("P", i) for i in range(4)] + [("T2", c) for c in range(4)] +
                   [("F", i) for i in range(4)])
        U_ALL = HB + 2 * HG - 1 + len(H_UNITS) + len(T_UNITS)
        LEAD = len(H_UNITS)
        units_before = alone(0, H_UNITS)
        units_first = turn_units(LEAD, True, False)
        units_turn = turn_units(LEAD - len(T_UNITS), True, True)
        units_last = turn_units(LEAD - len(T_UNITS), False, True)
        units_after = alone(LEAD - len(T_UNITS) + U_ALL - LEAD, T_UNITS)

        G = Ring(sem, "a_general", 2, U_ALL)
        M = Ring(sem, "a_max_scores", 3, NS1)
        S = Ring(sem, "a_scores", 2, NK * 2)
        attended_out = [sem(f"a_attended_out{s}") for s in range(2)]
        res_loaded = sem("a_residual_loaded")
        x2_ready = sem("a_x2_ready")
        x2_stored = sem("a_x2_stored")
        head_norm = sem("a_head_norm_ready")
        tail_norm = sem("a_tail_norm_ready")
        split_done = sem("a_split_done")
        stacked = [sem("a_q_stacked"), sem("a_k_stacked")]
        nm_ready = sem("a_minus_max_ready")
        nm_placed = [sem(f"a_minus_max_placed{m}") for m in range(HB)]
        pv_done = sem("a_probs_used")
        yT_ready = sem("a_yT_ready")
        v_taken = sem("a_v_taken")
        zeroed = sem("a_rows_zeroed")
        chain_n = Chain(sem, "a_minus_max_chain", HB * 3)
        chain_h = Chain(sem, "a_head_chain", 3)
        chain_t = Chain(sem, "a_tail_chain", 3 * 3)
        applied = sem("a_tail_norm_applied")
        x1_ready = sem("a_x1_ready")
        pchain = Chain(sem, "a_pool_chain", 2 * HB * 2 * 3)
        ln_h = LayerNorm(nc, ctx, sem, "a_ln_head", TT, 1, minus_half)
        ln_t = LayerNorm(nc, ctx, sem, "a_ln_tail", TT, 3, minus_half, on_act=True)
        GROUP = 16 * len(QTERM)

        def turns(eng, turn, head, tail):
            for what in HEAD_ALONE:
                head(0, 0, units_before, what)
            turn(0, units_first, True, False)
            with eng.Fori(1, B - 1) as b:
                turn(b, units_turn, True, True)
            turn(B - 1, units_last, False, True)
            for what in TAIL:
                tail(B - 1, B - 1, units_after, what)

        with nc.Block() as block:
            @block.sync
            def _(sp):
                G.begin(sp)
                M.begin(sp)
                S.begin(sp)
                for s in attended_out:
                    sp.sem_inc(s, 1)
                sp.sem_inc(split_done, 2)
                sp.sem_inc(x2_stored, 16)
                sp.sem_inc(pv_done, 2)
                for s in stacked:
                    sp.sem_inc(s, GROUP)
                sp.sem_inc(head_norm, 1)
                sp.sem_inc(x2_ready, 1)
                xv, x2v = batch_view(x_rows), batch_view(x2_dram)
                zv = rows_dram.rearrange("(e b p) d -> b p e d", p=P, e=SLOTS // P // B)

                def load_x(b):
                    sp.wait_ge(head_norm, b + 1)
                    sp.dma_start(x_in[:, :, :], of_batch(xv, b)).then_inc(x_loaded, 16)

                def stack(b, m, used):
                    if used is not None:
                        sp.wait_ge(pv_done, used)
                    if m == 1:
                        sp.dma_start(zv[bass.ds(b, 1), :, :, :].rearrange("a p e d -> p (a e) d"),
                                     zero[:, :].rearrange("p (a d) -> p a d", a=1).broadcast_to(
                                         [P, SLOTS // P // B, D])).then_inc(zeroed, 16)
                    for qk, terms, st in ((0, QTERM, q_st), (1, KTERM, k_st)):
                        sp.wait_ge(split_done, b * 8 + 4 * m + 2 * qk + 2 + 2)
                        for t, part in enumerate(terms):
                            sp.dma_start(st[DH0 * t:DH0 * t + DH0, 8 * m:8 * m + 8, :],
                                         parts[:, qk, part, :]).then_inc(stacked[qk], 16)

                def store_x2(b):
                    sp.wait_ge(x2_ready, b + 2)
                    sp.dma_start(of_batch(x2v, b), x_res[:, :, :]).then_inc(x2_stored, 16)

                def turn(b, with_head, with_tail):
                    for m in range(HB):
                        sp.wait_ge(nm_ready, b * HB + m + 1)
                        for t in range(3):
                            sp.dma_start(q_st[KS + t:KS + t + 1, 8 * m:8 * m + 8, :],
                                         nm_parts[:, m, t, :]).then_inc(nm_placed[m], 16)
                        if m == 0 and with_tail:
                            store_x2(b - 1)
                    sp.wait_ge(x2_stored, b * 16 + 16)
                    sp.dma_start(x_res[:, :, :], of_batch(xv, b)).then_inc(res_loaded, 16)
                    if with_head:
                        for m in range(HB):
                            stack(b + 1, m, b * NK + (m + 1) * (NK // 2) + 2)
                            if m == 0:
                                load_x(b + 2)

                stack(0, 0, None)
                load_x(1)
                stack(0, 1, None)
                turn(0, True, False)
                with sp.Fori(1, B - 2) as b:
                    turn(b, True, True)
                b = B - 2
                for m in range(HB):
                    sp.wait_ge(nm_ready, b * HB + m + 1)
                    for t in range(3):
                        sp.dma_start(q_st[KS + t:KS + t + 1, 8 * m:8 * m + 8, :],
                                     nm_parts[:, m, t, :]).then_inc(nm_placed[m], 16)
                    if m == 0:
                        store_x2(b - 1)
                sp.wait_ge(x2_stored, b * 16 + 16)
                sp.dma_start(x_res[:, :, :], of_batch(xv, b)).then_inc(res_loaded, 16)
                for m in range(HB):
                    stack(b + 1, m, b * NK + (m + 1) * (NK // 2) + 2)
                turn(B - 1, False, True)
                store_x2(B - 1)
                sp.wait_ge(x2_stored, B * 16 + 16)
                sp.dma_start(y_dram[SLOTS:SLOTS + P, :], zero[:, :]).then_inc(zeroed, 16)
                sp.wait_ge(zeroed, 16 * (B + 1))

            @block.tensor
            def _(pe):
                def turn_norm(r, u, i):
                    half, c = i // CD, i % CD
                    G.wait_free(pe, r, u)
                    for j in range(4):
                        last = nc.tensor.transpose(
                            psum_g[:, G.slot(u), j * P:(j + 1) * P],
                            xn[:, half * 4 + j, c * P:(c + 1) * P], ident[:, :])
                    last.then_inc(G.full[G.slot(u)], 1)

                def two_tiles(r, u, i, lhs, rhs, nk, which=(0, 1)):
                    if 0 in which:
                        G.wait_free(pe, r, u)
                    for jj in which:
                        j = 2 * i + jj
                        for c in range(nk):
                            last = nc.tensor.matmul(psum_g[:, G.slot(u), jj * D:(jj + 1) * D],
                                                    lhs[:, c, j * P:(j + 1) * P], rhs[:, c, :],
                                                    start=(c == 0), stop=(c == nk - 1))
                    if 1 in which:
                        last.then_inc(G.full[G.slot(u)], 1)

                def head(b, r, U, what):
                    name, i = what
                    if name == "T1":
                        pe.wait_ge(head_norm, b + 2)
                        for c in range(4):
                            turn_norm(r, U["T1", c], c)
                    elif name == "QK":
                        m, qk, half = i // 4, i // 2 % 2, i % 2
                        u = U[what]
                        if i == 0:
                            for c in (2, 3):
                                G.wait_evacuated(pe, r, U["T1", c])
                        G.wait_free(pe, r, u)
                        for c in range(CD):
                            last = nc.tensor.matmul(psum_g[:, G.slot(u), :],
                                                    w_qkv[:, c, qk * D + m * P:qk * D + (m + 1) * P],
                                                    xnT[:, c, half * HALF:(half + 1) * HALF],
                                                    start=(c == 0), stop=(c == CD - 1))
                        last.then_inc(G.full[G.slot(u)], 1)
                    elif name == "V":
                        two_tiles(r, U[what], i, xnT, w_qkv[:, :, 2 * D:3 * D], CD)

                def tail(b, r, U, what):
                    name, i = what
                    if name == "D":
                        denominators(b, r, U[what], 2 * HG - 1)
                    elif name == "P":
                        if i == 0:
                            pe.wait_ge(yT_ready, b * 2 * HG + 2 * HG)
                        two_tiles(r, U["P", i // 2], i // 2, yT, w_proj, HG, (i % 2,))
                    elif name == "T2":
                        if i == 0:
                            pe.wait_ge(tail_norm, b + 1)
                        turn_norm(r, U[what], i)
                    elif name == "F":
                        if i == 0:
                            for c in (2, 3):
                                G.wait_evacuated(pe, r, U["T2", c])
                        two_tiles(r, U[what], i, xnT, w_ffn, CD)

                def maxima(b, U, with_tail):
                    for n in range(NS1):
                        if with_tail and n in IN_MAXIMA:
                            tail(b - 1, b, U, IN_MAXIMA[n])
                        m, h8, tiles = n // NM, n // NMU % 8, MAXU[n % NMU]
                        h = 8 * m + h8
                        if n % NM == 0:
                            for st in stacked:
                                pe.wait_ge(st, b * (HB * GROUP) + (m + 2) * GROUP)
                        if n < 2:
                            S.wait_evacuated_before(pe, b, 2 * NK - 2 + n)
                        elif n == 2:
                            for out in attended_out:
                                pe.wait_ge(out, b * HG + 1)
                        M.wait_free(pe, b, n)
                        for a, j in enumerate(tiles):
                            s = psum_s[:, M.slot(n), a:, :].rearrange("p a n -> p (a n)")
                            w = (j + 1) * P
                            for k0 in range(0, w, HALF):
                                k1 = min(k0 + HALF, w)
                                nc.tensor.matmul(s[:, k0:k1], q_st[0:KS, h, j * P:(j + 1) * P],
                                                 k_st[0:KS, h, k0:k1], start=True, stop=False,
                                                 skip_group_check=True)
                            last = nc.tensor.matmul(s[:, j * P:w], ident_bf[:, :], mask_qk[:, :],
                                                    start=False, stop=True, skip_group_check=True)
                        last.then_inc(M.full[M.slot(n)], 1)
                        if n % NM == NM - 1:
                            M.wait_evacuated(pe, b, n)
                            u = U["M", m]
                            G.wait_free(pe, b, u)
                            nc.tensor.matmul(psum_g[0:8 * TT, G.slot(u), 0:P], mx[:, m, :],
                                             ident[:, :], start=True, stop=True
                                             ).then_inc(G.full[G.slot(u)], 1)

                def values(b, k):
                    hg, (i, half, q0) = k // NSEG, SEGS[k % NSEG]
                    w = (half + 1) * HALF - q0
                    v = hg * 2 + half
                    if i == 0:
                        pe.wait_ge(attended_out[v % 2], b * HG + v // 2 + 1)
                    for pair in range(2):
                        S.wait_evacuated(pe, b, k * 2 + pair)
                    for h4 in range(4):
                        h = hg * 4 + h4
                        last = nc.tensor.matmul(
                            psum_o[32 * h4:32 * h4 + 32, v % 2, q0 - half * HALF:HALF],
                            v_aug[:, i, h * DV0:h * DV0 + 32], probs[:, k % 2, h4, 0:w],
                            start=(i == 0), stop=True, skip_group_check=True)
                    last.then_inc(pv_done, 1)

                def denominators(b, r, u, v):
                    pe.wait_ge(attended_out[v % 2], b * HG + v // 2 + 2)
                    G.wait_free(pe, r, u)
                    nc.tensor.matmul(psum_g[:, G.slot(u), :], spread[:, :], oT[:, v % 2, :],
                                     start=True, stop=True).then_inc(G.full[G.slot(u)], 1)

                def attend(b, U, with_head):
                    pe.wait_ge(v_taken, b + 1)
                    for k in range(NK):
                        if with_head and k in IN_ATTEND:
                            head(b + 1, b, U, IN_ATTEND[k])
                        hg, n = k // NSEG, k % NSEG
                        i, half, q0 = SEGS[n]
                        if n == 0 and hg % 2 == 0:
                            pe.wait_ge(nm_placed[hg // 2], b * 48 + 48)
                        w = (half + 1) * HALF - q0
                        diagonal = q0 == i * P
                        for pair in range(2):
                            u = k * 2 + pair
                            S.wait_free(pe, b, u)
                            for p2 in range(2):
                                h = hg * 4 + pair * 2 + p2
                                s = psum_s[:, S.slot(u), p2, :]
                                last = nc.tensor.matmul(
                                    s[:, 0:w], k_st[0:KM, h, i * P:(i + 1) * P],
                                    q_st[0:KM, h, q0:q0 + w], start=True, stop=not diagonal,
                                    skip_group_check=True)
                                if diagonal:
                                    last = nc.tensor.matmul(s[:, 0:P], ident_bf[:, :],
                                                            mask_kq[:, :], start=False, stop=True,
                                                            skip_group_check=True)
                            last.then_inc(S.full[S.slot(u)], 1)
                        if k > 0:
                            values(b, k - 1)
                        d = den_after(n)
                        if d is not None and 2 * hg + d >= 0:
                            denominators(b, b, U["DEN", 2 * hg + d], 2 * hg + d)
                    values(b, NK - 1)

                def turn(b, U, with_head, with_tail):
                    maxima(b, U, with_tail)
                    attend(b, U, with_head)

                turns(pe, turn, head, tail)

            @block.scalar
            def _(act):
                def turned(r, u, i):
                    half, c = i // CD, i % CD
                    G.wait_full(act, r, u)
                    nc.scalar.copy(xnT[:, c, half * HALF:(half + 1) * HALF],
                                   psum_g[:, G.slot(u), :]).then_inc(G.evacuated[G.slot(u)], 1)

                def head(b, r, U, what):
                    name, i = what
                    if name == "T1":
                        for c in range(4):
                            turned(r, U["T1", c], c)
                    elif name == "QK":
                        u = U[what]
                        qk, m = i // 2 % 2, i // 4
                        G.wait_full(act, r, u)
                        act.wait_ge(split_done, b * 8 + i + 1)
                        nc.scalar.activation(qk_f[:, i % 2, :], psum_g[:, G.slot(u), :], ACT.Identity,
                                             bias=bias_qk[:, qk * HB + m:qk * HB + m + 1],
                                             scale=SCALE if qk == 0 else 1.0
                                             ).then_inc(G.evacuated[G.slot(u)], 1)

                def tail(b, r, U, what):
                    name, i = what
                    if name == "T2":
                        turned(r, U[what], i)
                    elif name == "P" and i % 2 == 0 or name == "F":
                        n = i // 2 if name == "P" else i
                        u = U[name, n]
                        if what == ("P", 0):
                            act.wait_ge(x2_ready, b + 1)
                        G.wait_full(act, r, u)
                        nc.scalar.copy(att[:, 2 * n:2 * n + 2, :],
                                       psum_g[:, G.slot(u), :].rearrange("p (j d) -> p j d", j=2)
                                       ).then_inc(G.evacuated[G.slot(u)], 1)
                    elif name == "LN":
                        src, dst = (x_res, xn) if i == 2 else (att, att)
                        ln_t.wait_power(act, b, i - 1)
                        for j in range(TT):
                            last = ln_t.apply(j, dst[:, j, :], src[:, j, :])
                        last.then_inc(tail_norm if i == 2 else applied, 1)

                def take_v(b, r, U):
                    G.wait_evacuated(act, r, U["V", 3])
                    act.wait_ge(pv_done, b * NK + 2)
                    nc.scalar.copy(
                        v_aug[:, :, 0:H0 * DV0].rearrange("p j (h d) -> p j h d", d=DV0)[:, :, :, 0:DH0],
                        v_new[:, :, :].rearrange("p j (h d) -> p j h d", d=DH0)
                        ).then_inc(v_taken, 1)

                def turn(b, U, with_head, with_tail):
                    if with_tail:
                        take_v(b, b - 1, units_turn)
                        for what in TAIL:
                            tail(b - 1, b, U, what)
                    else:
                        take_v(b, b, units_before)
                    for k in range(NK):
                        if with_head and k in IN_ATTEND:
                            head(b + 1, b, U, IN_ATTEND[k])
                        i, half, q0 = SEGS[k % NSEG]
                        w = (half + 1) * HALF - q0
                        act.wait_ge(pv_done, b * NK + k + 1)
                        for pair in range(2):
                            u = k * 2 + pair
                            S.wait_full(act, b, u)
                            nc.scalar.activation(probs[:, k % 2, 2 * pair:2 * pair + 2, 0:w],
                                                 psum_s[:, S.slot(u), :, 0:w],
                                                 ACT.Exp).then_inc(S.evacuated[S.slot(u)], 1)

                turns(act, turn, head, tail)

            @block.gpsimd
            def _(pool):
                ones = one[:, :].broadcast_to([P, HALF])

                def head(b, r, U, what):
                    name, i = what
                    if name == "LN":
                        ln_h.power(pool, b, 0)
                    elif name == "QK":
                        qk, m, half = i // 2 % 2, i // 4, i % 2
                        cols = slice(half * HALF, (half + 1) * HALF)
                        G.wait_evacuated(pool, r, U[what])
                        if half == 0:
                            pool.wait_ge(stacked[qk], b * (HB * GROUP) + (m + 1) * GROUP)
                        f = qk_f[:, i % 2, :]
                        pchain.at = 3 * i
                        pchain.link(pool, b, nc.gpsimd.tensor_tensor(parts[:, qk, 0, cols], f, ones,
                                                                     ALU.mult))
                        pchain.link(pool, b, nc.gpsimd.tensor_tensor(rest1[:, :], f, parts[:, qk, 0, cols],
                                                                     ALU.subtract))
                        pchain.link(pool, b, nc.gpsimd.tensor_tensor(parts[:, qk, 1, cols], rest1[:, :],
                                                                     ones, ALU.mult))
                        nc.gpsimd.tensor_tensor(parts[:, qk, 2, cols], rest1[:, :],
                                                parts[:, qk, 1, cols],
                                                ALU.subtract).then_inc(split_done, 1)
                        pool.wait_ge(split_done, b * 8 + i + 3)

                def tail(b, r, U, what):
                    name, i = what
                    if name != "LN":
                        return
                    ln_t.power(pool, b, i - 1)
                    if i != 2:
                        if i == 1:
                            pool.wait_ge(res_loaded, b * 16 + 16)
                        pool.wait_ge(applied, b * 2 + (i + 1) // 2)
                        nc.gpsimd.tensor_tensor(x_res[:, :, :], x_res[:, :, :], att[:, :, :],
                                                ALU.add).then_inc(x1_ready if i == 1 else x2_ready, 1)

                def turn(b, U, with_head, with_tail):
                    if with_tail:
                        for what in TAIL:
                            tail(b - 1, b, U, what)
                    if with_head:
                        for k in sorted(IN_ATTEND):
                            head(b + 1, b, U, IN_ATTEND[k])

                turns(pool, turn, head, tail)

            @block.vector
            def _(dve):
                def head(b, r, U, what):
                    name, i = what
                    if name == "LN":
                        dve.wait_ge(x_loaded, b * 16 + 16)
                        chain_h.at = 0
                        ln_h.variance(dve, b, 0, chain_h, lambda j: x_in[:, j, :])
                        ln_h.wait_power(dve, b, 0)
                        for j in range(TT):
                            last = ln_h.apply(j, xn[:, j, :], x_in[:, j, :])
                        last.then_inc(head_norm, 1)
                    elif name == "V":
                        u = U[what]
                        G.wait_full(dve, r, u)
                        nc.vector.tensor_tensor(
                            v_new[:, 2 * i:2 * i + 2, :],
                            psum_g[:, G.slot(u), :].rearrange("p (j n) -> p j n", j=2),
                            bias_v[:, :].rearrange("p (a n) -> p a n", a=1).broadcast_to([P, 2, D]),
                            ALU.add).then_inc(G.evacuated[G.slot(u)], 1)

                def tail(b, r, U, what):
                    name, i = what
                    if name == "D":
                        normalise(b, r, U[what], 2 * HG - 1)
                    elif name == "LN":
                        if i == 2:
                            dve.wait_ge(x1_ready, b + 1)
                        else:
                            for n in (2, 3):
                                G.wait_evacuated(dve, r, U["P" if i == 1 else "F", n])
                        chain_t.at = 3 * (i - 1)
                        src = x_res if i == 2 else att
                        ln_t.variance(dve, b, i - 1, chain_t, lambda j: src[:, j, :])

                def maxima(b, U, with_tail):
                    for n in range(NS1):
                        if with_tail and n in IN_MAXIMA:
                            tail(b - 1, b, U, IN_MAXIMA[n])
                        m, h8 = n // NM, n // NMU % 8
                        M.wait_full(dve, b, n)
                        for a, j in enumerate(MAXU[n % NMU]):
                            s = psum_s[:, M.slot(n), a:, :].rearrange("p a n -> p (a n)")
                            at = h8 * TT + j
                            last = nc.vector.tensor_reduce(mx[:, m, at:at + 1], s[:, 0:(j + 1) * P],
                                                           AX.X, ALU.max)
                        last.then_inc(M.evacuated[M.slot(n)], 1)
                        if n % NM < NM - 1:
                            continue
                        u = U["M", m]
                        G.wait_full(dve, b, u)
                        f = nm[:, m, :]
                        nc.vector.tensor_scalar(f, psum_g[0:8 * TT, G.slot(u), 0:P], -1.0, None,
                                                ALU.mult).then_inc(G.evacuated[G.slot(u)], 1)
                        G.wait_evacuated(dve, b, u)
                        chain_n.at = 3 * m
                        chain_n.link(dve, b, nc.vector.tensor_copy(nm_parts[:, m, 0, :], f))
                        chain_n.link(dve, b, nc.vector.tensor_tensor(nm_rest[:, :], f, nm_parts[:, m, 0, :],
                                                                     ALU.subtract))
                        chain_n.link(dve, b, nc.vector.tensor_copy(nm_parts[:, m, 1, :], nm_rest[:, :]))
                        nc.vector.tensor_tensor(nm_parts[:, m, 2, :], nm_rest[:, :],
                                                nm_parts[:, m, 1, :],
                                                ALU.subtract).then_inc(nm_ready, 1)

                def copy_out(b, v):
                    dve.wait_ge(pv_done, b * NK + v // 2 * NSEG + (4, NSEG)[v % 2] + 2)
                    nc.vector.tensor_copy(oT[:, v % 2, :], psum_o[:, v % 2, :]
                                          ).then_inc(attended_out[v % 2], 1)
                    dve.wait_ge(attended_out[v % 2], b * HG + v // 2 + 2)

                def normalise(b, r, u, v):
                    hg, half = v // 2, v % 2
                    G.wait_full(dve, r, u)
                    nc.vector.reciprocal(rden[:, :], psum_g[:, G.slot(u), :]
                                         ).then_inc(G.evacuated[G.slot(u)], 1)
                    G.wait_evacuated(dve, r, u)
                    nc.vector.tensor_tensor(
                        yT[:, hg, half * HALF:(half + 1) * HALF], oT[:, v % 2, :], rden[:, :],
                        ALU.mult).then_inc(yT_ready, 1)
                    dve.wait_ge(yT_ready, b * 2 * HG + v + 1)

                def turn(b, U, with_head, with_tail):
                    maxima(b, U, with_tail)
                    for k in range(NK):
                        if with_head and k in IN_ATTEND:
                            head(b + 1, b, U, IN_ATTEND[k])
                        hg, n = k // NSEG, k % NSEG
                        if n == 5:
                            copy_out(b, 2 * hg)
                        if n == 1 and hg > 0:
                            copy_out(b, 2 * hg - 1)
                        d = den_after(n)
                        if d is not None and 2 * hg + d >= 0:
                            normalise(b, b, U["DEN", 2 * hg + d], 2 * hg + d)
                    copy_out(b, 2 * HG - 1)

                turns(dve, turn, head, tail)


def linear_layer(nc, ident, minus_half, x2_dram, g1, be1, Wq, Wk, Wv, Wo, g2, be2, Wf1, Wf2, Wg,
                 x3_dram, xf_dram, logits):
    NP = H1 // 2
    NG = H1 // 4
    ME = E1 // P
    assert SUP == 2
    NGR = B * SUP
    NCH = G4 * NG
    NQK = 2 * NP
    OWN = [("QK", NQK), ("KT", 8), ("O", 8), ("W", 2), ("T2", CD), ("F1", MF), ("F2", 2)]
    OF_NEXT = [("T1", CD), ("V", 8)]
    OF_LAST = [("T3", CD), ("L", 2)]
    ORDER = OWN[0:1] + OF_LAST[0:1] + OWN[1:2] + OF_LAST[1:2] + OWN[2:3] + OF_NEXT[0:1] + OWN[3:4] + OF_NEXT[1:2] + OWN[4:]
    LAST_NORMS = (1, 2, 3, 5, 8, 9, 10, 12)
    FIRST_NORMS = (2, 3, 4, 7, 8, 9)
    N_NEXT, N_ALL = sum(n for _, n in OF_NEXT), sum(n for _, n in ORDER)
    N_LAST = sum(n for _, n in OF_LAST)

    def units(u0, stages):
        where = {}
        for name, n in stages:
            where[name] = u0
            u0 += n
        return where

    units_before = units(0, OF_NEXT)
    units_first = units(N_NEXT, [s for s in ORDER if s not in OF_LAST])
    BASE = N_NEXT - N_LAST
    units_group = units(BASE, ORDER)
    units_last = units(BASE, [s for s in ORDER if s not in OF_NEXT])
    units_after = units(BASE + N_ALL - N_NEXT, OF_LAST)

    with ExitStack() as ctx:
        def sb(name, shape, dt=F32):
            return ctx.enter_context(nc.sbuf_tensor(name, shape, dt))

        def sem(name):
            return ctx.enter_context(nc.semaphore(name))

        R = 3
        psum_g = ctx.enter_context(nc.psum_tensor("l_general", [P, R, HALF], F32))
        psum_a = ctx.enter_context(nc.psum_tensor("l_scores", [P, 2, HALF], F32))
        psum_n = ctx.enter_context(nc.psum_tensor("l_num", [P, 2, HALF], F32))
        psum_u = ctx.enter_context(nc.psum_tensor("l_update", [P, HALF], F32))

        w_qkv = {part: sb(f"l_w_qkv_{part}", [P, 3, CD, E1], F32R) for part in ("hi", "lo")}
        wo = sb("l_wo", [P, ME, D])
        wf1 = sb("l_wf1", [P, CD, DF])
        wf2 = sb("l_wf2", [P, MF, D])
        wg = sb("l_wg", [P, CD, E])
        affine = sb("l_affine", [P, CD, 4])
        keep = sb("l_keep", [P, P], BF16)
        x2 = sb("l_x2", [P, 2, G4, D])
        a3 = sb("l_a3", [P, 2, G4, D])
        norm = sb("l_norm", [P, G4, D])
        nT1 = {part: sb(f"l_nT1_{part}", [P, CD, HALF], F32R) for part in ("hi", "lo")}
        nT2 = sb("l_nT2", [P, CD, HALF])
        qT = sb("l_qT", [P, NP, HALF])
        kT = sb("l_kT", [P, NP, HALF])
        kt = sb("l_k", [P, G4, E1])
        v_aug = sb("l_v", [P, G4, H1, DV])
        state = sb("l_state", [P, NP, 2 * DV])
        scores = sb("l_scores_kept", [P, 2, 2, 4, P])
        den = sb("l_den", [P, 2, 4])
        o = sb("l_o", [P, 2, E1])
        oT = sb("l_oT", [P, ME, HALF])
        hT = qT
        ex = o[:, :, :].rearrange("p s (a n) -> p (s a) n", n=HALF)
        whole = ex[:, 0:CD, :]
        diff = scores[:, 0, :, :, :].rearrange("p c h q -> p c (h q)")

        load = sem("l_weights_loaded")
        raw_loaded = [sem(f"l_raw_weights_loaded{n}") for n in range(3)]
        made = sem("l_mask_made")
        filled = sem("l_constants_filled")
        w_hi = sem("l_weights_hi_ready")
        w_lo = sem("l_weights_lo_ready")
        raw = (qT[:, 0:NP // 2, :], qT[:, NP // 2:NP, :], kT[:, 0:NP // 2, :])
        raw_diff = (oT[:, 0:NP // 2, :], oT[:, NP // 2:NP, :], kT[:, NP // 2:NP, :])

        def part_of(part, n):
            return w_qkv[part][:, n, :, :].rearrange("p c (a k) -> p (c a) k", k=HALF)

        with nc.Block() as block:
            @block.gpsimd
            def _(pool):
                nc.gpsimd.memset(keep[:, :], 1.0).then_inc(made, 1)
                pool.wait_ge(made, 1)
                nc.gpsimd.affine_select(out=keep[:, :], in_=keep[:, :], compare_op=ALU.is_ge,
                                        fill=0.0, base=0, pattern=[[1, P]],
                                        channel_multiplier=-1).then_inc(made, 1)
                nc.gpsimd.memset(state[:, :, :], 0.0).then_inc(made, 1)
                pool.wait_ge(made, 3)

            @block.vector
            def _(dve):
                nc.vector.memset(v_aug[:, :, :, DH1:DV], 1.0).then_inc(filled, 1)
                dve.wait_ge(filled, 1)

        G = Ring(sem, "l_general", R, N_ALL)
        A = Ring(sem, "l_scores", 2, NCH)
        NUM = Ring(sem, "l_num", 2, NCH)
        UP = Ring(sem, "l_update", 1, NCH)
        x2_loaded = [sem(f"l_x2_loaded{i}") for i in range(2)]
        x3_ready = sem("l_x3_ready")
        xf_ready = sem("l_xf_ready")
        x3_stored = sem("l_x3_stored")
        xf_stored = sem("l_xf_stored")
        a3_ready = sem("l_a3_ready")
        a3_normed = sem("l_a3_normed")
        norm1_ready = sem("l_norm1_ready")
        norm2_ready = sem("l_norm2_ready")
        diff_ready = sem("l_nT1_difference_ready")
        hi_ready = sem("l_nT1_hi_ready")
        lo_ready = sem("l_nT1_lo_ready")
        ex_negated = sem("l_exp_negated")
        ex_ready = sem("l_exp_ready")
        cleared = sem("l_state_cleared")
        den_chain = Chain(sem, "l_den_chain", 2 * NCH)
        chain1 = Chain(sem, "l_norm1_chain", 6)
        chain2 = Chain(sem, "l_norm2_chain", 3)
        chain3 = Chain(sem, "l_norm3_chain", 6)
        ln1 = LayerNorm(nc, ctx, sem, "l_ln1", G4, 2, minus_half, on_act=True)
        ln2 = LayerNorm(nc, ctx, sem, "l_ln2", G4, 1, minus_half)
        ln3 = LayerNorm(nc, ctx, sem, "l_ln3", G4, 2, minus_half)

        def group_view(dram):
            return dram.rearrange("(g j p) d -> g p j d", p=P, j=G4)

        def of_group(view, g):
            return view[bass.ds(g, 1), :, :, :].rearrange("a p j d -> p (a j) d")

        def groups(eng, group):
            group(0, 0, 0, units_first, True, False)
            with eng.Fori(0, B - 1) as t:
                group(t * 2 + 1, t, 1, units_group, False, False)
                group(t * 2 + 2, t + 1, 0, units_group, False, False)
            group(NGR - 1, B - 1, 1, units_last, False, True)

        with nc.Block() as block:
            @block.sync
            def _(sp):
                for ring in (G, A, NUM, UP):
                    ring.begin(sp)
                sp.sem_inc(cleared, 1)
                x2v, x3v, xfv = group_view(x2_dram), group_view(x3_dram), group_view(xf_dram)
                sp.dma_start(x2[:, 0, :, :], of_group(x2v, 0)).then_inc(x2_loaded[0], 16)
                for n, w in enumerate((Wv, Wq, Wk)):
                    sp.dma_start(raw[n].rearrange("p (c a) n -> p c (a n)", c=CD),
                                 w.rearrange("(c p) n -> p c n", p=P)).then_inc(raw_loaded[n], 16)
                    if n == 0:
                        for k, vec in enumerate((g1, be1, g2, be2)):
                            sp.dma_start(affine[:, :, k], vec.rearrange("(c p) -> p c", p=P),
                                         allow_slow_non_contiguous=True).then_inc(raw_loaded[0], 16)
                for dst, w in ((wo, Wo), (wf1, Wf1), (wf2, Wf2), (wg, Wg)):
                    sp.dma_start(dst[:, :, :], w.rearrange("(c p) n -> p c n", p=P)).then_inc(load, 16)

                def store(g, s):
                    sp.wait_ge(x3_ready, g + 1)
                    sp.dma_start(of_group(x3v, g), x2[:, s, :, :]).then_inc(x3_stored, 16)
                    sp.wait_ge(xf_ready, g + 1)
                    sp.dma_start(of_group(xfv, g), norm[:, :, :]).then_inc(xf_stored, 16)

                def group(g, b, s, U, first, last):
                    if first:
                        sp.dma_start(x2[:, 1, :, :], of_group(x2v, 1)).then_inc(x2_loaded[1], 16)
                        return
                    store(g - 1, 1 - s)
                    if not last:
                        sp.wait_ge(x3_stored, g * 16)
                        sp.dma_start(x2[:, 1 - s, :, :], of_group(x2v, g + 1)).then_inc(x2_loaded[1 - s], 16)

                groups(sp, group)
                store(NGR - 1, 1)
                sp.wait_ge(x3_stored, NGR * 16)
                sp.wait_ge(xf_stored, NGR * 16)

            @block.tensor
            def _(pe):
                def turn(g, u0, norm):
                    for c in range(CD):
                        u = u0 + c
                        G.wait_free(pe, g, u)
                        for j in range(G4):
                            last = nc.tensor.transpose(psum_g[:, G.slot(u), j * P:(j + 1) * P],
                                                       norm[:, j, c * P:(c + 1) * P], ident[:, :])
                        last.then_inc(G.full[G.slot(u)], 1)

                def by_feature(g, u, w, cols, nT):
                    G.wait_free(pe, g, u)
                    for c in range(CD):
                        last = nc.tensor.matmul(psum_g[:, G.slot(u), :], w[:, c, cols], nT[:, c, :],
                                                start=(c == 0), stop=(c == CD - 1))
                    last.then_inc(G.full[G.slot(u)], 1)

                def two_tiles(g, u, i, lhs, rhs, nk):
                    G.wait_free(pe, g, u)
                    for jj in range(2):
                        j = 2 * i + jj
                        for k in range(nk):
                            last = nc.tensor.matmul(psum_g[:, G.slot(u), jj * D:(jj + 1) * D],
                                                    lhs[:, k, j * P:(j + 1) * P], rhs[:, k, :],
                                                    start=(k == 0), stop=(k == nk - 1))
                    last.then_inc(G.full[G.slot(u)], 1)

                def score(g, d):
                    j = d // 2
                    cols = slice(j * P, (j + 1) * P)
                    for h2 in range(2):
                        A.wait_free(pe, g, 2 * d + h2)
                    for i in range(4):
                        for h2 in range(2):
                            p, rows = d % 2 * 4 + i, slice(64 * h2, 64 * h2 + 64)
                            last = nc.tensor.matmul(psum_a[:, h2, i * P:(i + 1) * P],
                                                    kT[rows, p, cols], qT[rows, p, cols],
                                                    start=True, stop=True)
                            if i == 3:
                                last.then_inc(A.full[h2], 1)

                def turn_o(g, U, j):
                    NUM.wait_evacuated(pe, g, j * NG + NG - 1)
                    for half in range(2):
                        u = U["O"] + 2 * j + half
                        G.wait_free(pe, g, u)
                        for m in range(4):
                            last = nc.tensor.transpose(psum_g[:, G.slot(u), m * P:(m + 1) * P],
                                                       o[:, j % 2, (4 * half + m) * P:(4 * half + m + 1) * P],
                                                       ident[:, :])
                        last.then_inc(G.full[G.slot(u)], 1)

                def split_product(out, lhs, rhs):
                    terms = [(c, a, b) for c in range(CD)
                             for a, b in (("hi", "hi"), ("hi", "lo"), ("lo", "hi"))]
                    for k, (c, a, b) in enumerate(terms):
                        last = nc.tensor.matmul(out, lhs(a, c), rhs(b, c), start=(k == 0),
                                                stop=(k == len(terms) - 1))
                    return last

                def turn_next(r, g, U):
                    pe.wait_ge(norm1_ready, g + 1)
                    turn(r, U["T1"], norm)

                def next_v(r, g, U):
                    pe.wait_ge(lo_ready, CD * g + CD)
                    for j in range(G4):
                        for half in range(2):
                            u = U["V"] + 2 * j + half
                            G.wait_free(pe, r, u)
                            split_product(psum_g[:, G.slot(u), :],
                                          lambda a, c: nT1[a][:, c, j * P:(j + 1) * P],
                                          lambda b, c: w_qkv[b][:, 0, c, half * HALF:(half + 1) * HALF]
                                          ).then_inc(G.full[G.slot(u)], 1)

                def turn_last(r, g, U):
                    pe.wait_ge(xf_ready, g + 1)
                    turn(r, U["T3"], norm)

                def last_logits(r, U):
                    for i in range(2):
                        u = U["L"] + i
                        G.wait_free(pe, r, u)
                        for jj in range(2):
                            j = 2 * i + jj
                            for c in range(CD):
                                last = nc.tensor.matmul(psum_g[:, G.slot(u), jj * E:(jj + 1) * E],
                                                        nT2[:, c, j * P:(j + 1) * P], wg[:, c, :],
                                                        start=(c == 0), stop=(c == CD - 1))
                        last.then_inc(G.full[G.slot(u)], 1)

                def group(g, b, s, U, first, last_group):
                    for i in range(NQK):
                        u, cols = U["QK"] + i, slice(i % NP * P, (i % NP + 1) * P)
                        G.wait_free(pe, g, u)
                        split_product(psum_g[:, G.slot(u), :],
                                      lambda a, c: w_qkv[a][:, 1 + i // NP, c, cols],
                                      lambda b, c: nT1[b][:, c, :]).then_inc(G.full[G.slot(u)], 1)
                    if not first:
                        turn_last(g, g - 1, U)
                    for u in range(U["QK"] + NQK - R, U["QK"] + NQK):
                        G.wait_evacuated(pe, g, u)
                    score(g, 0)
                    for j in range(G4):
                        for half in range(2):
                            u = U["KT"] + 2 * j + half
                            G.wait_free(pe, g, u)
                            for m in range(4):
                                last = nc.tensor.transpose(psum_g[:, G.slot(u), m * P:(m + 1) * P],
                                                           kT[:, 4 * half + m, j * P:(j + 1) * P],
                                                           ident[:, :])
                            last.then_inc(G.full[G.slot(u)], 1)
                    if not first:
                        last_logits(g, U)
                    for u in range(U["KT"] + 8 - R, U["KT"] + 8):
                        G.wait_evacuated(pe, g, u)
                    if s == 0:
                        pe.wait_ge(cleared, b + 1)
                    for n in range(NCH):
                        j, g4, d = n // NG, n % NG, n // 2
                        if n % 2 == 0 and d + 1 < NCH // 2:
                            score(g, d + 1)
                        NUM.wait_free(pe, g, n)
                        if n % 2 == 0:
                            for h2 in range(2):
                                A.wait_evacuated(pe, g, 2 * d + h2)
                        for p2 in range(2):
                            p = 2 * g4 + p2
                            nc.tensor.matmul(psum_n[:, NUM.slot(n), p2 * 2 * DV:(p2 + 1) * 2 * DV],
                                             qT[:, p, j * P:(j + 1) * P], state[:, p, :],
                                             start=True, stop=False, skip_group_check=True)
                            for h2 in range(2):
                                h4 = 2 * p2 + h2
                                last = nc.tensor.matmul(
                                    psum_n[:, NUM.slot(n), h4 * DV:(h4 + 1) * DV],
                                    scores[:, d % 2, h2, p % 4, :], v_aug[:, j, 4 * g4 + h4, :],
                                    start=False, stop=True, skip_group_check=True)
                        last.then_inc(NUM.full[NUM.slot(n)], 1)
                        UP.wait_free(pe, g, n)
                        for p2 in range(2):
                            p = 2 * g4 + p2
                            last = nc.tensor.matmul(psum_u[:, p2 * 2 * DV:(p2 + 1) * 2 * DV],
                                                    kt[:, j, p * P:(p + 1) * P],
                                                    v_aug[:, j, 2 * p:2 * p + 2, :],
                                                    start=True, stop=True)
                        last.then_inc(UP.full[0], 1)
                        if g4 == 1 and j > 0:
                            turn_o(g, U, j - 1)
                    turn_o(g, U, G4 - 1)
                    if not last_group:
                        turn_next(g, g + 1, U)
                    for u in range(U["O"] + 8 - R, U["O"] + 8):
                        G.wait_evacuated(pe, g, u)
                    for i in range(2):
                        two_tiles(g, U["W"] + i, i, oT, wo, ME)
                    if not last_group:
                        next_v(g, g + 1, U)
                    pe.wait_ge(norm2_ready, g + 1)
                    turn(g, U["T2"], norm)
                    for c in range(CD):
                        G.wait_evacuated(pe, g, U["T2"] + c)
                    for m in range(MF):
                        by_feature(g, U["F1"] + m, wf1, slice(m * P, (m + 1) * P), nT2)
                    for u in range(U["F2"] - R, U["F2"]):
                        G.wait_evacuated(pe, g, u)
                    for i in range(2):
                        two_tiles(g, U["F2"] + i, i, hT, wf2, MF)

                turn_next(0, 0, units_before)
                pe.wait_ge(w_lo, 1)
                next_v(0, 0, units_before)
                pe.wait_ge(w_lo, 3)
                pe.wait_ge(load, 64)
                groups(pe, group)
                turn_last(NGR - 1, NGR - 1, units_after)
                for c in range(CD):
                    G.wait_evacuated(pe, NGR - 1, units_after["T3"] + c)
                last_logits(NGR - 1, units_after)

            @block.scalar
            def _(act):
                def turned(r, u0, nT, n):
                    for c in range(CD):
                        u = u0 + c
                        G.wait_full(act, r, u)
                        if n is None:
                            ins = nc.scalar.copy(nT[:, c, :], psum_g[:, G.slot(u), :])
                        else:
                            ins = nc.scalar.activation(nT[:, c, :], psum_g[:, G.slot(u), :], ACT.Identity,
                                                       bias=affine[:, c, n + 1:n + 2],
                                                       scale=affine[:, c, n:n + 1])
                        ins.then_inc(G.evacuated[G.slot(u)], 1)

                def first_norms(g, s, call, stored=None):
                    src, dst, ready = ((x2[:, s, :, :], a3[:, s, :, :], a3_ready),
                                       (a3[:, s, :, :], norm, norm1_ready))[call]
                    ln1.wait_power(act, g, call)
                    if call == 1 and stored is not None:
                        act.wait_ge(xf_stored, stored)
                    for j in range(G4):
                        last = ln1.apply(j, dst[:, j, :], src[:, j, :])
                    last.then_inc(ready, 1)

                def next_v(r, U):
                    for i in range(8):
                        u = U["V"] + i
                        j, half = i // 2, i % 2
                        G.wait_full(act, r, u)
                        nc.scalar.copy(v_aug[:, j, 8 * half:8 * half + 8, 0:DH1],
                                       psum_g[:, G.slot(u), :].rearrange("p (h d) -> p h d", d=DH1)
                                       ).then_inc(G.evacuated[G.slot(u)], 1)

                def group(g, b, s, U, first, last_group):
                    for i in range(NQK):
                        u = U["QK"] + i
                        G.wait_full(act, g, u)
                        nc.scalar.activation(ex[:, i % 4, :], psum_g[:, G.slot(u), :],
                                             ACT.Relu, scale=-1.0).then_inc(ex_negated, 1)
                        act.wait_ge(ex_negated, g * NQK + i + 1)
                        nc.scalar.activation(ex[:, i % 4, :], ex[:, i % 4, :], ACT.Exp,
                                             scale=-1.0).then_inc(ex_ready, 1)
                    if not first:
                        turned(g, U["T3"], nT2, None)
                    for i in range(8):
                        u = U["KT"] + i
                        j, half = i // 2, i % 2
                        G.wait_full(act, g, u)
                        nc.scalar.copy(kt[:, j, half * HALF:(half + 1) * HALF],
                                       psum_g[:, G.slot(u), :]).then_inc(G.evacuated[G.slot(u)], 1)
                    for i in range(8):
                        u = U["O"] + i
                        j, half = i // 2, i % 2
                        if not last_group and i in (0, 4):
                            first_norms(g + 1, 1 - s, i // 4, None if first else g * 16)
                        G.wait_full(act, g, u)
                        nc.scalar.copy(oT[:, 4 * half:4 * half + 4, j * P:(j + 1) * P],
                                       psum_g[:, G.slot(u), :].rearrange("p (m q) -> p m q", m=4)
                                       ).then_inc(G.evacuated[G.slot(u)], 1)
                    if not last_group:
                        turned(g, U["T1"], whole, 0)
                        next_v(g, U)
                    turned(g, U["T2"], nT2, 2)
                    for m in range(MF):
                        u = U["F1"] + m
                        G.wait_full(act, g, u)
                        nc.scalar.activation(hT[:, m, :], psum_g[:, G.slot(u), :],
                                             ACT.Gelu).then_inc(G.evacuated[G.slot(u)], 1)

                for call in range(2):
                    first_norms(0, 0, call)
                act.wait_ge(raw_loaded[0], 80)
                turned(0, units_before["T1"], whole, 0)
                next_v(0, units_before)
                groups(act, group)
                turned(NGR - 1, units_after["T3"], nT2, None)

            @block.gpsimd
            def _(pool):
                def low(g):
                    for c in range(CD):
                        pool.wait_ge(hi_ready, CD * g + c + 1)
                        nc.gpsimd.tensor_tensor(nT1["lo"][:, c, :], whole[:, c, :],
                                                nT1["hi"][:, c, :].bitcast(F32),
                                                ALU.subtract).then_inc(lo_ready, 1)

                def last_norms(g, s):
                    ln3.power(pool, g, 0)
                    pool.wait_ge(a3_normed, g + 1)
                    nc.gpsimd.tensor_tensor(x2[:, s, :, :], x2[:, s, :, :], a3[:, s, :, :],
                                            ALU.add).then_inc(x3_ready, 1)
                    ln3.power(pool, g, 1)

                def group(g, b, s, U, first, last_group):
                    if not first:
                        last_norms(g - 1, 1 - s)
                    if not last_group:
                        for call in range(2):
                            ln1.power(pool, g + 1, call)
                        low(g + 1)
                    ln2.power(pool, g, 0)
                    if s == 1 and not last_group:
                        nc.gpsimd.memset(state[:, :, :], 0.0).then_inc(cleared, 1)

                def low_weights(n):
                    pool.wait_ge(w_hi, 2 * n + 2)
                    nc.gpsimd.tensor_tensor(part_of("lo", n), raw[n], part_of("hi", n).bitcast(F32),
                                            ALU.subtract).then_inc(w_lo, 1)

                for call in range(2):
                    ln1.power(pool, 0, call)
                low_weights(0)
                low(0)
                low_weights(1)
                low_weights(2)
                groups(pool, group)
                last_norms(NGR - 1, 1)

            @block.vector
            def _(dve):
                def piece(ln, dve, g, call, chain, tile, k):
                    if k < 2:
                        ln.statistics(dve, g, chain, tile, range(2 * k, 2 * k + 2))
                    else:
                        ln.summed(dve, g, call, chain)

                def first_norms(g, b, s, part):
                    call, k = part // 3, part % 3
                    if part == 0:
                        dve.wait_ge(x2_loaded[s], b * 16 + 16)
                        chain1.at = 0
                    elif part == 3:
                        dve.wait_ge(a3_ready, g + 1)
                    src = a3 if call else x2
                    piece(ln1, dve, g, call, chain1, lambda j: src[:, s, j, :], k)

                def last_norms(g, s, part):
                    call, k = part // 4, part % 4
                    src = x2 if call else a3
                    if part == 0:
                        chain3.at = 0
                    elif part == 4:
                        dve.wait_ge(x3_ready, g + 1)
                    if k < 3:
                        piece(ln3, dve, g, call, chain3, lambda j: src[:, s, j, :], k)
                        return
                    ln3.wait_power(dve, g, call)
                    for j in range(G4):
                        last = ln3.apply(j, norm[:, j, :] if call else a3[:, s, j, :], src[:, s, j, :])
                    last.then_inc(xf_ready if call else a3_normed, 1)

                def high(r, g, U):
                    for c in range(CD):
                        G.wait_evacuated(dve, r, U["T1"] + c)
                        nc.vector.scalar_tensor_tensor(out=diff[:, c, :], in0=whole[:, c, :],
                                                       scalar=SPLIT, in1=whole[:, c, :], op0=ALU.mult,
                                                       op1=ALU.subtract).then_inc(diff_ready, 1)
                    for c in range(CD):
                        dve.wait_ge(diff_ready, CD * g + c + 1)
                        nc.vector.scalar_tensor_tensor(out=nT1["hi"][:, c, :], in0=whole[:, c, :],
                                                       scalar=SPLIT, in1=diff[:, c, :], op0=ALU.mult,
                                                       op1=ALU.subtract).then_inc(hi_ready, 1)

                def keep_logits(r, g, U):
                    for i in range(2):
                        u = U["L"] + i
                        G.wait_full(dve, r, u)
                        dst = logits[:, bass.ds(g * G4 + 2 * i, 2), :]
                        nc.vector.tensor_copy(dst, psum_g[:, G.slot(u), 0:2 * E].rearrange(
                            "p (j e) -> p j e", j=2)).then_inc(G.evacuated[G.slot(u)], 1)

                def mask_scores(g, d):
                    for h2 in range(2):
                        A.wait_full(dve, g, 2 * d + h2)
                        nc.vector.tensor_tensor(
                            scores[:, d % 2, h2, :, :],
                            psum_a[:, h2, :].rearrange("p (h q) -> p h q", h=4),
                            keep[:, :].rearrange("p (a q) -> p a q", a=1).broadcast_to([P, 4, P]),
                            ALU.mult).then_inc(A.evacuated[h2], 1)

                def add_a3(g, s, u0):
                    for i in range(2):
                        G.wait_full(dve, g, u0 + i)
                        nc.vector.tensor_tensor(a3[:, s, 2 * i:2 * i + 2, :],
                                                psum_g[:, G.slot(u0 + i), :].rearrange(
                                                    "p (j d) -> p j d", j=2),
                                                a3[:, s, 2 * i:2 * i + 2, :],
                                                ALU.add).then_inc(G.evacuated[G.slot(u0 + i)], 1)
                    for i in range(2):
                        G.wait_evacuated(dve, g, u0 + i)

                def group(g, b, s, U, first, last_group):
                    for i in range(NQK):
                        if not first and i in LAST_NORMS:
                            last_norms(g - 1, 1 - s, LAST_NORMS.index(i))
                        u = U["QK"] + i
                        dst = (qT if i < NP else kT)[:, i % NP, :]
                        dve.wait_ge(ex_ready, g * NQK + i + 1)
                        nc.vector.scalar_tensor_tensor(
                            out=dst, in0=psum_g[:, G.slot(u), :], scalar=0.0,
                            in1=ex[:, i % 4, :], op0=ALU.max, op1=ALU.add
                            ).then_inc(G.evacuated[G.slot(u)], 1)
                    mask_scores(g, 0)
                    if not first:
                        keep_logits(g, g - 1, U)
                    for n in range(NCH):
                        j, g4 = n // NG, n % NG
                        if not last_group and n in FIRST_NORMS:
                            first_norms(g + 1, b + s, 1 - s, FIRST_NORMS.index(n))
                        if n % 2 == 0 and n // 2 + 1 < NCH // 2:
                            mask_scores(g, n // 2 + 1)
                        NUM.wait_full(dve, g, n)
                        num = psum_n[:, NUM.slot(n), 0:4 * DV].rearrange("p (h d) -> p h d", d=DV)
                        den_chain.at = 2 * n
                        den_chain.link(dve, g, nc.vector.tensor_scalar(den[:, 0, :], num[:, :, DH1],
                                                                       EPS_DEN, None, ALU.max))
                        den_chain.link(dve, g, nc.vector.reciprocal(den[:, 1, :], den[:, 0, :]))
                        nc.vector.tensor_tensor(
                            o[:, j % 2, g4 * 4 * DH1:(g4 + 1) * 4 * DH1].rearrange(
                                "p (h d) -> p h d", d=DH1),
                            num[:, :, 0:DH1],
                            den[:, 1, :].rearrange("p (h a) -> p h a", a=1).broadcast_to([P, 4, DH1]),
                            ALU.mult).then_inc(NUM.evacuated[NUM.slot(n)], 1)
                        NUM.wait_evacuated(dve, g, n)
                        UP.wait_full(dve, g, n)
                        up = psum_u[:, 0:4 * DV].rearrange("p (a d) -> p a d", a=2)
                        for h2 in range(2):
                            rows, cols = slice(64 * h2, 64 * h2 + 64), slice(h2 * DV, h2 * DV + DV)
                            st = state[rows, 2 * g4:2 * g4 + 2, cols]
                            last = nc.vector.tensor_tensor(st, st, up[rows, :, cols], ALU.add)
                        last.then_inc(UP.evacuated[0], 1)
                    if not last_group:
                        high(g, g + 1, U)
                    add_a3(g, s, U["W"])
                    chain2.at = 0
                    ln2.variance(dve, g, 0, chain2, lambda j: a3[:, s, j, :])
                    ln2.wait_power(dve, g, 0)
                    if not first:
                        dve.wait_ge(xf_stored, g * 16)
                    for j in range(G4):
                        last = ln2.apply(j, norm[:, j, :], a3[:, s, j, :])
                    last.then_inc(norm2_ready, 1)
                    add_a3(g, s, U["F2"])

                def high_weights(n):
                    dve.wait_ge(raw_loaded[n], 80 if n == 0 else 16)
                    nc.vector.scalar_tensor_tensor(out=raw_diff[n], in0=raw[n], scalar=SPLIT,
                                                   in1=raw[n], op0=ALU.mult,
                                                   op1=ALU.subtract).then_inc(w_hi, 1)
                    dve.wait_ge(w_hi, 2 * n + 1)
                    nc.vector.scalar_tensor_tensor(out=part_of("hi", n), in0=raw[n], scalar=SPLIT,
                                                   in1=raw_diff[n], op0=ALU.mult,
                                                   op1=ALU.subtract).then_inc(w_hi, 1)

                for part in range(6):
                    first_norms(0, 0, 0, part)
                high_weights(0)
                high(0, 0, units_before)
                for n in (1, 2):
                    high_weights(n)
                groups(dve, group)
                for part in range(8):
                    last_norms(NGR - 1, 1, part)
                keep_logits(NGR - 1, NGR - 1, units_after)


def routing(nc, logits, xf_dram, rows_dram, w1, w2, from1, from2):
    NT = N // P
    with ExitStack() as ctx:
        def sb(name, shape, dt=F32):
            return ctx.enter_context(nc.sbuf_tensor(name, shape, dt))

        def sem(name):
            return ctx.enter_context(nc.semaphore(name))

        psum = ctx.enter_context(nc.psum_tensor("r_psum", [P, 2, HALF], F32))
        before = sb("r_before", [P, P])
        ones = sb("r_ones", [P, P])
        index = sb("r_index", [P, E])
        best = [sb("r_best", [P, NT]), sb("r_second", [P, NT])]
        place = [sb("r_place_first", [P, NT]), sb("r_place_second", [P, NT])]
        picked = [sb("r_picked_first", [P, NT, E]), sb("r_picked_second", [P, NT, E])]
        left = sb("r_left", [P, NT, E])
        t0 = sb("r_t0", [P, NT, E])
        both = sb("r_both", [P, NT, E])
        count = [sb("r_count0", [P, NT, E]), sb("r_count1", [P, NT, E])]
        kept = sb("r_kept", [P, NT])
        row = sb("r_row", [P, NT])
        gap = sb("r_gap", [P, NT])
        gate = [sb("r_gate_first", [P, NT]), sb("r_gate_second", [P, NT])]
        to = [sb("r_to_first", [P, NT], I32), sb("r_to_second", [P, NT], I32)]
        XG = 4
        xf = sb("r_xf", [P, 4, XG, D])

        made = sem("r_made")
        step = sem("r_step")
        gap_ready = sem("r_gap_ready")
        exp_ready = sem("r_exp_ready")
        picked_ready = sem("r_picked_ready")
        counted = sem("r_counted")
        to_ready = sem("r_to_ready")
        xf_loaded = [sem(f"r_xf_loaded{i}") for i in range(4)]
        scattered = [sem(f"r_scattered{i}") for i in range(4)]

        def spread(t):
            return t[:, :].rearrange("p (t a) -> p t a", a=1).broadcast_to([P, NT, E])

        with nc.Block() as block:
            @block.gpsimd
            def _(pool):
                for e in range(E):
                    nc.gpsimd.memset(index[:, e:e + 1], float(e - E)).then_inc(made, 1)
                nc.gpsimd.memset(ones[:, :], 1.0).then_inc(made, 1)
                nc.gpsimd.memset(before[:, :], 1.0).then_inc(made, 1)
                pool.wait_ge(made, E + 2)
                nc.gpsimd.affine_select(out=before[:, :], in_=before[:, :], compare_op=ALU.is_ge,
                                        fill=0.0, base=-1, pattern=[[1, P]],
                                        channel_multiplier=-1).then_inc(made, 1)
                pool.wait_ge(made, E + 3)
                pool.wait_ge(to_ready, 1)
                for g in range(NT // XG):
                    pool.wait_ge(xf_loaded[g % 4], 16 * (g // 4 + 1))
                    for j in range(XG):
                        for k in range(2):
                            nc.gpsimd.indirect_dma_start(
                                out=rows_dram,
                                out_offset=bass.IndirectOffsetOnAxis(
                                    ap=to[k][:, g * XG + j:g * XG + j + 1], axis=0),
                                in_=xf[:, g % 4, j, :], in_offset=None,
                                bounds_check=SLOTS - 1, oob_is_err=False
                            ).then_inc(scattered[g % 4], 16)
                for i in range(4):
                    pool.wait_ge(scattered[i], 16 * 2 * XG * (NT // XG // 4))

            @block.sync
            def _(sp):
                xv = xf_dram.rearrange("(g j p) d -> g p j d", p=P, j=XG)
                for g in range(NT // XG):
                    if g >= 4:
                        sp.wait_ge(scattered[g % 4], 16 * 2 * XG * (g // 4))
                    sp.dma_start(xf[:, g % 4, :, :], xv[g]).then_inc(xf_loaded[g % 4], 16)

            @block.tensor
            def _(pe):
                pe.wait_ge(made, E + 3)
                pe.wait_ge(picked_ready, 1)
                sel = both[:, :, :].rearrange("p t e -> p (t e)")
                nc.tensor.matmul(psum[:, 0, 0:NT * E], before[:, :], sel, start=True, stop=True)
                nc.tensor.matmul(psum[:, 1, 0:NT * E], ones[:, :], sel, start=True,
                                 stop=True).then_inc(counted, 1)

            @block.scalar
            def _(act):
                act.wait_ge(gap_ready, 1)
                nc.scalar.activation(gap[:, :], gap[:, :], ACT.Exp).then_inc(exp_ready, 1)

            @block.vector
            def _(dve):
                at = [0]

                def link(ins):
                    at[0] += 1
                    ins.then_inc(step, 1)
                    dve.wait_ge(step, at[0])

                idx = index[:, :].rearrange("p (a e) -> p a e", a=1).broadcast_to([P, NT, E])
                dve.wait_ge(made, E)
                src = logits
                for k in range(2):
                    link(nc.vector.tensor_reduce(best[k][:, :], src[:, :, :], AX.X, ALU.max))
                    link(nc.vector.tensor_tensor(t0[:, :, :], src[:, :, :], spread(best[k]), ALU.is_equal))
                    link(nc.vector.tensor_tensor(t0[:, :, :], t0[:, :, :], idx, ALU.mult))
                    link(nc.vector.tensor_reduce(place[k][:, :], t0[:, :, :], AX.X, ALU.min))
                    link(nc.vector.tensor_tensor(picked[k][:, :, :], idx, spread(place[k]), ALU.is_equal))
                    if k == 0:
                        link(nc.vector.scalar_tensor_tensor(out=left[:, :, :], in0=picked[0][:, :, :],
                                                            scalar=NEG, in1=logits[:, :, :],
                                                            op0=ALU.mult, op1=ALU.add))
                        src = left
                nc.vector.tensor_tensor(gap[:, :], best[1][:, :], best[0][:, :],
                                        ALU.subtract).then_inc(gap_ready, 1)
                nc.vector.tensor_tensor(both[:, :, :], picked[0][:, :, :], picked[1][:, :, :],
                                        ALU.add).then_inc(picked_ready, 1)
                dve.wait_ge(counted, 1)
                total = psum[:, 1, 0:NT * E].rearrange("p (t e) -> p t e", e=E)
                within = psum[:, 0, 0:NT * E].rearrange("p (t e) -> p t e", e=E)
                nc.vector.memset(count[0][:, 0:1, :], 0.0)
                link(nc.vector.tensor_copy(count[0][:, 1:NT, :], total[:, 0:NT - 1, :]))
                a, d = 0, 1
                while d < NT:
                    nc.vector.tensor_copy(count[1 - a][:, 0:d, :], count[a][:, 0:d, :])
                    link(nc.vector.tensor_tensor(count[1 - a][:, d:NT, :], count[a][:, d:NT, :],
                                                 count[a][:, 0:NT - d, :], ALU.add))
                    a, d = 1 - a, 2 * d
                link(nc.vector.tensor_tensor(count[a][:, :, :], count[a][:, :, :], within, ALU.add))
                dve.wait_ge(exp_ready, 1)
                link(nc.vector.tensor_scalar(gate[1][:, :], gap[:, :], 1.0, None, ALU.add))
                link(nc.vector.reciprocal(gate[0][:, :], gate[1][:, :]))
                link(nc.vector.tensor_tensor(gate[1][:, :], gate[0][:, :], gap[:, :], ALU.mult))
                for k, (w, source) in enumerate(((w1, from1), (w2, from2))):
                    link(nc.vector.tensor_tensor(t0[:, :, :], picked[k][:, :, :], count[a][:, :, :],
                                                 ALU.mult))
                    link(nc.vector.tensor_reduce(row[:, :], t0[:, :, :], AX.X, ALU.add))
                    link(nc.vector.tensor_scalar(kept[:, :], row[:, :], float(CAP), None, ALU.is_lt))
                    link(nc.vector.scalar_tensor_tensor(out=row[:, :], in0=place[k][:, :],
                                                        scalar=float(CT * P), in1=row[:, :],
                                                        op0=ALU.mult, op1=ALU.add))
                    link(nc.vector.tensor_tensor(row[:, :], row[:, :], kept[:, :], ALU.mult))
                    nc.vector.tensor_scalar(source[:, :], row[:, :], float(SLOTS), None, ALU.add)
                    ins = nc.vector.tensor_scalar(to[k][:, :], row[:, :], float(SLOTS), None, ALU.add)
                    link(ins)
                    link(nc.vector.tensor_tensor(w[:, :], gate[k][:, :], kept[:, :], ALU.mult))
                dve.sem_inc(to_ready, 1)


def experts(nc, ident, rows_dram, W1, b1, W2, b2, y_dram):
    MH = HE // P
    TURN = E // 2
    sizes = [CT // 5 + (i < CT % 5) for i in range(5)]
    GROUPS = [(sum(sizes[:i]), n) for i, n in enumerate(sizes)]
    NGR = len(GROUPS)
    NQ = 2 * NGR
    NW = 2 * CD * HE // HALF
    PAIRS = (("hi", "hi"), ("hi", "lo"), ("lo", "hi"))
    assert max(sizes) == 4 and min(sizes) == 3

    def splits(more):
        seq = [("T", 0, c) for c in range(CD)]
        for q in range(NQ):
            e2, at = q // NGR, q % NGR
            pieces = [("W", 1 - e2, 2 * at + k) for k in range(2)] if at < 4 else []
            if e2 == 1 and not more:
                pieces = []
            if q + 1 < NQ:
                seq += [("T", q + 1, c) for c in range(CD)]
            for half in range(2):
                seq += [("H", q, m) for m in range(4 * half, 4 * half + 4)]
                seq += pieces[half:half + 1]
        return seq

    NS = len(splits(True))
    TMP = 4
    assert 2 * 4 == NW and NS % TMP == 0 and NW % TMP == 0
    with ExitStack() as ctx:
        def sb(name, shape, dt=F32):
            return ctx.enter_context(nc.sbuf_tensor(name, shape, dt))

        def sem(name):
            return ctx.enter_context(nc.semaphore(name))

        psum_t = ctx.enter_context(nc.psum_tensor("e_turned", [P, 2, HALF], F32))
        psum_h = ctx.enter_context(nc.psum_tensor("e_hidden", [P, 4, HALF], F32))
        psum_y = ctx.enter_context(nc.psum_tensor("e_out", [P, 2, HALF], F32))
        raw = sb("e_weights", [P, NW, HALF])
        w = {part: sb(f"e_weights_{part}", [P, 2, NW, HALF], F32R) for part in ("hi", "lo")}
        b1_sb = sb("e_b1", [P, 2, MH])
        b2_sb = sb("e_b2", [P, 2, D])
        rows = sb("e_rows", [P, 4, D])
        whole = sb("e_to_split", [P, TMP, HALF])
        diff = sb("e_difference", [P, TMP, HALF])
        rT = {part: sb(f"e_rT_{part}", [P, 2, CD, HALF], F32R) for part in ("hi", "lo")}
        hT = {part: sb(f"e_hT_{part}", [P, 2, MH, HALF], F32R) for part in ("hi", "lo")}
        y = sb("e_y", [P, 2, 4, D])
        w1 = {part: w[part][:, :, 0:NW // 2, :].rearrange("p s (c a) n -> p s c (a n)", c=CD)
              for part in w}
        w2 = {part: w[part][:, :, NW // 2:NW, :].rearrange("p s k (a n) -> p s (k a) n", n=D)
              for part in w}

        TU = Ring(sem, "e_turned", 2, NQ * CD)
        HU = Ring(sem, "e_hidden", 4, NQ * MH)
        YU = Ring(sem, "e_out", 2, NQ * 2)
        raw_loaded = [sem("e_w1_loaded"), sem("e_w2_loaded")]
        b_loaded = [sem(f"e_biases_loaded{i}") for i in range(2)]
        rows_loaded = sem("e_rows_loaded")
        y_stored = [sem(f"e_y_stored{i}") for i in range(2)]
        diff_ready = sem("e_difference_ready")
        hi_ready = sem("e_hi_ready")
        lo_ready = sem("e_lo_ready")

        def count(i, n):
            return i * NS + NW + n + 1

        def turns(eng, turn):
            with eng.Fori(0, TURN - 1) as i:
                turn(i, splits(True), True)
            turn(TURN - 1, splits(False), False)

        def operands(what):
            kind, at, k = what[0:3]
            if kind == "W":
                return raw[:, k, :], w["hi"][:, at, k, :], w["lo"][:, at, k, :]
            n = GROUPS[at % NGR][1] * P
            dst = rT if kind == "T" else hT
            return whole[:, what[3], 0:n], dst["hi"][:, at % 2, k, 0:n], dst["lo"][:, at % 2, k, 0:n]

        def with_slots(seq):
            out, u = [], 0
            for what in seq:
                out.append(what + (u % TMP,))
                u += what[0] != "W"
            return out

        def of_expert(src, e, pattern, **sizes):
            return src[bass.ds(e, 1), :, :].rearrange(pattern, **sizes)

        with nc.Block() as block:
            @block.sync
            def _(sp):
                for ring in (TU, HU, YU):
                    ring.begin(sp)
                for s in y_stored:
                    sp.sem_inc(s, 16)
                rv = rows_dram.rearrange("(e t p) d -> e p t d", p=P, t=CT)

                def load_weights(e):
                    sp.dma_start(raw[:, 0:NW // 2, :].rearrange("p k n -> p (k n)"),
                                 of_expert(W1, e, "a (c p) n -> p (a c) n", p=P)
                                 ).then_inc(raw_loaded[0], 16)
                    sp.dma_start(raw[:, NW // 2:NW, :].rearrange("p k n -> p (k n)"),
                                 of_expert(W2, e, "a (c p) n -> p (a c) n", p=P)
                                 ).then_inc(raw_loaded[1], 16)

                def turn(i, seq, more):
                    for q in range(NQ):
                        e2, (t0, n) = q // NGR, GROUPS[q % NGR]
                        e = i * 2 + e2
                        if q % NGR == 0:
                            YU.wait_evacuated_before(sp, i, 2 * (e2 * NGR + NGR) - 1)
                            sp.dma_start(b1_sb[:, e2, :], b1[bass.ds(e, 1), :].rearrange(
                                "a (m p) -> p (a m)", p=P), allow_slow_non_contiguous=True
                                ).then_inc(b_loaded[e2], 16)
                            sp.dma_start(b2_sb[:, e2, :], b2[bass.ds(e, 1), :].rearrange(
                                "a d -> (a d)").partition_broadcast(P)).then_inc(b_loaded[e2], 16)
                        if q == 0:
                            TU.wait_evacuated_before(sp, i, NQ * CD - 1)
                        else:
                            TU.wait_evacuated(sp, i, q * CD - 1)
                        sp.dma_start(rows[:, 0:n, :],
                                     rv[bass.ds(e, 1), :, t0:t0 + n, :].rearrange("a p t d -> p (a t) d")
                                     ).then_inc(rows_loaded, 16)
                        if q % NGR == 0 and (e2 == 0 or more):
                            last = -1 if e2 == 0 else seq.index(("W", 1, NW - 1))
                            sp.wait_ge(lo_ready, count(i, last))
                            load_weights(e + 1)

                load_weights(0)
                turns(sp, turn)

            @block.tensor
            def _(pe):
                def turned(i, q):
                    n = GROUPS[q % NGR][1]
                    pe.wait_ge(rows_loaded, i * (16 * NQ) + 16 * q + 16)
                    for c in range(CD):
                        u = q * CD + c
                        TU.wait_free(pe, i, u)
                        for j in range(n):
                            last = nc.tensor.transpose(psum_t[:, c, j * P:(j + 1) * P],
                                                       rows[:, j, c * P:(c + 1) * P], ident[:, :])
                        last.then_inc(TU.full[c], 1)

                def hidden(i, q, seq):
                    e2, n = q // NGR, GROUPS[q % NGR][1]
                    pe.wait_ge(lo_ready, count(i, seq.index(("T", q, CD - 1))))
                    for m in range(MH):
                        u = q * MH + m
                        HU.wait_free(pe, i, u)
                        terms = [(c, a, b) for c in range(CD) for a, b in PAIRS]
                        for k, (c, a, b) in enumerate(terms):
                            last = nc.tensor.matmul(psum_h[:, HU.slot(u), 0:n * P],
                                                    w1[a][:, e2, c, m * P:(m + 1) * P],
                                                    rT[b][:, q % 2, c, 0:n * P],
                                                    start=(k == 0), stop=(k == len(terms) - 1))
                        last.then_inc(HU.full[HU.slot(u)], 1)

                def outer(i, q, seq):
                    e2, n = q // NGR, GROUPS[q % NGR][1]
                    pe.wait_ge(lo_ready, count(i, seq.index(("H", q, MH - 1))))
                    for s in range(2):
                        YU.wait_free(pe, i, 2 * q + s)
                        for j in range(2 * s, min(2 * s + 2, n)):
                            terms = [(m, a, b) for m in range(MH) for a, b in PAIRS]
                            for k, (m, a, b) in enumerate(terms):
                                last = nc.tensor.matmul(
                                    psum_y[:, s, (j - 2 * s) * D:(j - 2 * s + 1) * D],
                                    hT[a][:, q % 2, m, j * P:(j + 1) * P], w2[b][:, e2, m, :],
                                    start=(k == 0), stop=(k == len(terms) - 1))
                        last.then_inc(YU.full[s], 1)

                def turn(i, seq, more):
                    turned(i, 0)
                    for q in range(NQ):
                        if q + 1 < NQ:
                            turned(i, q + 1)
                        hidden(i, q, seq)
                        if q > 0:
                            outer(i, q - 1, seq)
                    outer(i, NQ - 1, seq)

                turns(pe, turn)

            @block.scalar
            def _(act):
                yv = y_dram[0:SLOTS, :].rearrange("(e t p) d -> e p t d", p=P, t=CT)

                def store(i, q):
                    e2, (t0, n) = q // NGR, GROUPS[q % NGR]
                    for s in range(2):
                        YU.wait_evacuated(act, i, 2 * q + s)
                    act.dma_start(yv[bass.ds(i * 2 + e2, 1), :, t0:t0 + n, :].rearrange(
                        "a p t d -> p (a t) d"), y[:, q % 2, 0:n, :]).then_inc(y_stored[q % 2], 16)

                def turn(i, seq, more):
                    mine = [(at, what) for at, what in enumerate(with_slots(seq)) if what[0] != "W"]
                    for k, (at, (kind, q, m, slot)) in enumerate(mine):
                        n = GROUPS[q % NGR][1] * P
                        if kind == "H" and m == 4 and q >= 2:
                            store(i, q - 2)
                        if kind == "H" and m == 0 and q % NGR == 0:
                            act.wait_ge(b_loaded[q // NGR], i * 32 + 32)
                        act.wait_ge(lo_ready, count(i, mine[k - TMP][0] if k >= TMP else k - TMP))
                        if kind == "T":
                            u = q * CD + m
                            TU.wait_full(act, i, u)
                            nc.scalar.copy(whole[:, slot, 0:n], psum_t[:, m, 0:n]
                                           ).then_inc(TU.evacuated[m], 1)
                        else:
                            u = q * MH + m
                            HU.wait_full(act, i, u)
                            nc.scalar.activation(whole[:, slot, 0:n], psum_h[:, HU.slot(u), 0:n],
                                                 ACT.Gelu_apprx_tanh, bias=b1_sb[:, q // NGR, m:m + 1]
                                                 ).then_inc(HU.evacuated[HU.slot(u)], 1)
                    store(i, NQ - 2)
                    store(i, NQ - 1)

                turns(act, turn)
                for s in y_stored:
                    act.wait_ge(s, 16 * (TURN * NGR + 1))

            @block.gpsimd
            def _(pool):
                def low(i, at, what):
                    x, hi, lo = operands(what)
                    pool.wait_ge(hi_ready, count(i, at))
                    nc.gpsimd.tensor_tensor(lo, x, hi.bitcast(F32), ALU.subtract).then_inc(lo_ready, 1)

                def turn(i, seq, more):
                    for at, what in enumerate(with_slots(seq)):
                        low(i, at, what)

                for k in range(NW):
                    low(0, k - NW, ("W", 0, k))
                turns(pool, turn)

            @block.vector
            def _(dve):
                def difference(i, at, what):
                    x = operands(what)[0]
                    kind, q, m = what[0:3]
                    if kind == "W":
                        if m % (NW // 2) == 0:
                            e = 0 if at < 0 else i * 2 + (1 if q == 1 else 2)
                            dve.wait_ge(raw_loaded[m // (NW // 2)], e * 16 + 16)
                    elif kind == "T":
                        TU.wait_evacuated(dve, i, q * CD + m)
                    else:
                        HU.wait_evacuated(dve, i, q * MH + m)
                    if at >= TMP - NW:
                        dve.wait_ge(hi_ready, count(i, at - TMP))
                    nc.vector.scalar_tensor_tensor(out=diff[:, at % TMP, 0:x.shape[-1]], in0=x,
                                                   scalar=SPLIT, in1=x, op0=ALU.mult,
                                                   op1=ALU.subtract).then_inc(diff_ready, 1)

                def high(i, at, what):
                    x, hi, lo = operands(what)
                    dve.wait_ge(diff_ready, count(i, at))
                    nc.vector.scalar_tensor_tensor(out=hi, in0=x, scalar=SPLIT,
                                                   in1=diff[:, at % TMP, 0:x.shape[-1]], op0=ALU.mult,
                                                   op1=ALU.subtract).then_inc(hi_ready, 1)

                def finish(i, q):
                    e2, n = q // NGR, GROUPS[q % NGR][1]
                    dve.wait_ge(y_stored[q % 2], i * (16 * NGR) + q // 2 * 16 + 16)
                    if q % NGR == 0:
                        dve.wait_ge(b_loaded[e2], i * 32 + 32)
                    for s in range(2):
                        j0, k = 2 * s, min(2, n - 2 * s)
                        YU.wait_full(dve, i, 2 * q + s)
                        nc.vector.tensor_tensor(
                            y[:, q % 2, j0:j0 + k, :],
                            psum_y[:, s, 0:k * D].rearrange("p (j d) -> p j d", d=D),
                            b2_sb[:, e2:e2 + 1, :].broadcast_to([P, k, D]),
                            ALU.add).then_inc(YU.evacuated[s], 1)

                def split(i, first, seq):
                    for k, what in enumerate(seq):
                        difference(i, first + k, what)
                        if k > 0:
                            high(i, first + k - 1, seq[k - 1])
                    high(i, first + len(seq) - 1, seq[-1])

                def turn(i, seq, more):
                    seq = with_slots(seq)
                    at = 0
                    for q in range(NQ):
                        n = 1 + max(k for k, what in enumerate(seq)
                                    if what[0:2] in (("H", q), ("T", q + 1)) or
                                    what[0] == "W" and k > 0 and
                                    seq[k - 1][0:2] in (("H", q), ("T", q + 1)))
                        split(i, at, seq[at:n])
                        at = n
                        if q > 0:
                            finish(i, q - 1)
                    finish(i, NQ - 1)

                split(0, -NW, [("W", 0, k) for k in range(NW)])
                turns(dve, turn)


def combine(nc, minus_half, y_dram, x3_dram, w1, w2, from1, from2, out_rows):
    XG = 4
    NG = N // P // XG
    R = 4
    with ExitStack() as ctx:
        def sb(name, shape, dt=F32):
            return ctx.enter_context(nc.sbuf_tensor(name, shape, dt))

        def sem(name):
            return ctx.enter_context(nc.semaphore(name))

        y1 = sb("f_y_first", [P, R, XG, D])
        y2 = sb("f_y_second", [P, R, XG, D])
        x3 = sb("f_x3", [P, R, XG, D])
        gathered = [sem(f"f_gathered{i}") for i in range(R)]
        x3_loaded = [sem(f"f_x3_loaded{i}") for i in range(R)]
        stored = [sem(f"f_stored{i}") for i in range(R)]
        out_ready = sem("f_out_ready")
        chain = Chain(sem, "f_dve_chain", 6 * NG)
        ln = LayerNorm(nc, ctx, sem, "f_ln", XG, NG, minus_half)
        xv = x3_dram.rearrange("(g j p) d -> g p j d", p=P, j=XG)
        ov = out_rows.rearrange("(g j p) d -> g p j d", p=P, j=XG)
        with nc.Block() as block:
            @block.gpsimd
            def _(pool):
                def gather(g):
                    if g >= R:
                        pool.wait_ge(out_ready, g - R + 1)
                    for j in range(XG):
                        t = g * XG + j
                        for dst, idx in ((y1, from1), (y2, from2)):
                            nc.gpsimd.indirect_dma_start(
                                out=dst[:, g % R, j, :], out_offset=None, in_=y_dram,
                                in_offset=bass.IndirectOffsetOnAxis(ap=idx[:, t:t + 1], axis=0)
                            ).then_inc(gathered[g % R], 16)

                gather(0)
                gather(1)
                for g in range(NG):
                    if g + 2 < NG:
                        gather(g + 2)
                    ln.power(pool, 0, g)

            @block.sync
            def _(sp):
                for g in range(NG):
                    if g >= R:
                        sp.wait_ge(stored[g % R], 16 * (g // R))
                    sp.dma_start(x3[:, g % R, :, :], xv[g]).then_inc(x3_loaded[g % R], 16)

            @block.scalar
            def _(act):
                for g in range(NG):
                    act.wait_ge(out_ready, g + 1)
                    act.dma_start(ov[g], x3[:, g % R, :, :]).then_inc(stored[g % R], 16)
                for s in stored:
                    act.wait_ge(s, 16 * (NG // R))

            @block.vector
            def _(dve):
                for g in range(NG):
                    r = g % R
                    dve.wait_ge(gathered[r], 32 * XG * (g // R + 1))
                    for j in range(XG):
                        t = g * XG + j
                        last = nc.vector.tensor_scalar(y1[:, r, j, :], y1[:, r, j, :], w1[:, t:t + 1],
                                                       None, ALU.mult)
                    chain.link(dve, 0, last)
                    for j in range(XG):
                        t = g * XG + j
                        last = nc.vector.scalar_tensor_tensor(
                            out=y1[:, r, j, :], in0=y2[:, r, j, :], scalar=w2[:, t:t + 1],
                            in1=y1[:, r, j, :], op0=ALU.mult, op1=ALU.add)
                    chain.link(dve, 0, last)
                    ln.variance(dve, 0, g, chain, lambda j: y1[:, r, j, :])
                    ln.wait_power(dve, 0, g)
                    for j in range(XG):
                        last = ln.apply(j, y1[:, r, j, :], y1[:, r, j, :])
                    chain.link(dve, 0, last)
                    dve.wait_ge(x3_loaded[r], 16 * (g // R + 1))
                    nc.vector.tensor_tensor(x3[:, r, :, :], x3[:, r, :, :], y1[:, r, :, :],
                                            ALU.add).then_inc(out_ready, 1)
                chain.done()


_INS = ['L0_attn_x', 'L0_attn_W_qkv', 'L0_attn_b_qkv', 'L0_attn_W_proj', 'L0_attn_b_proj',
        'L0_ffn_weight', 'L0_ffn_disha', 'L1_attn_ln1_g', 'L1_attn_ln1_b', 'L1_attn_Wq', 'L1_attn_Wk',
        'L1_attn_Wv', 'L1_attn_Wo', 'L1_attn_ln2_g', 'L1_attn_ln2_b', 'L1_attn_Wf1', 'L1_attn_Wf2',
        'L1_ffn_Wg', 'L1_ffn_W1', 'L1_ffn_b1', 'L1_ffn_W2', 'L1_ffn_b2']


def kernel(**inputs):
    import numpy as _np
    import concourse.bacc as _bacc
    from concourse.bass_utils import run_bass_kernel_spmd as _run

    nc = _bacc.Bacc("TRN2", target_bir_lowering=False, num_devices=1)
    arrays, args = {}, []
    for name in _INS:
        a = _np.ascontiguousarray(inputs[name])
        arrays[f"in_{name}_dram"] = a
        args.append(nc.dram_tensor(f"in_{name}_dram", a.shape, mybir.dt.from_np(a.dtype),
                                   kind="ExternalInput").ap())
    args.append(nc.dram_tensor("out_0_dram", (B, T, D), F32, kind="ExternalOutput").ap())
    build(nc, *args)
    r = _run(nc, [arrays], core_ids=[0])
    return r.results[0]["out_0_dram"]
```
